# Optimizing a Trainium2 kernel written in Bass

```python
import numpy as np
import jax
import jax.numpy as jnp

def _softmax(x, axis=-1):
    return jax.nn.softmax(x, axis=axis)

def _gelu(x):
    return jax.nn.gelu(x, approximate=True)

def _silu(x):
    return jax.nn.silu(x)

def _sigmoid(x):
    return jax.nn.sigmoid(x)

def _layernorm(x, axis=-1, eps=1e-05):
    m = jnp.mean(x, axis=axis, keepdims=True)
    v = jnp.var(x, axis=axis, keepdims=True)
    return (x - m) / jnp.sqrt(v + eps)

def _scatter_add(tgt, idx, src, axis=0):
    return tgt.at[idx].add(src)

def _segment_sum(src, seg, n):
    return jax.ops.segment_sum(src, seg, n)
kernel_name = 'mk_seq_preln_d2_jaxref_r8_2521b6'

def setup_inputs(seed: int=0):
    np.random.seed(seed)
    _w = jnp.asarray

    def _L0_attn_setup():
        import jax, jax.numpy as jnp
        import numpy as np
        FOCUS = 3
        EPS = 1e-06

        def _norm_last(t):
            return t / jnp.sum(t, axis=-1, keepdims=True)
        key = jax.random.key(seed)
        ks = jax.random.split(key, 6)
        B, N, C = (4, 512, 128)
        s = 0.02
        return {'x': jax.random.normal(ks[0], (B, N, C), jnp.float32), 'w_qkv': jax.random.normal(ks[1], (3 * C, C), jnp.float32) * s, 'w_proj': jax.random.normal(ks[2], (C, C), jnp.float32) * s, 'b_proj': jax.random.normal(ks[3], (C,), jnp.float32) * s, 'w_dwc': jax.random.normal(ks[4], (C, 3), jnp.float32) * s, 'b_dwc': jax.random.normal(ks[5], (C,), jnp.float32) * s}
    _L0_attn_in = _L0_attn_setup()

    def _L0_ffn_setup():
        import jax, jax.numpy as jnp
        import numpy as np
        N_EXPERTS = 8
        TOP_K = 2
        key = jax.random.key(seed)
        k1, k2, k3, k4 = jax.random.split(key, 4)
        B, T, C, H, E = (2, 256, 128, 512, N_EXPERTS)
        x = jax.random.normal(k1, (B, T, C), dtype=jnp.float32)
        router_w = jax.random.normal(k2, (E, C), dtype=jnp.float32) * 0.02
        w1 = jax.random.normal(k3, (E, C, H), dtype=jnp.float32) * (1.0 / np.sqrt(C))
        w2 = jax.random.normal(k4, (E, H, C), dtype=jnp.float32) * (1.0 / np.sqrt(H))
        return {'x': x, 'router_w': router_w, 'w1': w1, 'w2': w2}
    _L0_ffn_in = _L0_ffn_setup()

    def _L1_attn_setup():
        import jax, jax.numpy as jnp
        import numpy as np
        DIM = 128
        MULT = 1
        HID = DIM * MULT
        C = 8.0
        key = jax.random.key(seed)
        k_x, k_wa, k_wx, k_lam = jax.random.split(key, 4)
        B, T = (8, 512)
        x = jax.random.normal(k_x, (B, T, DIM), dtype=jnp.float32)
        std = DIM ** (-0.5)
        Wa = jax.random.normal(k_wa, (HID, DIM), dtype=jnp.float32) * std
        Wx = jax.random.normal(k_wx, (HID, DIM), dtype=jnp.float32) * std
        ba = jnp.zeros((HID,), dtype=jnp.float32)
        bx = jnp.zeros((HID,), dtype=jnp.float32)
        lo = float(np.log(0.9 / 0.1))
        hi = float(np.log(0.999 / 0.001))
        Lam = jax.random.uniform(k_lam, (HID,), dtype=jnp.float32, minval=lo, maxval=hi)
        return {'x': x, 'Wa': Wa, 'Wx': Wx, 'ba': ba, 'bx': bx, 'Lam': Lam}
    _L1_attn_in = _L1_attn_setup()

    def _L1_ffn_setup():
        import jax, jax.numpy as jnp
        import numpy as np
        B, L, D = (2, 128, 128)
        HID, E, K = (256, 8, 2)
        key = jax.random.key(seed)
        ks = jax.random.split(key, 4)
        std = 0.02
        return {'x': jax.random.normal(ks[0], (B, L, D), dtype=jnp.float32), 'router_scale': jnp.ones((D,), dtype=jnp.float32), 'router_w': jax.random.normal(ks[1], (D, E), dtype=jnp.float32) * std, 'gating_w': jax.random.normal(ks[2], (E, 2, HID, D), dtype=jnp.float32) * std, 'linear_w': jax.random.normal(ks[3], (E, HID, D), dtype=jnp.float32) * std, 'per_expert_scale': jnp.ones((E,), dtype=jnp.float32)}
    _L1_ffn_in = _L1_ffn_setup()
    _d = {'L0_attn_x': _L0_attn_in['x'], 'L0_attn_w_qkv': _L0_attn_in['w_qkv'], 'L0_attn_w_proj': _L0_attn_in['w_proj'], 'L0_attn_b_proj': _L0_attn_in['b_proj'], 'L0_attn_w_dwc': _L0_attn_in['w_dwc'], 'L0_attn_b_dwc': _L0_attn_in['b_dwc'], 'L0_ffn_router_w': _L0_ffn_in['router_w'], 'L0_ffn_w1': _L0_ffn_in['w1'], 'L0_ffn_w2': _L0_ffn_in['w2'], 'L1_attn_Wa': _L1_attn_in['Wa'], 'L1_attn_Wx': _L1_attn_in['Wx'], 'L1_attn_ba': _L1_attn_in['ba'], 'L1_attn_bx': _L1_attn_in['bx'], 'L1_attn_Lam': _L1_attn_in['Lam'], 'L1_ffn_router_scale': _L1_ffn_in['router_scale'], 'L1_ffn_router_w': _L1_ffn_in['router_w'], 'L1_ffn_gating_w': _L1_ffn_in['gating_w'], 'L1_ffn_linear_w': _L1_ffn_in['linear_w'], 'L1_ffn_per_expert_scale': _L1_ffn_in['per_expert_scale']}
    _x0 = _d['L0_attn_x']
    _d['L0_attn_x'] = jax.random.normal(jax.random.fold_in(jax.random.key(seed), 1), (2, 1024, 128), dtype=_x0.dtype)
    del _x0
    return _d

def reference(L0_attn_x, L0_attn_w_qkv, L0_attn_w_proj, L0_attn_b_proj, L0_attn_w_dwc, L0_attn_b_dwc, L0_ffn_router_w, L0_ffn_w1, L0_ffn_w2, L1_attn_Wa, L1_attn_Wx, L1_attn_ba, L1_attn_bx, L1_attn_Lam, L1_ffn_router_scale, L1_ffn_router_w, L1_ffn_gating_w, L1_ffn_linear_w, L1_ffn_per_expert_scale):

    def _L0_attn_ref(x, w_qkv, w_proj, b_proj, w_dwc, b_dwc):
        import jax, jax.numpy as jnp
        import numpy as np
        FOCUS = 3
        EPS = 1e-06

        def _norm_last(t):
            return t / jnp.sum(t, axis=-1, keepdims=True)
        B, N, C = x.shape
        H = 16
        d = C // H
        qkv = jnp.einsum('bnc,oc->bno', x, w_qkv).reshape(B, N, 3, H, d)
        qkv = jnp.transpose(qkv, (2, 0, 3, 1, 4))
        q, k, v = (qkv[0], qkv[1], qkv[2])
        q = _norm_last(jax.nn.relu(q) + EPS)
        k = _norm_last(jax.nn.relu(k) + EPS)
        q = _norm_last(q ** FOCUS)
        k = _norm_last(k ** FOCUS)
        kv = jnp.einsum('bhnd,bhne->bhde', k, v)
        z = 1.0 / (jnp.einsum('bhnd,bhd->bhn', q, k.sum(axis=2)) + EPS)
        out = jnp.einsum('bhnd,bhde,bhn->bhne', q, kv, z)
        out = jnp.transpose(out, (0, 2, 1, 3)).reshape(B, N, C)
        xp = jnp.pad(out, ((0, 0), (1, 1), (0, 0)))
        conv = xp[:, 0:N, :] * w_dwc[:, 0] + xp[:, 1:N + 1, :] * w_dwc[:, 1] + xp[:, 2:N + 2, :] * w_dwc[:, 2] + b_dwc
        out = out + conv
        return jnp.einsum('bnc,oc->bno', out, w_proj) + b_proj

    def _L0_ffn_ref(x, router_w, w1, w2):
        import jax, jax.numpy as jnp
        import numpy as np
        N_EXPERTS = 8
        TOP_K = 2
        B, T, C = x.shape
        E = N_EXPERTS
        xf = x.reshape(-1, C)
        logits = jnp.einsum('nc,ec->ne', xf, router_w)
        probs = jax.nn.softmax(logits, axis=-1)
        top_w, top_i = jax.lax.top_k(probs, TOP_K)
        top_w = top_w / jnp.sum(top_w, axis=-1, keepdims=True)
        comb = jnp.einsum('nk,nke->ne', top_w, jax.nn.one_hot(top_i, E, dtype=xf.dtype))
        h = jax.nn.gelu(jnp.einsum('nc,ech->enh', xf, w1), approximate=False)
        y = jnp.einsum('enh,ehc->enc', h, w2)
        out = jnp.einsum('ne,enc->nc', comb, y)
        return out.reshape(B, T, C)

    def _L1_attn_ref(x, Wa, Wx, ba, bx, Lam):
        import jax, jax.numpy as jnp
        import numpy as np
        DIM = 128
        MULT = 1
        HID = DIM * MULT
        C = 8.0
        r = jax.nn.sigmoid(jnp.einsum('btd,dh->bth', x, Wa) + ba)
        i = jax.nn.sigmoid(jnp.einsum('btd,dh->bth', x, Wx) + bx)
        a = jax.nn.sigmoid(Lam)
        at = a * jnp.exp(-r * jnp.log(jnp.asarray(C, x.dtype)))
        bt = jnp.sqrt(1.0 - at * at) * (i * x)

        def combine(e1, e2):
            a1, b1 = e1
            a2, b2 = e2
            return (a2 * a1, a2 * b1 + b2)
        _, y = jax.lax.associative_scan(combine, (at, bt), axis=1)
        return y

    def _L1_ffn_ref(x, router_scale, router_w, gating_w, linear_w, per_expert_scale):
        import jax, jax.numpy as jnp
        import numpy as np
        B, L, D = (2, 128, 128)
        HID, E, K = (256, 8, 2)
        d = x.shape[-1]
        var = jnp.mean(jnp.square(x), axis=-1, keepdims=True)
        r_in = x * jax.lax.rsqrt(var + 1e-06)
        r_in = r_in * jax.lax.rsqrt(jnp.array(d, dtype=r_in.dtype)) * router_scale
        logits = jnp.dot(r_in, router_w).astype(jnp.float32)
        probs = jax.nn.softmax(logits, axis=-1)
        _, top_k_idx = jax.lax.top_k(logits, K)
        indicator = jax.nn.one_hot(top_k_idx, probs.shape[-1], dtype=probs.dtype)
        gate_weights = indicator.sum(axis=-2) * probs
        renorm = jnp.sum(gate_weights, axis=-1, keepdims=True)
        renorm = jnp.where(renorm > 0.0, renorm, 1.0)
        weights = probs / renorm
        top_k_w = jnp.take_along_axis(weights, top_k_idx, axis=-1)
        combine = jnp.einsum('blke,blk->ble', indicator, top_k_w)
        combine = combine * per_expert_scale
        gate0 = jnp.einsum('bld,ehd->bleh', x, gating_w[:, 0])
        gate1 = jnp.einsum('bld,ehd->bleh', x, gating_w[:, 1])
        act = jax.nn.gelu(gate0) * gate1
        out = jnp.einsum('bleh,ehd,ble->bld', act, linear_w, combine)
        return out.astype(x.dtype)
    x = L0_attn_x
    x = x + _L0_attn_ref(_layernorm(x, axis=-1), L0_attn_w_qkv, L0_attn_w_proj, L0_attn_b_proj, L0_attn_w_dwc, L0_attn_b_dwc)
    x = x + _L0_ffn_ref(_layernorm(x, axis=-1), L0_ffn_router_w, L0_ffn_w1, L0_ffn_w2)
    x = x + _L1_attn_ref(_layernorm(x, axis=-1), L1_attn_Wa, L1_attn_Wx, L1_attn_ba, L1_attn_bx, L1_attn_Lam)
    x = x + _L1_ffn_ref(_layernorm(x, axis=-1), L1_ffn_router_scale, L1_ffn_router_w, L1_ffn_gating_w, L1_ffn_linear_w, L1_ffn_per_expert_scale)
    return x

_drawn_inputs = setup_inputs


def setup_inputs(seed=0):
    import zlib

    import numpy as np

    out = dict(_drawn_inputs(seed))
    spreads = {'L1_attn_ba': (0.0, 0.8),
     'L1_attn_bx': (0.0, 0.596),
     'L1_ffn_router_scale': (1.0, 0.6),
     'L1_ffn_per_expert_scale': (1.0, 0.6)}
    factors = {'L0_attn_w_dwc': 6.052,
     'L1_attn_Lam': 8.0,
     'L1_ffn_router_w': 8.0,
     'L1_ffn_gating_w': 8.0,
     'L1_ffn_linear_w': 8.0}
    for name, (base, spread) in spreads.items():
        noise = np.random.default_rng([zlib.crc32(name.encode()), seed]).standard_normal(out[name].shape)
        drawn = base * np.exp(spread * noise) if base else spread * noise
        out[name] = jnp.asarray(drawn.astype(out[name].dtype))
    for name, factor in factors.items():
        out[name] = (out[name] * factor).astype(out[name].dtype)
    return out
```

```python
import concourse.bass as bass
from concourse import mybir
from contextlib import ExitStack

BATCH, SEQ, CH = 2, 1024, 128
TOKENS = BATCH * SEQ
P = 128
TILES = TOKENS // P
TG = 4
GROUPS = TILES // TG
GT = TG * P
HEADS = 16
HD = CH // HEADS
FOCUS_EPS = 1e-6
LN_EPS = 1e-5
RMS_EPS = 1e-6
EXPERTS, TOP = 8, 2
HID0, HID1 = 512, 256
SLOT_TILES = TOKENS * TOP // P + EXPERTS - 1
REG = TOKENS + P
DUMP = EXPERTS * REG
DUMP_TILES = SLOT_TILES - TOKENS * TOP // P + 1
XROWS = DUMP + DUMP_TILES * P
XW = CH + 2
NO_ROW = 1 << 20
CHUNK = 1024
WCOLS = EXPERTS * (HID0 + HID0 + 2 * HID1 + HID1)
CHUNKS = WCOLS // CHUNK
CHUNKS0 = EXPERTS * 2 * HID0 // CHUNK
WRES = EXPERTS * 2 * HID0
UP_COLS = EXPERTS * 512
C_DWC, C_BDWC, C_BA, C_BX, C_LAM, C_RS, C_R0, C_R1, C_END = 0, 3, 4, 5, 6, 7, 8, 16, 24


def two_layers(nc, x, wqkv, wproj, cols, rows, wpack, wa, wx, out, upto=99):
    f32, f32r, i32, u32 = mybir.dt.float32, mybir.dt.float32r, mybir.dt.int32, mybir.dt.uint32
    ALU, ACT, AX = mybir.AluOpType, mybir.ActivationFunctionType, mybir.AxisListType
    import numpy as np

    x_v = x.rearrange("b (t p) c -> p (b t) c", p=P)
    out_v = out.rearrange("b (t p) c -> p (b t) c", p=P)
    slots_d = [nc.dram_tensor(f"slots{l}", [XROWS, XW], f32).ap() for l in range(2)]
    ys_d = [nc.dram_tensor(f"expert_out{l}", [TOP * TOKENS, CH], f32).ap() for l in range(2)]

    ctx = ExitStack()
    with ctx:
        def sb(name, shape, dt=f32):
            return ctx.enter_context(nc.sbuf_tensor(name, shape, dt))

        def sem(name):
            return ctx.enter_context(nc.semaphore(name))

        X = sb("X", [P, TILES, CH])
        XN = sb("XN", [P, TILES, CH])
        XNT = sb("XNT", [P, GROUPS, GT])
        BQ = sb("BQ", [P, 2, GROUPS, GT])
        O = sb("O", [P, BATCH, SEQ + 2])
        PBF = sb("PBF", [P, TOP * TILES * XW])
        PB = PBF[:, :].rearrange("p (k t c) -> p k t c", k=TOP, t=TILES)
        SQ = PBF[:, 0:4 * GT].rearrange("p (a b n) -> p a b n", a=2, b=2)
        REC = PBF[:, 4 * GT:8 * GT].rearrange("p (a b n) -> p a b n", a=2, b=2)
        W = sb("W", [P, 2 * WRES], f32r)
        RAW = sb("RAW", [P, 2, CHUNK])
        WQKV = sb("WQKV", [P, 3 * CH])
        WP = sb("WP", [P, CH])
        WK = sb("WK", [P, 3, CH])
        WA = sb("WA", [P, CH])
        WX = sb("WX", [P, CH])
        COLS = sb("COLS", [P, C_END])
        ROWS = sb("ROWS", [1, CH + EXPERTS])
        BIAS = sb("BIAS", [P, CH + EXPERTS])
        BD = sb("BD", [P, P])
        IDENT = sb("IDENT", [P, P])
        UPPER = sb("UPPER", [P, P])
        ONES = sb("ONES", [P, P])
        HEADM = sb("HEADM", [P, P])
        NEGHALF = sb("NEGHALF", [P, TG])
        PAD = sb("PAD", [P, XW])
        IOTA8 = sb("IOTA8", [P, EXPERTS])
        EBASE = sb("EBASE", [P, EXPERTS])
        JIDX = sb("JIDX", [P, SLOT_TILES])
        KV = sb("KV", [P, BATCH, CH])
        KS = sb("KS", [P, BATCH, 1])
        KSB = sb("KSB", [P, BATCH, CH])
        V1 = sb("V1", [P, 2, TG, CH + 1])
        KNT = sb("KNT", [P, 2, TG, CH])
        REC3 = sb("REC3", [P, 2, GT])
        ST = sb("ST", [P, 4, TILES, 6])
        MV = sb("MV", [P, 4, TILES, 2])
        VE = sb("VE", [P, 5, TILES])
        RSTD = sb("RSTD", [P, 5, TILES])
        ALAM = sb("ALAM", [P, 1])
        RSC = sb("RSC", [P, EXPERTS])
        SSQ = sb("SSQ", [P, TILES])
        SQJ = sb("SQJ", [P, 2, CH])
        LG = sb("LG", [P, 2, TILES, EXPERTS])
        V8 = sb("V8", [P, 2, TILES, 8])
        I8 = sb("I8", [P, 2, TILES, 8], u32)
        IF = sb("IF", [P, 2, TILES, TOP])
        OH = sb("OH", [P, 2, TILES, TOP * EXPERTS])
        M = sb("M", [P, 2, TILES, EXPERTS])
        MC = sb("MC", [P, 2, TILES + 1, EXPERTS])
        EX = sb("EX", [P, 2, TILES, 8])
        PR = sb("PR", [P, 2, TILES, 8])
        SP8 = sb("SP8", [P, 2, TG, EXPERTS])
        SPP = sb("SPP", [P, 2, TG, TOP * EXPERTS])
        SL = sb("SL", [P, 2, TILES, TOP], i32)
        CNT = sb("CNT", [P, 2, 4, EXPERTS])
        CNTI = sb("CNTI", [P, 2, 3, EXPERTS], i32)
        TE = sb("TE", [P, 2, SLOT_TILES * EXPERTS])
        TR = sb("TR", [P, 3, SLOT_TILES])
        TBL = sb("TBL", [P, 2, 2, SLOT_TILES], i32)
        xnt = XNT[:, :, :].rearrange("p g n -> p (g n)")
        xn = XN[:, :, :].rearrange("p t c -> p (t c)")
        XS = [xnt[:, i * XW:(i + 1) * XW] for i in range(3)]
        META = sb("META", [P, 2, SLOT_TILES, 2])
        YROW = [sb(f"YROW{i}", [P, 1], i32) for i in range(3)]
        XH = [sb(f"XH{i}", [P, P], f32r) for i in range(3)]
        XL = [sb(f"XL{i}", [P, P], f32r) for i in range(3)]
        H = [xn[:, i * HID0:(i + 1) * HID0] for i in range(3)]
        G0 = [xnt[:, 512 + i * HID1:512 + (i + 1) * HID1] for i in range(3)]
        HH = [sb(f"HH{i}", [P, HID0], f32r) for i in range(3)]
        HL = [sb(f"HL{i}", [P, HID0], f32r) for i in range(3)]
        YS = [xnt[:, 1280 + i * CH:1280 + (i + 1) * CH] for i in range(3)]

        bank = [ctx.enter_context(nc.psum_tensor(f"bank{i}", [P, 512], f32)) for i in range(8)]

        Q, K = BQ[:, 0], BQ[:, 1]

        def part(c, low):
            at = (c if c < CHUNKS0 else c - CHUNKS0) * CHUNK
            if at < UP_COLS:
                at += low * UP_COLS
                return W[:, at:at + CHUNK]
            pairs = W[:, 2 * at:2 * (at + CHUNK)].rearrange("p (n two c) -> p n two c", two=2, c=CH)
            return pairs[:, :, low, :]

        def chunk(c):
            at = (c if c < CHUNKS0 else c - CHUNKS0) * CHUNK
            raw = RAW[:, c % 2, :]
            return raw if at < UP_COLS else raw.rearrange("p (n c) -> p n c", c=CH)

        s = {}
        names = """x0 x1 x2 x3 wqkv wproj small wawx const dest wraw0 wraw1 whi wlo dumped out
          xnT_ps xnT q k v uq uk vsb s1q s1k r1q r1k q1 k1 q2 k2 q3 k3 s3k r3k kn knT_ps knT kv kvb
          num den rden o proj xb x1a dvc bias_ps bias wk bd rsc alam
          t3_ps t3 r_ps i_ps r i e t2 om sq at ix bt yscan yT xc""".split()
        for n in names:
            s[n] = sem("s_" + n)
        for n in """stats aggr ve rstd norm xs0 xs1 xs2 xt xh xl h1 gel h ht hh hl y ys yo0 yo1 yo2
              meta sent yrow ylo ysfree""".split():
            s[n] = sem("s_" + n)
        for l in range(2):
            for n in """nT_ps nT logit_ps lg exps ex sel rank_ps slot row scat count_ps padrow pads table
              ssq mse rms sum
              yl0 yl1 yl2 yl3 res chain""".split():
                s[f"{n}_{l}"] = sem(f"s_{n}_{l}")

        block = ctx.enter_context(nc.Block())
        NCONST = 0

        def sp_ffn(sp, l):
            B, RB = l * SLOT_TILES, l * 16 * (SLOT_TILES // 3)
            sp.wait_ge(s[f"padrow_{l}"], 1)
            for e in range(EXPERTS):
                r = sp.value_load(CNTI[0:1, l, 0, e:e + 1], min_val=e * REG, max_val=e * REG + TOKENS)
                sp.dma_start(slots_d[l][bass.ds(r, P), :], PAD[:, :]).then_inc(s[f"pads_{l}"], 16)
            sp.wait_ge(s[f"table_{l}"], 1)
            sp.wait_ge(s[f"scat_{l}"], 16 * TILES * TOP)
            sp.wait_ge(s[f"pads_{l}"], 16 * EXPERTS)

            def load(j, i, u):
                r = sp.value_load(TBL[0:1, l, 0, j], min_val=0, max_val=XROWS - P)
                if i is not None:
                    sp.wait_ge(s["xt"], B + i * 3 + (u - 2))
                    sp.wait_ge(s["meta"], B + i * 3 + (u - 2))
                sp.dma_start(XS[u][:, :], slots_d[l][bass.ds(r, P), :]).then_inc(s[f"xs{u}"], 16)
            for u in range(3):
                load(slice(u, u + 1), None, u)
            with sp.Fori(1, SLOT_TILES // 3) as i:
                for u in range(3):
                    load(bass.ds(i * 3 + u, 1), i, u)

            for u in range(3):
                sp.wait_ge(s[f"yo{u}"], RB + 16 * (SLOT_TILES // 3))
            for g in range(GROUPS):
                for k in range(TOP):
                    r0 = k * TOKENS + g * GT
                    sp.dma_start(BQ[:, k, g].rearrange("p (t c) -> p t c", t=TG),
                                 ys_d[l][r0:r0 + GT, :].rearrange("(t p) c -> p t c", p=P)
                                 ).then_inc(s[f"yl{g}_{l}"], 16)

        @block.sync
        def _(sp):
            for g in range(GROUPS):
                sp.dma_start(X[:, g * TG:(g + 1) * TG, :], x_v[:, g * TG:(g + 1) * TG, :]
                             ).then_inc(s[f"x{g}"], 16)
                if g == 0:
                    sp.dma_start(WQKV[:, :], wqkv).then_inc(s["wqkv"], 16)

            def weights(first, end):
                for c in range(first, end):
                    if c >= 2:
                        sp.wait_ge(s["whi"], c - 1)
                        sp.wait_ge(s["wlo"], c - 1)
                    sp.dma_start(RAW[:, c % 2, :], wpack[:, c * CHUNK:(c + 1) * CHUNK]
                                 ).then_inc(s[f"wraw{c % 2}"], 16)
            weights(0, CHUNKS0 + 2 if upto >= 4 else CHUNKS0)
            sp.wait_ge(s["const"], 11)
            for l in range(2):
                for d in range(DUMP_TILES):
                    sp.dma_start(slots_d[l][DUMP + d * P:DUMP + (d + 1) * P, :], PAD[:, :]
                                 ).then_inc(s["dumped"], 16)
            sp.wait_ge(s["dumped"], 16 * 2 * DUMP_TILES)
            if upto >= 3:
                sp_ffn(sp, 0)
            if upto >= 4:
                weights(CHUNKS0 + 2, CHUNKS)
            if upto >= 5:
                sp_ffn(sp, 1)
            if upto < 4:
                sp.wait_ge(s["wawx"], 32)
            done = {1: "x1a", 2: "x1a", 3: "res_0", 4: "xc"}.get(upto, "res_1")
            for g in range(GROUPS):
                sp.wait_ge(s[done], g + 1)
                sp.dma_start(out_v[:, g * TG:(g + 1) * TG, :], X[:, g * TG:(g + 1) * TG, :]
                             ).then_inc(s["out"], 16)
            sp.wait_ge(s["out"], 16 * GROUPS)

        def pool_rstd(pool, l, g):
            sl = slice(g * TG, (g + 1) * TG)
            pool.wait_ge(s["ve"], l * GROUPS + g + 1)
            nc.gpsimd.tensor_tensor(RSTD[:, l, sl], VE[:, l, sl], NEGHALF[:, :], ALU.pow
                                    ).then_inc(s["rstd"], 1)

        def pool_route(pool, l, g):
            if l == 1:
                pool.wait_ge(s["mse_1"], g + 1)
                sl = slice(g * TG, (g + 1) * TG)
                nc.gpsimd.tensor_tensor(RSTD[:, 4, sl], VE[:, 4, sl], NEGHALF[:, :], ALU.pow
                                        ).then_inc(s["rms_1"], 1)

        def pool_scatter(pool, l, g):
            pool.wait_ge(s[f"slot_{l}"], g + 1)
            pool.wait_ge(s[f"row_{l}"], g + 1)
            for t in range(g * TG, (g + 1) * TG):
                for k in range(TOP):
                    nc.gpsimd.indirect_dma_start(
                        slots_d[l][:, :], bass.IndirectOffsetOnAxis(SL[:, l, t, k:k + 1], 0),
                        PB[:, k, t, :], None, bounds_check=XROWS - 1, oob_is_err=False
                    ).then_inc(s[f"scat_{l}"], 16)

        def pool_ffn(pool, l):
            B, RB = l * SLOT_TILES, l * 16 * (SLOT_TILES // 3)
            def send(j, u, n, ring):
                if ring is not None:
                    pool.wait_ge(s[f"yo{u}"], RB + ring)
                pool.sem_inc(s["ysfree"], 1)
                pool.wait_ge(s["ys"], B + n)
                pool.sem_inc(s["sent"], 1)
                nc.gpsimd.tensor_copy(YROW[u][:, :], META[:, l, j, 0:1].bitcast(i32)).then_inc(s["yrow"], 1)
                pool.wait_ge(s["yrow"], B + n)
                pool.sem_inc(s["sent"], 1)
                nc.gpsimd.indirect_dma_start(
                    ys_d[l][:, :], bass.IndirectOffsetOnAxis(YROW[u][:, :], 0),
                    YS[u][:, :], None, bounds_check=TOP * TOKENS - 1, oob_is_err=False
                ).then_inc(s[f"yo{u}"], 16)
            for u in range(3):
                send(slice(u, u + 1), u, u + 1, None)
            with pool.Fori(1, SLOT_TILES // 3) as i:
                for u in range(3):
                    send(bass.ds(i * 3 + u, 1), u, i * 3 + (u + 1), i * 16)

        def pool_combine(pool, l):
            for g in range(GROUPS):
                pool.wait_ge(s[f"yl{g}_{l}"], 16 * TOP)
                nc.gpsimd.tensor_tensor(Q[:, g], Q[:, g], K[:, g], ALU.add).then_inc(s[f"sum_{l}"], 1)

        @block.gpsimd
        def _(pool):
            g_ = nc.gpsimd
            c = [0]

            def const(ins, wait=True):
                c[0] += 1
                ins.then_inc(s["const"], 1)
                if wait:
                    pool.wait_ge(s["const"], c[0])
            const(g_.memset(NEGHALF[:, :], -0.5), False)
            const(g_.memset(ONES[:, :], 1.0), False)
            const(g_.memset(IDENT[:, :], 0.0), False)
            const(g_.memset(UPPER[:, :], 1.0), False)
            const(g_.memset(HEADM[:, :], 1.0), False)
            const(g_.memset(PAD[:, :], 0.0))
            const(g_.affine_select(out=IDENT[:, :], in_=IDENT[:, :], compare_op=ALU.not_equal, fill=1.0,
                                   base=0, pattern=[[-1, P]], channel_multiplier=1), False)
            const(g_.affine_select(out=UPPER[:, :], in_=UPPER[:, :], compare_op=ALU.is_gt, fill=0.0,
                                   base=0, pattern=[[1, P]], channel_multiplier=-1), False)
            hm = HEADM[:, :].rearrange("p (h d) -> p h d", d=HD)
            const(g_.affine_select(out=hm, in_=hm, compare_op=ALU.is_ge, fill=0.0,
                                   base=0, pattern=[[-HD, HEADS], [0, HD]], channel_multiplier=1))
            const(g_.affine_select(out=hm, in_=hm, compare_op=ALU.is_ge, fill=0.0,
                                   base=HD - 1, pattern=[[HD, HEADS], [0, HD]], channel_multiplier=-1), False)
            const(g_.memset(PAD[:, CH:CH + 1].bitcast(i32), NO_ROW), False)
            for l in range(2):
                const(g_.memset(MC[:, l, 0, :], 0.0), False)
            for b in range(BATCH):
                const(g_.memset(O[:, b, 0:1], 0.0), False)
                const(g_.memset(O[:, b, SEQ + 1:SEQ + 2], 0.0), False)
            for i in range(2):
                const(g_.memset(V1[:, i, :, CH:CH + 1], 1.0), False)
            const(g_.iota(IOTA8[:, :], pattern=[[1, EXPERTS]], base=0, channel_multiplier=0,
                          allow_small_or_imprecise_dtypes=True), False)
            const(g_.iota(EBASE[:, :], pattern=[[REG, EXPERTS]], base=0, channel_multiplier=0,
                          allow_small_or_imprecise_dtypes=True), False)
            const(g_.iota(JIDX[:, :], pattern=[[1, SLOT_TILES]], base=0, channel_multiplier=0,
                          allow_small_or_imprecise_dtypes=True))
            assert c[0] == NC_TOTAL, c[0]

            for g in range(GROUPS):
                pool_rstd(pool, 0, g)
            wl = [0]

            def low(n, end=CHUNKS0):
                for _ in range(n):
                    k = wl[0]
                    if k >= end:
                        return
                    wl[0] += 1
                    pool.wait_ge(s["whi"], k + 1)
                    g_.tensor_tensor(part(k, 1), chunk(k), part(k, 0).bitcast(f32), ALU.subtract
                                     ).then_inc(s["wlo"], 1)
            for st in range(GROUPS + 1):
                if st >= 1:
                    g = st - 1
                    pool.wait_ge(s["r3k"], g + 1)
                    g_.tensor_tensor(K[:, g], K[:, g], REC3[:, g % 2], ALU.mult).then_inc(s["kn"], 1)
                low(2)
                if st < GROUPS:
                    g = st
                    pool.wait_ge(s["k2"], g + 1)
                    g_.tensor_tensor(K[:, g], SQ[:, 1, g % 2], K[:, g], ALU.mult).then_inc(s["k3"], 1)
                    pool.wait_ge(s["q2"], g + 1)
                    g_.tensor_tensor(Q[:, g], SQ[:, 0, g % 2], Q[:, g], ALU.mult).then_inc(s["q3"], 1)
                    pool.wait_ge(s["bias"], 1)
                    pool.wait_ge(s["norm"], TG * (g + 1))
                    g_.tensor_tensor(X[:, g * TG:(g + 1) * TG, :], X[:, g * TG:(g + 1) * TG, :],
                                     BIAS[:, 0:CH].unsqueeze(1).to_broadcast([P, TG, CH]), ALU.add
                                     ).then_inc(s["xb"], 1)
                low(1)
            low(CHUNKS0)
            if upto >= 2:
                pool.wait_ge(s["o"], GROUPS)
                g_.iota(PB[:, :, :, CH:CH + 1].rearrange("p k t a -> p k (t a)").bitcast(i32),
                        pattern=[[TOKENS, TOP], [P, TILES]], base=0, channel_multiplier=1).then_inc(s["dest"], 1)
                for g in range(GROUPS):
                    pool_rstd(pool, 1, g)
                    if g == 1:
                        pool.wait_ge(s["dest"], 1)
                    if g >= 1:
                        pool_scatter(pool, 0, g - 1)
                pool_scatter(pool, 0, GROUPS - 1)
            if upto >= 3:
                pool_ffn(pool, 0)
                pool_combine(pool, 0)
            if upto >= 4:
                pool.wait_ge(s["y"], SLOT_TILES)
                low(CHUNKS, CHUNKS)
                for g in range(GROUPS):
                    pool_rstd(pool, 2, g)
                for g in range(GROUPS):
                    pool.wait_ge(s["i"], g + 1)
                    g_.tensor_tensor(K[:, g], K[:, g], XNT[:, g], ALU.mult).then_inc(s["ix"], 1)
            if upto >= 5:
                for g in range(GROUPS):
                    pool_rstd(pool, 3, g)
                    pool_route(pool, 1, g)
                    if g >= 1:
                        pool_scatter(pool, 1, g - 1)
                pool_scatter(pool, 1, GROUPS - 1)
                pool_ffn(pool, 1)
                pool_combine(pool, 1)

        def act_copy(act, dst, src, sm):
            nc.scalar.activation(dst, src, ACT.Copy).then_inc(s[sm], 1)

        def act_route(act, l, g):
            act.wait_ge(s[f"nT_ps_{l}"], g + 1)
            act_copy(act, XNT[:, g], bank[g % 2][:, :], f"nT_{l}")
            if l == 1:
                for t in range(g * TG, (g + 1) * TG):
                    act.wait_ge(s["norm"], 3 * TILES + t + 1)
                    if t >= 2:
                        act.wait_ge(s["ssq_1"], t - 1)
                    nc.scalar.activation(SQJ[:, t % 2], PB[:, 0, t, 0:CH], ACT.Square,
                                         accum_out=SSQ[:, t:t + 1]).then_inc(s["ssq_1"], 1)

        def act_exps(act, l, g):
            sl = slice(g * TG, (g + 1) * TG)
            act.wait_ge(s[f"exps_{l}"], g + 1)
            nc.scalar.activation(EX[:, l, sl], EX[:, l, sl], ACT.Exp).then_inc(s[f"ex_{l}"], 1)

        def act_ffn(act, l):
            B, RB = l * SLOT_TILES, l * 16 * (SLOT_TILES // 3)
            F = HID0 if l == 0 else HID1

            def first(u, n):
                act.wait_ge(s["xt"], B + n)
                act_copy(act, XH[u][:, :], bank[0][:, 0:P], "xh")

            def gelu(u, n, old):
                act.wait_ge(s["h1"], B + n)
                if old is not None:
                    act.wait_ge(s["ht"] if l == 0 else s["h"], old)
                if l == 0:
                    nc.scalar.activation(H[u][:, :], bank[1 + u][:, :], ACT.Gelu).then_inc(s["gel"], 1)
                else:
                    nc.scalar.activation(G0[u][:, :], bank[1 + u][:, 0:F], ACT.Gelu_apprx_tanh
                                         ).then_inc(s["gel"], 1)

            def high(u, n, old):
                act.wait_ge(s["ht"], B + n)
                if old is not None:
                    act.wait_ge(s["y"], B + old)
                act_copy(act, HH[u][:, 0:F], bank[4 + u][:, 0:F], "hh")

            def weigh_low(u, j, n):
                act.wait_ge(s["y"], B + n)
                act.wait_ge(s["meta"], B + n)
                act.wait_ge(s["ysfree"], B + n)
                nc.scalar.activation(YS[u][:, :], bank[7][:, CH:2 * CH], ACT.Copy, scale=META[:, l, j, 1]
                                     ).then_inc(s["ylo"], 1)

            def tile(j):
                return slice(j, j + 1)
            first(0, 1)
            for u in range(3):
                first((u + 1) % 3, u + 2)
                gelu(u, u + 1, None)
                if u >= 1:
                    high(u - 1, u, None)
            weigh_low(0, tile(0), 1)
            with act.Fori(1, SLOT_TILES // 3 - 1) as i:
                for u in range(3):
                    first((u + 1) % 3, i * 3 + (u + 2))
                    gelu(u, i * 3 + (u + 1), i * 3 + (u - 2))
                    high((u + 2) % 3, i * 3 + u, i * 3 + (u - 3) if u else None)
                    weigh_low((u + 1) % 3, bass.ds(i * 3 + (u - 2), 1), i * 3 + (u - 1))
            last = SLOT_TILES - 3
            for u in range(3):
                if u < 2:
                    first(u + 1, last + u + 2)
                gelu(u, last + u + 1, last + u - 2)
                high((u + 2) % 3, last + u, last + u - 3)
                weigh_low((u + 1) % 3, tile(last + u - 2), last + u - 1)
            high(2, last + 3, last)
            weigh_low(1, tile(last + 1), last + 2)
            weigh_low(2, tile(last + 2), last + 3)

        @block.scalar
        def _(act):
            a_ = nc.scalar
            act.dma_start(COLS[:, :], cols).then_inc(s["small"], 16)
            act.dma_start(ROWS[:, :], rows).then_inc(s["small"], 16)
            act.dma_start(WP[:, :], wproj).then_inc(s["wproj"], 16)
            act.dma_start(WA[:, :], wa).then_inc(s["wawx"], 16)
            act.dma_start(WX[:, :], wx).then_inc(s["wawx"], 16)
            wh = [0]

            def high(n, end=CHUNKS0):
                for _ in range(n):
                    k = wh[0]
                    if k >= end:
                        return
                    wh[0] += 1
                    act.wait_ge(s[f"wraw{k % 2}"], 16 * (k // 2 + 1))
                    act_copy(act, part(k, 0), chunk(k), "whi")
            act.wait_ge(s["bias_ps"], 1)
            act_copy(act, BIAS[:, :], bank[7][:, 0:CH + EXPERTS], "bias")
            for st in range(GROUPS + 1):
                g = st
                if st < GROUPS:
                    act.wait_ge(s["xnT_ps"], g + 1)
                    act_copy(act, XNT[:, g], bank[g % 2][:, :], "xnT")
                    act.wait_ge(s["v"], g + 1)
                    if g >= 2:
                        act.wait_ge(s["kv"], g - 1)
                    act_copy(act, V1[:, g % 2, :, 0:CH],
                             bank[4][:, :].rearrange("p (t c) -> p t c", t=TG), "vsb")
                    high(1)
                    act.wait_ge(s["k1"], g + 1)
                    if g >= 2:
                        act.wait_ge(s["k3"], g - 1)
                        act.wait_ge(s["q3"], g - 1)
                    a_.activation(SQ[:, 1, g % 2], K[:, g], ACT.Square).then_inc(s["k2"], 1)
                    act.wait_ge(s["q1"], g + 1)
                    a_.activation(SQ[:, 0, g % 2], Q[:, g], ACT.Square).then_inc(s["q2"], 1)
                if st >= 1:
                    g = st - 1
                    act.wait_ge(s["knT_ps"], g + 1)
                    if g >= 2:
                        act.wait_ge(s["kv"], g - 1)
                    act_copy(act, KNT[:, g % 2], bank[5][:, :].rearrange("p (t c) -> p t c", t=TG), "knT")
                high(2)
            high(CHUNKS0)
            if upto >= 2:
                for g in range(GROUPS):
                    act_route(act, 0, g)
                    if g >= 1:
                        act_exps(act, 0, g - 1)
                act_exps(act, 0, GROUPS - 1)
            if upto >= 3:
                act_ffn(act, 0)
            if upto >= 4:
                act.wait_ge(s["y"], SLOT_TILES)
                high(CHUNKS, CHUNKS)
                act.wait_ge(s["small"], 32)
                a_.activation(ALAM[:, :], COLS[:, C_LAM:C_LAM + 1], ACT.Sigmoid).then_inc(s["alam"], 1)
                for g in range(GROUPS):
                    act.wait_ge(s["t3_ps"], g + 1)
                    act_copy(act, XNT[:, g], bank[g % 2][:, :], "t3")
                    if g == 0:
                        act.wait_ge(s["res_0"], GROUPS)
                    act.wait_ge(s["r_ps"], g + 1)
                    a_.activation(Q[:, g], bank[2 + g % 2][:, :], ACT.Sigmoid,
                                  bias=COLS[:, C_BA:C_BA + 1]).then_inc(s["r"], 1)
                    act.wait_ge(s["i_ps"], g + 1)
                    a_.activation(K[:, g], bank[4 + g % 2][:, :], ACT.Sigmoid,
                                  bias=COLS[:, C_BX:C_BX + 1]).then_inc(s["i"], 1)
                act.wait_ge(s["alam"], 1)
                for g in range(GROUPS):
                    act.wait_ge(s["r"], g + 1)
                    a_.activation(Q[:, g], Q[:, g], ACT.Exp, scale=-float(np.log(8.0))).then_inc(s["e"], 1)
                for g in range(GROUPS):
                    act.wait_ge(s["at"], g + 1)
                    act.wait_ge(s["t3_ps"], GROUPS)
                    a_.activation(XN[:, g * TG:(g + 1) * TG], Q[:, g].rearrange("p (t c) -> p t c", t=TG),
                                  ACT.Square).then_inc(s["t2"], 1)
                for g in range(GROUPS):
                    act.wait_ge(s["om"], g + 1)
                    a_.activation(XN[:, g * TG:(g + 1) * TG], XN[:, g * TG:(g + 1) * TG],
                                  ACT.Sqrt).then_inc(s["sq"], 1)
            if upto >= 5:
                for g in range(GROUPS):
                    act_route(act, 1, g)
                    if g >= 1:
                        act_exps(act, 1, g - 1)
                act_exps(act, 1, GROUPS - 1)
                act_ffn(act, 1)

        def transposes(pe, dst, src, g, ln, sm_out):
            for t in range(TG):
                if ln is not None:
                    pe.wait_ge(s["norm"], ln * TILES + g * TG + t + 1)
                last = nc.tensor.transpose(dst[:, t * P:(t + 1) * P], src(t), IDENT[:, :])
            last.then_inc(s[sm_out], 1)

        def pe_route(pe, l, g):
            if g >= 2:
                pe.wait_ge(s[f"nT_{l}"], g - 1)
            transposes(pe, bank[g % 2], lambda t: PB[:, 0, g * TG + t, 0:CH], g, 2 * l + 1,
                       f"nT_ps_{l}")

        def pe_logits(pe, l, g):
            pe.wait_ge(s[f"nT_{l}"], g + 1)
            if l == 1:
                pe.wait_ge(s["rsc"], 1)
            if g >= 2:
                pe.wait_ge(s[f"lg_{l}"], g - 1)
            rw = COLS[:, C_R0:C_R0 + EXPERTS] if l == 0 else RSC[:, :]
            for t in range(TG):
                last = nc.tensor.matmul(bank[2 + g % 2][:, t * EXPERTS:(t + 1) * EXPERTS],
                                        XNT[:, g, t * P:(t + 1) * P], rw, start=True, stop=True)
            last.then_inc(s[f"logit_ps_{l}"], 1)

        def pe_rank(pe, l, g):
            pe.wait_ge(s[f"sel_{l}"], g + 1)
            if g >= 2:
                pe.wait_ge(s[f"slot_{l}"], g - 1)
            o = bank[4 + g % 2][:, 0:TG * EXPERTS]
            nc.tensor.matmul(o, UPPER[:, :], M[:, l, g * TG:(g + 1) * TG, :], start=True, stop=False)
            nc.tensor.matmul(o, ONES[:, :], MC[:, l, g * TG:(g + 1) * TG, :], start=False, stop=True
                             ).then_inc(s[f"rank_ps_{l}"], 1)
            if g == GROUPS - 1:
                nc.tensor.matmul(bank[6][:, 0:EXPERTS], ONES[:, :], MC[:, l, TILES, :], start=True, stop=True
                                 ).then_inc(s[f"count_ps_{l}"], 1)

        def pe_ffn(pe, l):
            B, RB = l * SLOT_TILES, l * 16 * (SLOT_TILES // 3)
            F = HID0 if l == 0 else HID1
            up_h, up_l = (W[:, i * UP_COLS:(i + 1) * UP_COLS].rearrange("p (e n) -> p e n", e=EXPERTS)
                          for i in range(2))
            dn = W[:, 2 * UP_COLS:2 * UP_COLS + 2 * EXPERTS * F].rearrange("p (e k n) -> p e k n", e=EXPERTS, n=2 * CH)
            held = [pe.alloc_register(f"expert{u}_{l}") for u in range(3)]

            def fetch(u, j):
                pe.reg_load(held[u], TBL[0:1, l, 1, j])

            def expert(u):
                return pe.snap(held[u], min_val=0, max_val=EXPERTS - 1)

            def xpose(u, i, old):
                pe.wait_ge(s[f"xs{u}"], RB + i)
                if old is not None:
                    pe.wait_ge(s["xl"], B + old)
                nc.tensor.transpose(bank[0][:, 0:P], XS[u][:, 0:CH], IDENT[:, :]).then_inc(s["xt"], 1)

            def up(u, n, old):
                e = expert(u)
                pe.wait_ge(s["xh"], B + n)
                pe.wait_ge(s["xl"], B + n)
                if old is not None:
                    pe.wait_ge(s["gel"] if l == 0 else s["h"], old)
                o = bank[1 + u][:, :]
                nc.tensor.matmul(o, XH[u][:, :], up_h[:, bass.ds(e, 1), :], start=True, stop=False)
                nc.tensor.matmul(o, XH[u][:, :], up_l[:, bass.ds(e, 1), :], start=False, stop=False)
                nc.tensor.matmul(o, XL[u][:, :], up_h[:, bass.ds(e, 1), :], start=False, stop=True
                                 ).then_inc(s["h1"], 1)

            def hxpose(u, n, old):
                pe.wait_ge(s["gel"] if l == 0 else s["h"], n)
                if old is not None:
                    pe.wait_ge(s["hl"], B + old)
                for k in range(F // P):
                    last = nc.tensor.transpose(bank[4 + u][:, k * P:(k + 1) * P], H[u][:, k * P:(k + 1) * P],
                                               IDENT[:, :])
                last.then_inc(s["ht"], 1)

            def down(u, n, old):
                e = expert(u)
                pe.wait_ge(s["hh"], B + n)
                pe.wait_ge(s["hl"], B + n)
                if old is not None:
                    pe.wait_ge(s["ys"], B + old)
                nk = F // P
                for k in range(nk):
                    ks = slice(k * P, (k + 1) * P)
                    nc.tensor.matmul(bank[7][:, 0:2 * CH], HH[u][:, ks], dn[:, bass.ds(e, 1), k, :],
                                     start=(k == 0), stop=False)
                for k in range(nk):
                    ks = slice(k * P, (k + 1) * P)
                    last = nc.tensor.matmul(bank[7][:, 0:CH], HL[u][:, ks], dn[:, bass.ds(e, 1), k, 0:CH],
                                            start=False, stop=(k == nk - 1))
                last.then_inc(s["y"], 1)

            last = SLOT_TILES - 3
            pe.wait_ge(s[f"table_{l}"], 1)
            fetch(0, slice(0, 1))
            xpose(0, 16, None)
            for u in range(3):
                xpose((u + 1) % 3, 16 * (1 + (u + 1) // 3), u + 1)
                up(u, u + 1, None)
                if u >= 1:
                    hxpose(u - 1, u, None)
                if u == 2:
                    down(0, 1, None)
                fetch((u + 1) % 3, slice(u + 1, u + 2))
            with pe.Fori(1, SLOT_TILES // 3 - 1) as i:
                for u in range(3):
                    xpose((u + 1) % 3, (i + (1 + (u + 1) // 3)) * 16, i * 3 + (u + 1))
                    up(u, i * 3 + (u + 1), i * 3 + (u - 2))
                    hxpose((u + 2) % 3, i * 3 + u, i * 3 + (u - 3) if u else None)
                    down((u + 1) % 3, i * 3 + (u - 1), i * 3 + (u - 2))
                    fetch((u + 1) % 3, bass.ds(i * 3 + (u + 1), 1))
            for u in range(3):
                if u < 2:
                    xpose(u + 1, 16 * (SLOT_TILES // 3), last + u + 1)
                up(u, last + u + 1, last + u - 2)
                hxpose((u + 2) % 3, last + u, last + u - 3)
                down((u + 1) % 3, last + u - 1, last + u - 2)
                if u < 2:
                    fetch(u + 1, slice(last + u + 1, last + u + 2))
            hxpose(2, last + 3, last)
            for u in (1, 2):
                down(u, last + u + 1, last + u)

        @block.tensor
        def _(pe):
            mm = nc.tensor.matmul
            pe.wait_ge(s["const"], NC_TOTAL)
            pe.wait_ge(s["small"], 32)
            pe.wait_ge(s["wproj"], 16)
            pe.wait_ge(s["bd"], 1)
            mm(bank[7][:, 0:CH], BD[:, :], WP[:, :], start=True, stop=False)
            mm(bank[7][:, 0:CH], ONES[0:1, :], ROWS[0:1, 0:CH], start=False, stop=True)
            mm(bank[7][:, CH:CH + EXPERTS], ONES[0:1, :], ROWS[0:1, CH:CH + EXPERTS], start=True, stop=True
               ).then_inc(s["bias_ps"], 1)

            def project(g):
                if g == 0:
                    pe.wait_ge(s["wqkv"], 16)
                if g >= 2:
                    pe.wait_ge(s["xnT"], g - 1)
                transposes(pe, bank[g % 2], lambda t: XN[:, g * TG + t, :], g, 0, "xnT_ps")
                pe.wait_ge(s["xnT"], g + 1)
                if g >= 1:
                    pe.wait_ge(s["uk"], g)
                mm(bank[3][:, :], WQKV[:, CH:2 * CH], XNT[:, g], start=True, stop=True).then_inc(s["k"], 1)
                if g >= 1:
                    pe.wait_ge(s["uq"], g)
                mm(bank[2][:, :], WQKV[:, 0:CH], XNT[:, g], start=True, stop=True).then_inc(s["q"], 1)
                if g >= 1:
                    pe.wait_ge(s["vsb"], g)
                for t in range(TG):
                    last = mm(bank[4][:, t * P:(t + 1) * P], XNT[:, g, t * P:(t + 1) * P],
                              WQKV[:, 2 * CH:3 * CH], start=True, stop=True)
                last.then_inc(s["v"], 1)

            def head_sums(g):
                pe.wait_ge(s["uk"], g + 1)
                if g >= 1:
                    pe.wait_ge(s["r3k"], g)
                mm(bank[6][:, :], HEADM[:, :], K[:, g], start=True, stop=True).then_inc(s["s1k"], 1)
                pe.wait_ge(s["uq"], g + 1)
                if g >= 2:
                    pe.wait_ge(s["knT"], g - 1)
                mm(bank[5][:, :], HEADM[:, :], Q[:, g], start=True, stop=True).then_inc(s["s1q"], 1)

            def cube_sums(g):
                pe.wait_ge(s["k3"], g + 1)
                pe.wait_ge(s["r1k"], g + 1)
                mm(bank[6][:, :], HEADM[:, :], K[:, g], start=True, stop=True).then_inc(s["s3k"], 1)

            def kv_sum(g):
                pe.wait_ge(s["kn"], g + 1)
                pe.wait_ge(s["r1q"], min(g + 2, GROUPS))
                transposes(pe, bank[5], lambda t: K[:, g, t * P:(t + 1) * P], g, None, "knT_ps")
                pe.wait_ge(s["knT"], g + 1)
                pe.wait_ge(s["vsb"], g + 1)
                if g == 0:
                    pe.wait_ge(s["bias"], 1)
                if g == 2:
                    pe.wait_ge(s["kvb"], 1)
                for t in range(TG):
                    last = mm(bank[7][:, 0:CH + 1], KNT[:, g % 2, t, :], V1[:, g % 2, t, :],
                              start=(g % 2 == 0 and t == 0), stop=(g % 2 == 1 and t == TG - 1))
                last.then_inc(s["kv"], 1)

            def attend(g):
                pe.wait_ge(s["kvb"], g // 2 + 1)
                pe.wait_ge(s["q3"], g + 1)
                pe.wait_ge(s["uk"], GROUPS)
                pe.wait_ge(s["uq"], GROUPS)
                if g >= 1:
                    pe.wait_ge(s["rden"], g)
                mm(bank[3][:, :], KSB[:, g // 2], Q[:, g], start=True, stop=True).then_inc(s["den"], 1)
                if g >= 1:
                    pe.wait_ge(s["o"], g)
                mm(bank[2][:, :], KV[:, g // 2], Q[:, g], start=True, stop=True).then_inc(s["num"], 1)

            def output(g):
                pe.wait_ge(s["o"], 2 * (g // 2) + 2)
                pe.wait_ge(s["wk"], 3)
                if g >= 2:
                    pe.wait_ge(s["x1a"], g - 1)
                b, first = g // 2, (g % 2) * GT
                for t in range(TG):
                    for k in range(3):
                        at = first + t * P + k
                        last = mm(bank[g % 2][:, t * P:(t + 1) * P], O[:, b, at:at + P], WK[:, k, :],
                                  start=(k == 0), stop=(k == 2))
                last.then_inc(s["proj"], 1)

            for st in range(GROUPS):
                project(st)
                if st >= 1:
                    cube_sums(st - 1)
                head_sums(st)
                if st >= 1:
                    kv_sum(st - 1)
            for g in (0, 1):
                attend(g)
            cube_sums(GROUPS - 1)
            for g in (0, 1):
                output(g)
            kv_sum(GROUPS - 1)
            for g in (2, 3):
                attend(g)
            for g in (2, 3):
                output(g)

            def routing(l):
                pe_route(pe, l, 0)
                for g in range(GROUPS):
                    pe_logits(pe, l, g)
                    if g + 1 < GROUPS:
                        pe_route(pe, l, g + 1)
                    pe_rank(pe, l, g)
            if upto >= 2:
                pe.wait_ge(s["proj"], GROUPS)
                pe.wait_ge(s["x1a"], GROUPS)
                routing(0)
            if upto >= 3:
                pe_ffn(pe, 0)
            if upto >= 4:
                pe.wait_ge(s["wawx"], 32)
                for g in range(GROUPS):
                    if g >= 2:
                        pe.wait_ge(s["t3"], g - 1)
                    transposes(pe, bank[g % 2], lambda t: XN[:, g * TG + t, :], g, 2, "t3_ps")
                    pe.wait_ge(s["t3"], g + 1)
                    if g >= 2:
                        pe.wait_ge(s["i"], g - 1)
                    mm(bank[2 + g % 2][:, :], WA[:, :], XNT[:, g], start=True, stop=True).then_inc(s["r_ps"], 1)
                    mm(bank[4 + g % 2][:, :], WX[:, :], XNT[:, g], start=True, stop=True).then_inc(s["i_ps"], 1)
                pe.wait_ge(s["ys"], SLOT_TILES)
                for g in range(GROUPS):
                    pe.wait_ge(s["yscan"], g + 1)
                    if g >= 2:
                        pe.wait_ge(s["xc"], g - 1)
                    b, first = g // 2, 1 + (g % 2) * GT
                    transposes(pe, bank[6 + g % 2], lambda t: O[:, b, first + t * P:first + (t + 1) * P], g,
                               None, "yT")
            if upto >= 5:
                routing(1)
                pe_ffn(pe, 1)

        def ln_stats(v, l, g, src):
            for t in range(g * TG, (g + 1) * TG):
                nc.vector.bn_stats(ST[:, l, t], src(t)).then_inc(s["stats"], 1)
            for t in range(g * TG, (g + 1) * TG):
                v.wait_ge(s["stats"], l * TILES + t + 1)
                nc.vector.bn_aggr(MV[:, l, t], ST[:, l, t]).then_inc(s["aggr"], 1)
            v.wait_ge(s["aggr"], l * TILES + TG * (g + 1))
            sl = slice(g * TG, (g + 1) * TG)
            nc.vector.tensor_scalar_add(VE[:, l, sl], MV[:, l, sl, 1], LN_EPS).then_inc(s["ve"], 1)

        def ln_norm(v, l, g, src, dst):
            v.wait_ge(s["rstd"], l * GROUPS + g + 1)
            for t in range(g * TG, (g + 1) * TG):
                nc.vector.tensor_scalar(dst(t), src(t), MV[:, l, t, 0:1], RSTD[:, l, t:t + 1],
                                        ALU.subtract, ALU.mult).then_inc(s["norm"], 1)

        def dve_route(v, l, g, chain):
            V = nc.vector
            sl = slice(g * TG, (g + 1) * TG)

            def link(ins):
                chain[0] += 1
                ins.then_inc(s[f"chain_{l}"], 1)
                v.wait_ge(s[f"chain_{l}"], chain[0])

            def plain(ins):
                chain[0] += 1
                ins.then_inc(s[f"chain_{l}"], 1)
            v.wait_ge(s["norm"], (2 * l + 1) * TILES + TG * (g + 1))
            V.tensor_copy(PB[:, 1, sl, 0:CH], PB[:, 0, sl, 0:CH]).then_inc(s[f"chain_{l}"], 1)
            chain[0] += 1
            logit = bank[2 + g % 2][:, 0:TG * EXPERTS].rearrange("p (t e) -> p t e", e=EXPERTS)
            if l == 1:
                v.wait_ge(s["ssq_1"], TG * (g + 1))
                V.tensor_scalar(VE[:, 4, sl], SSQ[:, sl], 1.0 / CH, RMS_EPS, ALU.mult, ALU.add
                                ).then_inc(s["mse_1"], 1)
                v.wait_ge(s["rms_1"], g + 1)
                link(V.tensor_scalar_mul(SSQ[:, sl], RSTD[:, 4, sl], float(np.float32(CH) ** np.float32(-0.5))))
                v.wait_ge(s[f"logit_ps_{l}"], g + 1)
                V.tensor_tensor(LG[:, l, sl], logit, SSQ[:, sl].unsqueeze(2).to_broadcast([P, TG, EXPERTS]),
                                ALU.mult).then_inc(s[f"lg_{l}"], 1)
            else:
                v.wait_ge(s[f"logit_ps_{l}"], g + 1)
                V.tensor_copy(LG[:, l, sl], logit).then_inc(s[f"lg_{l}"], 1)
            v.wait_ge(s[f"lg_{l}"], g + 1)
            for t in range(g * TG, (g + 1) * TG):
                plain(V.max(V8[:, l, t], LG[:, l, t]))
            v.wait_ge(s[f"chain_{l}"], chain[0])
            for t in range(g * TG, (g + 1) * TG):
                plain(V.max_index(I8[:, l, t], V8[:, l, t], LG[:, l, t]))
            V.tensor_tensor(EX[:, l, sl], V8[:, l, sl], V8[:, l, sl, 0:1].to_broadcast([P, TG, 8]), ALU.subtract
                            ).then_inc(s[f"exps_{l}"], 1)
            v.wait_ge(s[f"chain_{l}"], chain[0])
            link(V.tensor_copy(IF[:, l, sl], I8[:, l, sl, 0:TOP]))
            for k in range(TOP):
                plain(V.tensor_tensor(OH[:, l, sl, k * EXPERTS:(k + 1) * EXPERTS],
                                      IOTA8[:, :].unsqueeze(1).to_broadcast([P, TG, EXPERTS]),
                                      IF[:, l, sl, k:k + 1].to_broadcast([P, TG, EXPERTS]), ALU.is_equal))
            v.wait_ge(s[f"chain_{l}"], chain[0])
            link(V.tensor_tensor(M[:, l, sl], OH[:, l, sl, 0:EXPERTS], OH[:, l, sl, EXPERTS:], ALU.add))
            for t in range(g * TG, (g + 1) * TG):
                if t % TG < TG - 1:
                    link(V.tensor_tensor(MC[:, l, t + 1], MC[:, l, t], M[:, l, t], ALU.add))
                else:
                    V.tensor_tensor(MC[:, l, t + 1], MC[:, l, t], M[:, l, t], ALU.add).then_inc(s[f"sel_{l}"], 1)
            v.wait_ge(s[f"sel_{l}"], g + 1)

        def dve_slots(v, l, g, chain):
            V = nc.vector
            sl = slice(g * TG, (g + 1) * TG)

            def link(ins):
                chain[0] += 1
                ins.then_inc(s[f"chain_{l}"], 1)
                v.wait_ge(s[f"chain_{l}"], chain[0])
            v.wait_ge(s[f"rank_ps_{l}"], g + 1)
            rank = bank[4 + g % 2][:, 0:TG * EXPERTS].rearrange("p (t e) -> p t e", e=EXPERTS)
            sp8, spp = SP8[:, g % 2], SPP[:, g % 2]
            link(V.tensor_tensor(sp8, rank, EBASE[:, :].unsqueeze(1).to_broadcast([P, TG, EXPERTS]), ALU.add))
            for k in range(TOP):
                ks = slice(k * EXPERTS, (k + 1) * EXPERTS)
                link(V.tensor_tensor(spp[:, :, ks], sp8, OH[:, l, sl, ks], ALU.mult))
            with nc.allow_low_precision(reason="whole numbers below 2**24: exact"):
                V.tensor_reduce(SL[:, l, sl], spp.rearrange("p t (k e) -> p t k e", e=EXPERTS), AX.X, ALU.add
                                ).then_inc(s[f"slot_{l}"], 1)
            v.wait_ge(s[f"ex_{l}"], g + 1)
            pr = PR[:, l, sl]
            link(V.tensor_reduce(pr[:, :, 0:1], EX[:, l, sl], AX.X, ALU.add))
            link(V.reciprocal(pr[:, :, 1:2], pr[:, :, 0:1]))
            prob = pr[:, :, 2:4]
            link(V.tensor_tensor(prob, EX[:, l, sl, 0:TOP], pr[:, :, 1:2].to_broadcast([P, TG, TOP]), ALU.mult))
            link(V.tensor_tensor(pr[:, :, 4:5], prob[:, :, 0:1], prob[:, :, 1:2], ALU.add))
            if l == 1:
                link(V.tensor_scalar(pr[:, :, 6:7], pr[:, :, 4:5], 0.0, None, ALU.is_gt))
                link(V.tensor_tensor(pr[:, :, 4:5], pr[:, :, 4:5], pr[:, :, 6:7], ALU.mult))
                link(V.tensor_scalar(pr[:, :, 6:7], pr[:, :, 6:7], -1.0, 1.0, ALU.mult, ALU.add))
                link(V.tensor_tensor(pr[:, :, 4:5], pr[:, :, 4:5], pr[:, :, 6:7], ALU.add))
            link(V.reciprocal(pr[:, :, 5:6], pr[:, :, 4:5]))
            wt = PB[:, :, sl, CH + 1:CH + 2].rearrange("p k t a -> p t (k a)")
            if l == 0:
                V.tensor_tensor(wt, prob, pr[:, :, 5:6].to_broadcast([P, TG, TOP]), ALU.mult
                                ).then_inc(s[f"row_{l}"], 1)
            else:
                link(V.tensor_tensor(prob, prob, pr[:, :, 5:6].to_broadcast([P, TG, TOP]), ALU.mult))
                v.wait_ge(s["slot_1"], g + 1)
                for k in range(TOP):
                    ks = slice(k * EXPERTS, (k + 1) * EXPERTS)
                    link(V.tensor_tensor(spp[:, :, ks], OH[:, l, sl, ks],
                                         BIAS[:, CH:].unsqueeze(1).to_broadcast([P, TG, EXPERTS]), ALU.mult))
                link(V.tensor_reduce(pr[:, :, 6:8], spp.rearrange("p t (k e) -> p t k e", e=EXPERTS), AX.X, ALU.add))
                V.tensor_tensor(wt, prob, pr[:, :, 6:8], ALU.mult).then_inc(s[f"row_{l}"], 1)

        def dve_table(v, l, chain):
            V = nc.vector

            def link(ins):
                chain[0] += 1
                ins.then_inc(s[f"chain_{l}"], 1)
                v.wait_ge(s[f"chain_{l}"], chain[0])
            v.wait_ge(s[f"count_ps_{l}"], 1)
            n = bank[6][:, 0:EXPERTS]
            V.tensor_tensor(CNTI[:, l, 0], n, EBASE[:, :], ALU.add).then_inc(s[f"padrow_{l}"], 1)
            link(V.tensor_scalar_add(CNTI[:, l, 1], n, float(P - 1)))
            link(V.tensor_single_scalar(CNTI[:, l, 2], CNTI[:, l, 1], P.bit_length() - 1, ALU.logical_shift_right))
            link(V.tensor_copy(CNT[:, l, 0], CNTI[:, l, 2]))
            link(V.tensor_tensor_scan(CNT[:, l, 1], ONES[:, 0:EXPERTS], CNT[:, l, 0], 0.0, ALU.mult, ALU.add))
            full = [P, SLOT_TILES, EXPERTS]
            ends = CNT[:, l, 1].unsqueeze(1).to_broadcast(full)
            past = TE[:, 0].rearrange("p (j e) -> p j e", e=EXPERTS)
            begin = TE[:, 1].rearrange("p (j e) -> p j e", e=EXPERTS)
            link(V.tensor_tensor(past, JIDX[:, :].unsqueeze(2).to_broadcast(full), ends, ALU.is_ge))
            link(V.tensor_tensor(begin, past, ends, ALU.mult))
            link(V.tensor_reduce(TR[:, 0], past, AX.X, ALU.add))
            link(V.tensor_reduce(TR[:, 1], begin, AX.X, ALU.max))
            link(V.tensor_tensor(TR[:, 1], JIDX[:, :], TR[:, 1], ALU.subtract))
            link(V.tensor_scalar_mul(TR[:, 1], TR[:, 1], float(P)))
            link(V.scalar_tensor_tensor(TBL[:, l, 0], TR[:, 0], float(REG), TR[:, 1], ALU.mult, ALU.add))
            V.tensor_scalar_min(TBL[:, l, 1], TR[:, 0], float(EXPERTS - 1)).then_inc(s[f"table_{l}"], 1)

        def dve_ffn(v, l):
            B, RB = l * SLOT_TILES, l * 16 * (SLOT_TILES // 3)
            V = nc.vector
            F = HID0 if l == 0 else HID1

            def xlow(u, j, n, ring):
                v.wait_ge(s["xh"], B + n)
                V.tensor_tensor(XL[u][:, :], bank[0][:, 0:P], XH[u][:, :].bitcast(f32), ALU.subtract
                                ).then_inc(s["xl"], 1)
                v.wait_ge(s[f"xs{u}"], RB + ring)
                V.tensor_copy(META[:, l, j, :], XS[u][:, CH:CH + 2].unsqueeze(1)).then_inc(s["meta"], 1)

            def weigh(u, j, n):
                w = META[:, l, j, 1]
                v.wait_ge(s["ylo"], B + n)
                V.scalar_tensor_tensor(YS[u][:, :], bank[7][:, 0:CH], w, YS[u][:, :], ALU.mult, ALU.add
                                       ).then_inc(s["ys"], 1)

            def gate(u, n, old):
                v.wait_ge(s["gel"], B + n)
                if old is not None:
                    v.wait_ge(s["ht"], B + old)
                V.tensor_tensor(H[u][:, 0:F], bank[1 + u][:, F:2 * F], G0[u][:, :], ALU.mult
                                ).then_inc(s["h"], 1)

            def hlow(u, n):
                v.wait_ge(s["hh"], B + n)
                V.tensor_tensor(HL[u][:, 0:F], bank[4 + u][:, 0:F], HH[u][:, 0:F].bitcast(f32), ALU.subtract
                                ).then_inc(s["hl"], 1)

            last, R = SLOT_TILES - 3, SLOT_TILES // 3

            def tile(j):
                return slice(j, j + 1)
            xlow(0, tile(0), 1, 16)
            for u in range(3):
                xlow((u + 1) % 3, tile(u + 1), u + 2, 16 * (1 + (u + 1) // 3))
                if l == 1:
                    gate(u, u + 1, None)
                if u >= 1:
                    hlow(u - 1, u)
            weigh(0, tile(0), 1)
            with v.Fori(1, R - 1) as i:
                for u in range(3):
                    xlow((u + 1) % 3, bass.ds(i * 3 + (u + 1), 1), i * 3 + (u + 2), (i + (1 + (u + 1) // 3)) * 16)
                    hlow((u + 2) % 3, i * 3 + u)
                    if l == 1:
                        gate(u, i * 3 + (u + 1), i * 3 + (u - 2))
                    weigh((u + 1) % 3, bass.ds(i * 3 + (u - 2), 1), i * 3 + (u - 1))
            for u in range(3):
                if u < 2:
                    xlow(u + 1, tile(last + u + 1), last + u + 2, 16 * R)
                hlow((u + 2) % 3, last + u)
                if l == 1:
                    gate(u, last + u + 1, last + u - 2)
                weigh((u + 1) % 3, tile(last + u - 2), last + u - 1)
            hlow(2, last + 3)
            for u in (1, 2):
                weigh(u, tile(last + u), last + u + 1)

        def dve_residual(v, l):
            for g in range(GROUPS):
                v.wait_ge(s[f"sum_{l}"], g + 1)
                sl = slice(g * TG, (g + 1) * TG)
                nc.vector.tensor_tensor(X[:, sl], X[:, sl], Q[:, g].rearrange("p (t c) -> p t c", t=TG), ALU.add
                                        ).then_inc(s[f"res_{l}"], 1)

        @block.vector
        def _(v):
            V = nc.vector
            xrow = lambda t: X[:, t, :]
            v.wait_ge(s["small"], 32)
            v.wait_ge(s["const"], NC_TOTAL)
            V.tensor_scalar_mul(BD[:, :], ONES[:, :], COLS[:, C_BDWC:C_BDWC + 1]).then_inc(s["bd"], 1)
            V.tensor_scalar_mul(RSC[:, :], COLS[:, C_R1:C_R1 + EXPERTS], COLS[:, C_RS:C_RS + 1]
                                ).then_inc(s["rsc"], 1)
            v.wait_ge(s["x0"], 16)
            ln_stats(v, 0, 0, xrow)
            for g in range(GROUPS):
                if g + 1 < GROUPS:
                    v.wait_ge(s[f"x{g + 1}"], 16)
                    ln_stats(v, 0, g + 1, xrow)
                ln_norm(v, 0, g, xrow, lambda t: XN[:, t, :])
            v.wait_ge(s["wproj"], 16)
            V.tensor_scalar_mul(WK[:, 0], WP[:, :], COLS[:, 0:1]).then_inc(s["wk"], 1)
            V.tensor_scalar_mul(WK[:, 2], WP[:, :], COLS[:, 2:3]).then_inc(s["wk"], 1)
            V.scalar_tensor_tensor(WK[:, 1], WP[:, :], COLS[:, 1:2], WP[:, :], ALU.mult, ALU.add
                                   ).then_inc(s["wk"], 1)

            def cube_norm(g):
                v.wait_ge(s["s3k"], g + 1)
                if g >= 2:
                    v.wait_ge(s["kn"], g - 1)
                V.reciprocal(REC3[:, g % 2], bank[6][:, :]).then_inc(s["r3k"], 1)

            def kv_block(b):
                v.wait_ge(s["kv"], 2 * b + 2)
                V.tensor_scalar_add(KS[:, b], bank[7][:, CH:CH + 1], FOCUS_EPS).then_inc(s["dvc"], 1)
                V.tensor_tensor(KV[:, b], bank[7][:, 0:CH], HEADM[:, :], ALU.mult).then_inc(s["dvc"], 1)
                v.wait_ge(s["dvc"], 2 * b + 2)
                V.tensor_scalar_mul(KSB[:, b], HEADM[:, :], KS[:, b]).then_inc(s["kvb"], 1)

            def attended(g):
                v.wait_ge(s["den"], g + 1)
                v.wait_ge(s["q1"], GROUPS)
                V.reciprocal(REC[:, 0, g % 2], bank[3][:, :]).then_inc(s["rden"], 1)
                v.wait_ge(s["num"], g + 1)
                v.wait_ge(s["rden"], g + 1)
                V.tensor_tensor(O[:, g // 2, 1 + (g % 2) * GT:1 + (g % 2 + 1) * GT], bank[2][:, :],
                                REC[:, 0, g % 2], ALU.mult).then_inc(s["o"], 1)

            def projected(g):
                v.wait_ge(s["proj"], g + 1)
                v.wait_ge(s["xb"], g + 1)
                V.tensor_tensor(X[:, g * TG:(g + 1) * TG, :],
                                bank[g % 2][:, :].rearrange("p (t c) -> p t c", t=TG),
                                X[:, g * TG:(g + 1) * TG, :], ALU.add).then_inc(s["x1a"], 1)

            for g in range(GROUPS):
                v.wait_ge(s["k"], g + 1)
                V.tensor_scalar(K[:, g], bank[3][:, :], 0.0, FOCUS_EPS, ALU.max, ALU.add).then_inc(s["uk"], 1)
                v.wait_ge(s["q"], g + 1)
                V.tensor_scalar(Q[:, g], bank[2][:, :], 0.0, FOCUS_EPS, ALU.max, ALU.add).then_inc(s["uq"], 1)
                if g >= 1:
                    cube_norm(g - 1)
                v.wait_ge(s["s1k"], g + 1)
                V.reciprocal(REC[:, 1, g % 2], bank[6][:, :]).then_inc(s["r1k"], 1)
                v.wait_ge(s["s1q"], g + 1)
                V.reciprocal(REC[:, 0, g % 2], bank[5][:, :]).then_inc(s["r1q"], 1)
                v.wait_ge(s["r1k"], g + 1)
                V.tensor_tensor(K[:, g], K[:, g], REC[:, 1, g % 2], ALU.mult).then_inc(s["k1"], 1)
                v.wait_ge(s["r1q"], g + 1)
                V.tensor_tensor(Q[:, g], Q[:, g], REC[:, 0, g % 2], ALU.mult).then_inc(s["q1"], 1)
                if g == 2:
                    kv_block(0)
            attended(0)
            attended(1)
            cube_norm(GROUPS - 1)
            projected(0)
            projected(1)
            kv_block(1)
            attended(2)
            attended(3)
            projected(2)
            projected(3)
            pbrow = lambda t: PB[:, 0, t, 0:CH]

            def routing(l, before):
                chain = [0]
                before(0)
                ln_stats(v, 2 * l + 1, 0, xrow)
                for g in range(GROUPS):
                    if g + 1 < GROUPS:
                        before(g + 1)
                        ln_stats(v, 2 * l + 1, g + 1, xrow)
                    ln_norm(v, 2 * l + 1, g, xrow, pbrow)
                    if g >= 1:
                        dve_slots(v, l, g - 1, chain)
                    dve_route(v, l, g, chain)
                dve_slots(v, l, GROUPS - 1, chain)
                dve_table(v, l, chain)
            if upto >= 2:
                v.wait_ge(s["x1a"], 2)

                def before0(g):
                    v.wait_ge(s["x1a"], g + 1)
                routing(0, before0)
            if upto >= 3:
                dve_ffn(v, 0)
                dve_residual(v, 0)
            if upto >= 4:
                v.wait_ge(s["res_0"], 1)
                ln_stats(v, 2, 0, xrow)
                for g in range(GROUPS):
                    if g + 1 < GROUPS:
                        v.wait_ge(s["res_0"], g + 2)
                        ln_stats(v, 2, g + 1, xrow)
                    ln_norm(v, 2, g, xrow, lambda t: XN[:, t, :])
                v.wait_ge(s["alam"], 1)
                for g in range(GROUPS):
                    v.wait_ge(s["e"], g + 1)
                    V.tensor_scalar_mul(Q[:, g], Q[:, g], ALAM[:, :]).then_inc(s["at"], 1)
                for g in range(GROUPS):
                    v.wait_ge(s["t2"], g + 1)
                    V.tensor_scalar(XN[:, g * TG:(g + 1) * TG], XN[:, g * TG:(g + 1) * TG], -1.0, 1.0,
                                    ALU.mult, ALU.add).then_inc(s["om"], 1)

                def recurrence(g):
                    v.wait_ge(s["sq"], g + 1)
                    v.wait_ge(s["ix"], g + 1)
                    V.tensor_tensor(K[:, g], K[:, g], XN[:, g * TG:(g + 1) * TG].rearrange("p t c -> p (t c)"),
                                    ALU.mult).then_inc(s["bt"], 1)
                    v.wait_ge(s["bt"], g + 1)
                    v.wait_ge(s["at"], g + 1)
                    if g:
                        v.wait_ge(s["yscan"], g)
                    b, first = g // 2, 1 + (g % 2) * GT
                    V.tensor_tensor_scan(O[:, b, first:first + GT], Q[:, g], K[:, g],
                                         0.0 if g % 2 == 0 else O[:, b, first - 1:first],
                                         ALU.mult, ALU.add).then_inc(s["yscan"], 1)

                def added(g):
                    v.wait_ge(s["yT"], g + 1)
                    V.tensor_tensor(X[:, g * TG:(g + 1) * TG, :],
                                    bank[6 + g % 2][:, :].rearrange("p (t c) -> p t c", t=TG),
                                    X[:, g * TG:(g + 1) * TG, :], ALU.add).then_inc(s["xc"], 1)
                for g in range(GROUPS):
                    recurrence(g)
                if upto == 4:
                    for g in range(GROUPS):
                        added(g)
            if upto >= 5:
                def before1(g):
                    added(g)
                    v.wait_ge(s["xc"], g + 1)
                routing(1, before1)
                dve_ffn(v, 1)
                dve_residual(v, 1)


NC_TOTAL = 22


_INS = ["x", "wqkv", "wproj", "cols", "rows", "wpack", "wa", "wx"]


def layout(i):
    import numpy as np
    c = np.ascontiguousarray
    cols = np.concatenate([
        i["L0_attn_w_dwc"], i["L0_attn_b_dwc"][:, None], i["L1_attn_ba"][:, None], i["L1_attn_bx"][:, None],
        i["L1_attn_Lam"][:, None], i["L1_ffn_router_scale"][:, None], i["L0_ffn_router_w"].T,
        i["L1_ffn_router_w"]], axis=1)
    rows = np.concatenate([i["L0_attn_b_proj"], i["L1_ffn_per_expert_scale"]])[None, :]
    w1 = i["L0_ffn_w1"].transpose(1, 0, 2).reshape(P, -1)
    w2 = i["L0_ffn_w2"].reshape(EXPERTS, HID0 // P, P, CH).transpose(2, 0, 1, 3).reshape(P, -1)
    gate = i["L1_ffn_gating_w"].transpose(3, 0, 1, 2).reshape(P, -1)
    lin = i["L1_ffn_linear_w"].reshape(EXPERTS, HID1 // P, P, CH).transpose(2, 0, 1, 3).reshape(P, -1)
    return {"x": c(i["L0_attn_x"]), "wqkv": c(i["L0_attn_w_qkv"].T), "wproj": c(i["L0_attn_w_proj"].T),
            "cols": c(cols), "rows": c(rows), "wpack": c(np.concatenate([w1, w2, gate, lin], axis=1)),
            "wa": c(i["L1_attn_Wa"]), "wx": c(i["L1_attn_Wx"])}


def kernel(**inputs):
    import numpy as _np
    import concourse.bacc as _bacc
    from concourse import mybir as _mybir
    from concourse.bass_utils import run_bass_kernel_spmd as _run

    nc = _bacc.Bacc("TRN2", target_bir_lowering=False, num_devices=1)
    laid = layout({k: _np.asarray(v) for k, v in inputs.items()})
    args = [nc.dram_tensor(f"in_{n}", laid[n].shape, _mybir.dt.from_np(laid[n].dtype), kind="ExternalInput").ap()
            for n in _INS]
    out = nc.dram_tensor("out_0", (BATCH, SEQ, CH), _mybir.dt.float32, kind="ExternalOutput").ap()
    two_layers(nc, *args, out, upto=UPTO)
    r = _run(nc, [{f"in_{n}": laid[n] for n in _INS}], core_ids=[0])
    return r.results[0]["out_0"]


UPTO = 5
```

```python
import concourse.bass as bass
from concourse import mybir
from contextlib import ExitStack

BATCH, SEQ, CH = 2, 1024, 128
TOKENS = BATCH * SEQ
P = 128
TILES = TOKENS // P
TG = 4
GROUPS = TILES // TG
GT = TG * P
BT = TILES // BATCH
BG = GROUPS // BATCH
HEADS = 16
HD = CH // HEADS
FOCUS_EPS = 1e-6
LN_EPS = 1e-5
RMS_EPS = 1e-6
EXPERTS, TOP = 8, 2
HID0, HID1 = 512, 256
SLOT_TILES = TOKENS * TOP // P + EXPERTS - 1
PEEL, STEPS = 3, 6
ROUNDS = (SLOT_TILES - PEEL - 1) // STEPS
LAST = PEEL + ROUNDS * STEPS
REG = TOKENS + P
DUMP = EXPERTS * REG
DUMP_TILES = SLOT_TILES - TOKENS * TOP // P + 1
XROWS = DUMP + DUMP_TILES * P
XW = CH + 2
NO_ROW = 1 << 20
CHUNK = 1024
WCOLS = EXPERTS * (HID0 + HID0 + 2 * HID1 + HID1)
CHUNKS = WCOLS // CHUNK
CHUNKS0 = EXPERTS * 2 * HID0 // CHUNK
WRES = EXPERTS * 2 * HID0
UP_COLS = EXPERTS * 512
C_DWC, C_BDWC, C_BA, C_BX, C_LAM, C_RS, C_R0, C_R1, C_END = 0, 3, 4, 5, 6, 7, 8, 16, 24


def two_layers(nc, x, wqkv, wproj, cols, rows, wpack, wa, wx, out, upto=99):
    f32, f32r, i32, u32 = mybir.dt.float32, mybir.dt.float32r, mybir.dt.int32, mybir.dt.uint32
    ALU, ACT, AX = mybir.AluOpType, mybir.ActivationFunctionType, mybir.AxisListType
    import numpy as np

    x_v = x.rearrange("b (t p) c -> p (b t) c", p=P)
    out_v = out.rearrange("b (t p) c -> p (b t) c", p=P)
    slots_d = [nc.dram_tensor(f"slots{l}", [XROWS, XW], f32).ap() for l in range(2)]
    ys_d = [nc.dram_tensor(f"expert_out{l}", [TOP * TOKENS, CH], f32).ap() for l in range(2)]

    ctx = ExitStack()
    with ctx:
        def sb(name, shape, dt=f32):
            return ctx.enter_context(nc.sbuf_tensor(name, shape, dt))

        def sem(name):
            return ctx.enter_context(nc.semaphore(name))

        X = sb("X", [P, TILES, CH])
        XN = sb("XN", [P, TILES, CH])
        XNT = sb("XNT", [P, GROUPS, GT])
        BQ = sb("BQ", [P, 2, GROUPS, GT])
        O = sb("O", [P, BATCH, SEQ + 2])
        PBF = sb("PBF", [P, TOP * TILES * XW])
        PB = PBF[:, :].rearrange("p (k t c) -> p k t c", k=TOP, t=TILES)
        SQ = PBF[:, 0:4 * GT].rearrange("p (a b n) -> p a b n", a=2, b=2)
        OTM = PBF[:, 4 * GT:6 * GT].rearrange("p (b t c) -> p b t c", b=2, t=TG)
        W = sb("W", [P, 2 * WRES], f32r)
        RAW = sb("RAW", [P, 2, CHUNK])
        WQKV = sb("WQKV", [P, 3 * CH])
        WP = sb("WP", [P, CH])
        WK = sb("WK", [P, 3, CH])
        WA = sb("WA", [P, CH])
        WX = sb("WX", [P, CH])
        COLS = sb("COLS", [P, C_END])
        ROWS = sb("ROWS", [1, CH + EXPERTS])
        BIAS = sb("BIAS", [P, CH + EXPERTS])
        BD = sb("BD", [P, P])
        IDENT = sb("IDENT", [P, P])
        NLOWER = sb("NLOWER", [P, P])
        RESET = sb("RESET", [P, EXPERTS, BT])
        ONES = sb("ONES", [P, P])
        HEADM = sb("HEADM", [P, P])
        NEGHALF = sb("NEGHALF", [P, TG])
        PAD = sb("PAD", [P, XW])
        IOTA8 = sb("IOTA8", [P, EXPERTS])
        EBASE = sb("EBASE", [P, EXPERTS])
        JIDX = sb("JIDX", [P, SLOT_TILES])
        KV = sb("KV", [P, BATCH, CH])
        KSB = sb("KSB", [P, BATCH, HEADS])
        VR = sb("VR", [P, 2, TG, CH + HEADS])
        S3 = sb("S3", [P, 2, TG, HEADS])
        RD = sb("RD", [P, 2, TG, HEADS])
        EPSC = sb("EPSC", [P, 1])
        ST = sb("ST", [P, 4, TILES, 6])
        MV = sb("MV", [P, 4, TILES, 2])
        VE = sb("VE", [P, 5, TILES])
        RSTD = sb("RSTD", [P, 5, TILES])
        ALAM = sb("ALAM", [P, 1])
        RSC = sb("RSC", [P, EXPERTS])
        RMS = sb("RMS", [P, TILES])
        LG = sb("LG", [P, 2, TILES, EXPERTS])
        V8 = sb("V8", [P, 2, TILES, 8])
        I8 = sb("I8", [P, 2, TILES, 8], u32)
        IF = sb("IF", [P, 2, TILES, TOP])
        OH = sb("OH", [P, 2, TILES, TOP, EXPERTS])
        M = sb("M", [P, 2, BATCH, EXPERTS, BT])
        MC = sb("MC", [P, 2, BATCH, EXPERTS, BT])
        EX = sb("EX", [P, 2, TILES, 8])
        PR = sb("PR", [P, 2, TILES, 8])
        SP8 = sb("SP8", [P, 2, BT, EXPERTS])
        SPP = sb("SPP", [P, 2, BT, TOP, EXPERTS])
        SL = sb("SL", [P, 2, TILES, TOP], i32)
        CNT = sb("CNT", [P, 2, 4, EXPERTS])
        CNTI = sb("CNTI", [P, 2, 3, EXPERTS], i32)
        TE = sb("TE", [P, 2, SLOT_TILES * EXPERTS])
        TR = sb("TR", [P, 3, SLOT_TILES])
        TBL = sb("TBL", [P, 2, 2, SLOT_TILES], i32)
        xnt = XNT[:, :, :].rearrange("p g n -> p (g n)")
        xn = XN[:, :, :].rearrange("p t c -> p (t c)")
        XS = [xnt[:, i * XW:(i + 1) * XW] for i in range(3)]
        META = sb("META", [P, 2, SLOT_TILES, 2])
        YROW = [sb(f"YROW{i}", [P, 1], i32) for i in range(3)]
        XH = [sb(f"XH{i}", [P, P], f32r) for i in range(3)]
        XL = [sb(f"XL{i}", [P, P], f32r) for i in range(3)]
        H = [xn[:, i * HID0:(i + 1) * HID0] for i in range(3)]
        G0 = [xnt[:, 512 + i * HID1:512 + (i + 1) * HID1] for i in range(3)]
        HH = [sb(f"HH{i}", [P, HID0], f32r) for i in range(3)]
        HL = [sb(f"HL{i}", [P, HID0], f32r) for i in range(3)]
        YS = [xnt[:, 1280 + i * CH:1280 + (i + 1) * CH] for i in range(3)]

        bank = [ctx.enter_context(nc.psum_tensor(f"bank{i}", [P, 512], f32)) for i in range(8)]

        Q, K = BQ[:, 0], BQ[:, 1]
        v_bank = [bank[3], bank[7]] * 2
        num_bank = [bank[6], bank[4]] * 2
        den_bank = [bank[2], bank[1], bank[2], bank[5]]
        turn_bank = [[bank[0], bank[1], bank[3], bank[7]], [bank[0], bank[1]] * 2]
        logit_bank = [[bank[6], bank[2]], [bank[2], bank[3]]]
        rank_bank = [[bank[4], bank[5]], [bank[4], bank[5]]]

        def part(c, low):
            at = (c if c < CHUNKS0 else c - CHUNKS0) * CHUNK
            if at < UP_COLS:
                at += low * UP_COLS
                return W[:, at:at + CHUNK]
            pairs = W[:, 2 * at:2 * (at + CHUNK)].rearrange("p (n two c) -> p n two c", two=2, c=CH)
            return pairs[:, :, low, :]

        def chunk(c):
            at = (c if c < CHUNKS0 else c - CHUNKS0) * CHUNK
            raw = RAW[:, c % 2, :]
            return raw if at < UP_COLS else raw.rearrange("p (n c) -> p n c", c=CH)

        s = {}
        names = """x0 x1 x2 x3 wqkv wproj small wawx const dest wraw0 wraw1 whi wlo dumped out
          xnT_ps xnT q k v rq rk q2 k2 q3 k3 s3 r3 vr kv kvb
          num rden ot oT_ps o proj xb x1a bias_ps bias wk bd rsc alam
          t3_ps t3 r_ps i_ps r i e t2 sq at msq ix bt yscan yT xc""".split()
        for n in names:
            s[n] = sem("s_" + n)
        for n in """stats aggr ve rstd norm xs0 xs1 xs2 xt xh xl h1 gel h ht hh hl y ys yo0 yo1 yo2
              meta sent yrow ylo ysfree""".split():
            s[n] = sem("s_" + n)
        for l in range(2):
            for n in """nT_ps nT logit_ps lg exps ex sel rank_ps slot row copy scat padrow pads table
              mse rms sum
              yl0 yl1 yl2 yl3 res chain""".split():
                s[f"{n}_{l}"] = sem(f"s_{n}_{l}")

        block = ctx.enter_context(nc.Block())
        NCONST = 0

        def tile(c, i):
            return c if i is None else i * STEPS + c

        def column(c, i):
            return slice(c, c + 1) if i is None else bass.ds(i * STEPS + c, 1)

        def dma_count(c, i):
            return 16 * (c // 3 + 1) if i is None else (i * (STEPS // 3) + (c // 3 + 1)) * 16

        def pipeline(engine, step):
            for c in range(PEEL):
                step(c, None)
            with engine.Fori(0, ROUNDS) as i:
                for c in range(PEEL, PEEL + STEPS):
                    step(c, i)
            for c in range(LAST, SLOT_TILES):
                step(c, None)

        def sp_ffn(sp, l):
            B, RB = l * SLOT_TILES, l * 16 * (SLOT_TILES // 3)
            sp.wait_ge(s[f"padrow_{l}"], 1)
            for e in range(EXPERTS):
                r = sp.value_load(CNTI[0:1, l, 0, e:e + 1], min_val=e * REG, max_val=e * REG + TOKENS)
                sp.dma_start(slots_d[l][bass.ds(r, P), :], PAD[:, :]).then_inc(s[f"pads_{l}"], 16)
            sp.wait_ge(s[f"table_{l}"], 1)
            sp.wait_ge(s[f"scat_{l}"], 16 * TILES * TOP)
            sp.wait_ge(s[f"pads_{l}"], 16 * EXPERTS)

            def load(c, i):
                row = sp.value_load(TBL[0:1, l, 0, column(c, i)], min_val=0, max_val=XROWS - P)
                if c >= 3:
                    sp.wait_ge(s["meta"], tile(c, i) + (B - 2))
                sp.dma_start(XS[c % 3][:, :], slots_d[l][bass.ds(row, P), :]).then_inc(s[f"xs{c % 3}"], 16)
            pipeline(sp, load)

            for u in range(3):
                sp.wait_ge(s[f"yo{u}"], RB + 16 * (SLOT_TILES // 3))
            for g in range(GROUPS):
                for k in range(TOP):
                    r0 = k * TOKENS + g * GT
                    sp.dma_start(BQ[:, k, g].rearrange("p (t c) -> p t c", t=TG),
                                 ys_d[l][r0:r0 + GT, :].rearrange("(t p) c -> p t c", p=P)
                                 ).then_inc(s[f"yl{g}_{l}"], 16)

        @block.sync
        def _(sp):
            for g in range(GROUPS):
                sp.dma_start(X[:, g * TG:(g + 1) * TG, :], x_v[:, g * TG:(g + 1) * TG, :]
                             ).then_inc(s[f"x{g}"], 16)
                if g == 0:
                    sp.dma_start(WQKV[:, :], wqkv).then_inc(s["wqkv"], 16)

            def weights(first, end):
                for c in range(first, end):
                    if c >= 2:
                        sp.wait_ge(s["whi"], c - 1)
                        sp.wait_ge(s["wlo"], c - 1)
                    sp.dma_start(RAW[:, c % 2, :], wpack[:, c * CHUNK:(c + 1) * CHUNK]
                                 ).then_inc(s[f"wraw{c % 2}"], 16)
            weights(0, CHUNKS0 + 2 if upto >= 4 else CHUNKS0)
            sp.wait_ge(s["const"], 11)
            for l in range(2):
                for d in range(DUMP_TILES):
                    sp.dma_start(slots_d[l][DUMP + d * P:DUMP + (d + 1) * P, :], PAD[:, :]
                                 ).then_inc(s["dumped"], 16)
            sp.wait_ge(s["dumped"], 16 * 2 * DUMP_TILES)
            if upto >= 3:
                sp_ffn(sp, 0)
            if upto >= 4:
                weights(CHUNKS0 + 2, CHUNKS)
            if upto >= 5:
                sp_ffn(sp, 1)
            if upto < 4:
                sp.wait_ge(s["wawx"], 32)
            done = {1: "x1a", 2: "x1a", 3: "res_0", 4: "xc"}.get(upto, "res_1")
            for g in range(GROUPS):
                sp.wait_ge(s[done], g + 1)
                sp.dma_start(out_v[:, g * TG:(g + 1) * TG, :], X[:, g * TG:(g + 1) * TG, :]
                             ).then_inc(s["out"], 16)
            sp.wait_ge(s["out"], 16 * GROUPS)

        def pool_rstd(pool, l, g):
            sl = slice(g * TG, (g + 1) * TG)
            pool.wait_ge(s["ve"], l * GROUPS + g + 1)
            nc.gpsimd.tensor_tensor(RSTD[:, l, sl], VE[:, l, sl], NEGHALF[:, :], ALU.pow
                                    ).then_inc(s["rstd"], 1)

        def pool_rms(pool, b):
            sl = slice(b * BT, (b + 1) * BT)
            pool.wait_ge(s["mse_1"], b + 1)
            nc.gpsimd.tensor_tensor(RSTD[:, 4, sl], VE[:, 4, sl],
                                    NEGHALF[:, 0:1].to_broadcast([P, BT]), ALU.pow).then_inc(s["rms_1"], 1)

        def pool_scatter(pool, l, b, tiles):
            pool.wait_ge(s[f"slot_{l}"], b + 1)
            pool.wait_ge(s[f"row_{l}"], b + 1)
            pool.wait_ge(s[f"copy_{l}"], b + 1)
            for t in range(b * BT + tiles.start, b * BT + tiles.stop):
                for k in range(TOP):
                    nc.gpsimd.indirect_dma_start(
                        slots_d[l][:, :], bass.IndirectOffsetOnAxis(SL[:, l, t, k:k + 1], 0),
                        PB[:, k, t, :], None, bounds_check=XROWS - 1, oob_is_err=False
                    ).then_inc(s[f"scat_{l}"], 16)

        def pool_ffn(pool, l):
            B, RB = l * SLOT_TILES, l * 16 * (SLOT_TILES // 3)
            def send(c, i):
                if c >= 3:
                    pool.wait_ge(s[f"yo{c % 3}"], dma_count(c - 3, i) + RB)
                pool.sem_inc(s["ysfree"], 1)
                pool.wait_ge(s["yrow"], tile(c, i) + (B + 1))
                pool.sem_inc(s["sent"], 1)
                nc.gpsimd.indirect_dma_start(
                    ys_d[l][:, :], bass.IndirectOffsetOnAxis(YROW[c % 3][:, :], 0),
                    YS[c % 3][:, :], None, bounds_check=TOP * TOKENS - 1, oob_is_err=False
                ).then_inc(s[f"yo{c % 3}"], 16)
            pipeline(pool, send)

        def pool_sum(pool, l, g):
            pool.wait_ge(s[f"yl{g}_{l}"], 16 * TOP)
            nc.gpsimd.tensor_tensor(Q[:, g], Q[:, g], K[:, g], ALU.add).then_inc(s[f"sum_{l}"], 1)

        @block.gpsimd
        def _(pool):
            g_ = nc.gpsimd
            c = [0]

            def const(ins, wait=True):
                c[0] += 1
                ins.then_inc(s["const"], 1)
                if wait:
                    pool.wait_ge(s["const"], c[0])
            const(g_.memset(NEGHALF[:, :], -0.5), False)
            const(g_.memset(ONES[:, :], 1.0), False)
            const(g_.memset(IDENT[:, :], 0.0), False)
            const(g_.memset(NLOWER[:, :], -1.0), False)
            const(g_.memset(RESET[:, :, :], 1.0), False)
            const(g_.memset(HEADM[:, :], 1.0), False)
            const(g_.memset(PAD[:, :], 0.0))
            const(g_.affine_select(out=IDENT[:, :], in_=IDENT[:, :], compare_op=ALU.not_equal, fill=1.0,
                                   base=0, pattern=[[-1, P]], channel_multiplier=1), False)
            const(g_.affine_select(out=NLOWER[:, :], in_=NLOWER[:, :], compare_op=ALU.is_ge, fill=0.0,
                                   base=0, pattern=[[-1, P]], channel_multiplier=1), False)
            const(g_.memset(RESET[:, :, 0:1], 0.0), False)
            hm = HEADM[:, :].rearrange("p (h d) -> p h d", d=HD)
            const(g_.affine_select(out=hm, in_=hm, compare_op=ALU.is_ge, fill=0.0,
                                   base=0, pattern=[[-HD, HEADS], [0, HD]], channel_multiplier=1))
            const(g_.affine_select(out=hm, in_=hm, compare_op=ALU.is_ge, fill=0.0,
                                   base=HD - 1, pattern=[[HD, HEADS], [0, HD]], channel_multiplier=-1), False)
            const(g_.memset(PAD[:, CH:CH + 1], float(NO_ROW)), False)
            for b in range(BATCH):
                const(g_.memset(O[:, b, 0:1], 0.0), False)
                const(g_.memset(O[:, b, SEQ + 1:SEQ + 2], 0.0), False)
            const(g_.memset(EPSC[:, :], FOCUS_EPS), False)
            const(g_.iota(IOTA8[:, :], pattern=[[1, EXPERTS]], base=0, channel_multiplier=0,
                          allow_small_or_imprecise_dtypes=True), False)
            const(g_.iota(EBASE[:, :], pattern=[[REG, EXPERTS]], base=0, channel_multiplier=0,
                          allow_small_or_imprecise_dtypes=True), False)
            const(g_.iota(JIDX[:, :], pattern=[[1, SLOT_TILES]], base=0, channel_multiplier=0,
                          allow_small_or_imprecise_dtypes=True))
            assert c[0] == NC_TOTAL, c[0]

            for g in range(GROUPS):
                pool_rstd(pool, 0, g)
            wl = [0]

            def low(n, end=CHUNKS0):
                for _ in range(n):
                    k = wl[0]
                    if k >= end:
                        return
                    wl[0] += 1
                    pool.wait_ge(s["whi"], k + 1)
                    g_.tensor_tensor(part(k, 1), chunk(k), part(k, 0).bitcast(f32), ALU.subtract
                                     ).then_inc(s["wlo"], 1)
            pool.wait_ge(s["bias"], 1)
            for g in range(GROUPS):
                pool.wait_ge(s["norm"], TG * (g + 1))
                g_.tensor_tensor(X[:, g * TG:(g + 1) * TG, :], X[:, g * TG:(g + 1) * TG, :],
                                 BIAS[:, 0:CH].unsqueeze(1).to_broadcast([P, TG, CH]), ALU.add
                                 ).then_inc(s["xb"], 1)
                low(1)
            if upto < 2:
                low(CHUNKS0)
            if upto >= 2:
                pool_rstd(pool, 1, 0)
                pool_rstd(pool, 1, 1)
                pool.wait_ge(s["o"], GROUPS)
                g_.iota(PB[:, :, :, CH:CH + 1].rearrange("p k t a -> p k (t a)"),
                        pattern=[[TOKENS, TOP], [P, TILES]], base=0, channel_multiplier=1,
                        allow_small_or_imprecise_dtypes=True).then_inc(s["dest"], 1)
                low(CHUNKS0)
                pool_rstd(pool, 1, 2)
                pool_rstd(pool, 1, 3)
                pool.wait_ge(s["dest"], 1)
                for b in range(BATCH):
                    pool_scatter(pool, 0, b, range(BT))
            if upto >= 3:
                pool_ffn(pool, 0)
                if upto == 3:
                    for g in range(GROUPS):
                        pool_sum(pool, 0, g)
            if upto >= 4:
                pool_sum(pool, 0, 0)
                for g in range(1, GROUPS):
                    pool_sum(pool, 0, g)
                    pool_rstd(pool, 2, g - 1)
                pool_rstd(pool, 2, GROUPS - 1)
                for g in range(GROUPS):
                    pool.wait_ge(s["i"], g + 1)
                    g_.tensor_tensor(K[:, g], K[:, g], XNT[:, g], ALU.mult).then_inc(s["ix"], 1)
            if upto >= 5:
                pool_rstd(pool, 3, 0)
                pool_rstd(pool, 3, 1)
                pool_rms(pool, 0)
                pool_rstd(pool, 3, 2)
                pool_rstd(pool, 3, 3)
                pool_scatter(pool, 1, 0, range(0, 2))
                pool_rms(pool, 1)
                pool_scatter(pool, 1, 0, range(2, BT))
                pool_scatter(pool, 1, 1, range(BT))
                pool_ffn(pool, 1)
                for g in range(GROUPS):
                    pool_sum(pool, 1, g)

        def act_copy(act, dst, src, sm):
            nc.scalar.activation(dst, src, ACT.Copy).then_inc(s[sm], 1)

        def act_turned(act, l, g):
            act.wait_ge(s[f"nT_ps_{l}"], g + 1)
            act_copy(act, XNT[:, g], turn_bank[l][g][:, :], f"nT_{l}")

        def act_second(act, l, b):
            sl = slice(b * BT, (b + 1) * BT)
            act.wait_ge(s["norm"], (2 * l + 1) * TILES + BT * (b + 1))
            act_copy(act, PB[:, 1, sl, 0:CH], PB[:, 0, sl, 0:CH], f"copy_{l}")

        def act_exps(act, l, b):
            sl = slice(b * BT, (b + 1) * BT)
            act.wait_ge(s[f"exps_{l}"], b + 1)
            nc.scalar.activation(EX[:, l, sl], EX[:, l, sl], ACT.Exp).then_inc(s[f"ex_{l}"], 1)

        def act_ffn(act, l):
            B, RB = l * SLOT_TILES, l * 16 * (SLOT_TILES // 3)
            F = HID0 if l == 0 else HID1

            def first(c, i):
                act.wait_ge(s["xt"], tile(c, i) + (B + 1))
                act_copy(act, XH[c % 3][:, :], bank[0][:, 0:P], "xh")

            def gelu(c, i):
                act.wait_ge(s["h1"], tile(c, i) + (B + 1))
                if l == 0:
                    nc.scalar.activation(H[c % 3][:, :], bank[1 + c % 3][:, :], ACT.Gelu).then_inc(s["gel"], 1)
                else:
                    nc.scalar.activation(G0[c % 3][:, :], bank[1 + c % 3][:, 0:F], ACT.Gelu_apprx_tanh
                                         ).then_inc(s["gel"], 1)

            def high(c, i):
                act.wait_ge(s["ht"], tile(c, i) + (B + 1))
                act_copy(act, HH[c % 3][:, 0:F], bank[4 + c % 2][:, 0:F], "hh")

            def weigh_low(c, i):
                act.wait_ge(s["y"], tile(c, i) + (B + 1))
                act.wait_ge(s["ysfree"], tile(c, i) + (B + 1))
                nc.scalar.activation(YS[c % 3][:, :], bank[6 + c % 2][:, CH:2 * CH], ACT.Copy,
                                     scale=META[:, l, column(c, i), 1]).then_inc(s["ylo"], 1)

            def step(c, i):
                if c + 1 < SLOT_TILES:
                    first(c + 1, i)
                if c >= 3:
                    weigh_low(c - 3, i)
                gelu(c, i)
                if c >= 1:
                    high(c - 1, i)
            first(0, None)
            pipeline(act, step)
            weigh_low(SLOT_TILES - 3, None)
            high(SLOT_TILES - 1, None)
            weigh_low(SLOT_TILES - 2, None)
            weigh_low(SLOT_TILES - 1, None)

        @block.scalar
        def _(act):
            a_ = nc.scalar
            act.dma_start(COLS[:, :], cols).then_inc(s["small"], 16)
            act.dma_start(ROWS[:, :], rows).then_inc(s["small"], 16)
            act.dma_start(WP[:, :], wproj).then_inc(s["wproj"], 16)
            act.dma_start(WA[:, :], wa).then_inc(s["wawx"], 16)
            act.dma_start(WX[:, :], wx).then_inc(s["wawx"], 16)
            wh = [0]

            def high(n, end=CHUNKS0):
                for _ in range(n):
                    k = wh[0]
                    if k >= end:
                        return
                    wh[0] += 1
                    act.wait_ge(s[f"wraw{k % 2}"], 16 * (k // 2 + 1))
                    act_copy(act, part(k, 0), chunk(k), "whi")
            act.wait_ge(s["bias_ps"], 1)
            act_copy(act, BIAS[:, :], bank[7][:, 0:CH + EXPERTS], "bias")

            def turned(g):
                act.wait_ge(s["xnT_ps"], g + 1)
                act_copy(act, XNT[:, g], bank[g % 2][:, :], "xnT")

            def squares(g):
                act.wait_ge(s["k"], g + 1)
                a_.activation(K[:, g], bank[2][:, :], ACT.Relu).then_inc(s["rk"], 1)
                act.wait_ge(s["rk"], g + 1)
                if g >= 2:
                    act.wait_ge(s["k3"], g - 1)
                a_.activation(SQ[:, 1, g % 2], K[:, g], ACT.Square, bias=EPSC[:, :]).then_inc(s["k2"], 1)
                act.wait_ge(s["q"], g + 1)
                a_.activation(Q[:, g], bank[4][:, :], ACT.Relu).then_inc(s["rq"], 1)
                act.wait_ge(s["rq"], g + 1)
                if g >= 2:
                    act.wait_ge(s["q3"], g - 1)
                a_.activation(SQ[:, 0, g % 2], Q[:, g], ACT.Square, bias=EPSC[:, :]).then_inc(s["q2"], 1)

            def attention_out(g):
                act.wait_ge(s["oT_ps"], g + 1)
                act_copy(act, O[:, g // 2, 1 + (g % 2) * GT:1 + (g % 2 + 1) * GT], v_bank[g][:, :],
                         "o")
            turned(0)
            for g in range(GROUPS):
                if g + 1 < GROUPS:
                    turned(g + 1)
                squares(g)
                if g < 2:
                    high(1)
            high(1)
            attention_out(0)
            attention_out(1)
            high(1)
            attention_out(2)
            high(1)
            attention_out(3)
            if upto < 2:
                high(CHUNKS0)
            if upto >= 2:
                act_turned(act, 0, 0)
                act_turned(act, 0, 1)
                act_second(act, 0, 0)
                high(1)
                act_exps(act, 0, 0)
                high(CHUNKS0)
                act_turned(act, 0, 2)
                act_turned(act, 0, 3)
                act_second(act, 0, 1)
                act_exps(act, 0, 1)
            if upto >= 3:
                act_ffn(act, 0)
            if upto >= 4:
                act.wait_ge(s["y"], SLOT_TILES)
                high(2, CHUNKS)
                act.wait_ge(s["small"], 32)
                a_.activation(ALAM[:, :], COLS[:, C_LAM:C_LAM + 1], ACT.Sigmoid).then_inc(s["alam"], 1)

                def gates(g):
                    act.wait_ge(s["t3_ps"], g + 1)
                    act_copy(act, XNT[:, g], bank[g % 2][:, :], "t3")
                    act.wait_ge(s["res_0"], g + 1)
                    act.wait_ge(s["r_ps"], g + 1)
                    a_.activation(Q[:, g], bank[2 + g % 2][:, :], ACT.Sigmoid,
                                  bias=COLS[:, C_BA:C_BA + 1]).then_inc(s["r"], 1)
                    act.wait_ge(s["i_ps"], g + 1)
                    a_.activation(K[:, g], bank[4 + g % 2][:, :], ACT.Sigmoid,
                                  bias=COLS[:, C_BX:C_BX + 1]).then_inc(s["i"], 1)

                def decay(groups):
                    for g in groups:
                        act.wait_ge(s["r"], g + 1)
                        a_.activation(Q[:, g], Q[:, g], ACT.Exp, scale=-float(np.log(8.0))).then_inc(s["e"], 1)
                    act.wait_ge(s["alam"], 1)
                    for g in groups:
                        act.wait_ge(s["e"], g + 1)
                        a_.activation(XN[:, g * TG:(g + 1) * TG], Q[:, g].rearrange("p (t c) -> p t c", t=TG),
                                      ACT.Square, scale=ALAM[:, :]).then_inc(s["t2"], 1)
                    for g in groups:
                        act.wait_ge(s["t2"], g + 1)
                        a_.activation(XN[:, g * TG:(g + 1) * TG], XN[:, g * TG:(g + 1) * TG],
                                      ACT.Sqrt, scale=-1.0, bias=ONES[:, 0:1]).then_inc(s["sq"], 1)
                gates(0)
                gates(1)
                decay((0, 1))
                gates(2)
                gates(3)
                decay((2, 3))
                high(2, CHUNKS)
            if upto == 4:
                high(CHUNKS, CHUNKS)
            if upto >= 5:
                act_turned(act, 1, 0)
                act_turned(act, 1, 1)
                act_second(act, 1, 0)
                act_exps(act, 1, 0)
                act_turned(act, 1, 2)
                act_turned(act, 1, 3)
                act_second(act, 1, 1)
                act_exps(act, 1, 1)
                high(CHUNKS, CHUNKS)
                act_ffn(act, 1)

        def transposes(pe, dst, src, g, ln, sm_out):
            for t in range(TG):
                if ln is not None:
                    pe.wait_ge(s["norm"], ln * TILES + g * TG + t + 1)
                last = nc.tensor.transpose(dst[:, t * P:(t + 1) * P], src(t), IDENT[:, :])
            last.then_inc(s[sm_out], 1)

        def pe_turn(pe, l, g):
            if l == 1 and g >= 2:
                pe.wait_ge(s["nT_1"], g - 1)
            transposes(pe, turn_bank[l][g], lambda t: PB[:, 0, g * TG + t, 0:CH], g, 2 * l + 1, f"nT_ps_{l}")

        def pe_logits(pe, l, b):
            if l == 1:
                pe.wait_ge(s["rsc"], 1)
            rw = COLS[:, C_R0:C_R0 + EXPERTS] if l == 0 else RSC[:, :]
            for g in range(b * BG, (b + 1) * BG):
                pe.wait_ge(s[f"nT_{l}"], g + 1)
                for t in range(TG):
                    at = ((g % BG) * TG + t) * EXPERTS
                    last = nc.tensor.matmul(logit_bank[l][b][:, at:at + EXPERTS], XNT[:, g, t * P:(t + 1) * P],
                                            rw, start=True, stop=True)
            last.then_inc(s[f"logit_ps_{l}"], 1)

        def pe_rank(pe, l, b):
            pe.wait_ge(s[f"sel_{l}"], b + 1)
            o = rank_bank[l][b][:, 0:BT * EXPERTS].rearrange("p (t e) -> p t e", e=EXPERTS)
            nc.tensor.matmul(o, NLOWER[:, :], M[:, l, b].rearrange("p e t -> p t e"), start=True, stop=False)
            last = nc.tensor.matmul(o, ONES[:, :], MC[:, l, b].rearrange("p e t -> p t e"), start=False, stop=(b == 0))
            if b == 1:
                before = MC[:, l, 0, :, BT - 1]
                nc.tensor.matmul(o, ONES[:, :], before.unsqueeze(1).to_broadcast([P, BT, EXPERTS]),
                                 start=False, stop=True)
                n = rank_bank[l][b][:, BT * EXPERTS:(BT + 1) * EXPERTS]
                nc.tensor.matmul(n, ONES[:, :], before, start=True, stop=False)
                last = nc.tensor.matmul(n, ONES[:, :], MC[:, l, 1, :, BT - 1], start=False, stop=True)
            last.then_inc(s[f"rank_ps_{l}"], 1)

        def pe_ffn(pe, l):
            B, RB = l * SLOT_TILES, l * 16 * (SLOT_TILES // 3)
            F = HID0 if l == 0 else HID1
            up_h, up_l = (W[:, i * UP_COLS:(i + 1) * UP_COLS].rearrange("p (e n) -> p e n", e=EXPERTS)
                          for i in range(2))
            dn = W[:, 2 * UP_COLS:2 * UP_COLS + 2 * EXPERTS * F].rearrange("p (e k n) -> p e k n", e=EXPERTS, n=2 * CH)
            held = [pe.alloc_register(f"expert{u}_{l}") for u in range(3)]

            def fetch(c, i):
                pe.reg_load(held[c % 3], TBL[0:1, l, 1, column(c, i)])

            def expert(c):
                return pe.snap(held[c % 3], min_val=0, max_val=EXPERTS - 1)

            def xpose(c, i):
                pe.wait_ge(s[f"xs{c % 3}"], dma_count(c, i) + RB)
                if c >= 1:
                    pe.wait_ge(s["xl"], tile(c, i) + B)
                nc.tensor.transpose(bank[0][:, 0:P], XS[c % 3][:, 0:CH], IDENT[:, :]).then_inc(s["xt"], 1)

            def up(c):
                e = expert(c)
                o = bank[1 + c % 3][:, :]
                nc.tensor.matmul(o, XH[c % 3][:, :], up_h[:, bass.ds(e, 1), :], start=True, stop=False)
                nc.tensor.matmul(o, XH[c % 3][:, :], up_l[:, bass.ds(e, 1), :], start=False, stop=False)
                nc.tensor.matmul(o, XL[c % 3][:, :], up_h[:, bass.ds(e, 1), :], start=False, stop=True
                                 ).then_inc(s["h1"], 1)

            def hxpose(c, i):
                if l == 0:
                    pe.wait_ge(s["gel"], tile(c, i) + 1)
                else:
                    pe.wait_ge(s["h"], tile(c, i) + 1)
                for k in range(F // P):
                    last = nc.tensor.transpose(bank[4 + c % 2][:, k * P:(k + 1) * P],
                                               H[c % 3][:, k * P:(k + 1) * P], IDENT[:, :])
                last.then_inc(s["ht"], 1)

            def down(c, i):
                e = expert(c)
                pe.wait_ge(s["hl"], tile(c, i) + (B + 1))
                if c >= 2:
                    pe.wait_ge(s["ys"], tile(c, i) + (B - 1))
                nk, o = F // P, bank[6 + c % 2]
                for k in range(nk):
                    ks = slice(k * P, (k + 1) * P)
                    nc.tensor.matmul(o[:, 0:2 * CH], HH[c % 3][:, ks], dn[:, bass.ds(e, 1), k, :],
                                     start=(k == 0), stop=False)
                for k in range(nk):
                    ks = slice(k * P, (k + 1) * P)
                    last = nc.tensor.matmul(o[:, 0:CH], HL[c % 3][:, ks], dn[:, bass.ds(e, 1), k, 0:CH],
                                            start=False, stop=(k == nk - 1))
                last.then_inc(s["y"], 1)

            def step(c, i):
                if c + 1 < SLOT_TILES:
                    xpose(c + 1, i)
                else:
                    pe.wait_ge(s["xl"], B + SLOT_TILES)
                up(c)
                if c >= 1:
                    hxpose(c - 1, i)
                if c >= 2:
                    down(c - 2, i)
                if c + 1 < SLOT_TILES:
                    fetch(c + 1, i)
            pe.wait_ge(s[f"table_{l}"], 1)
            fetch(0, None)
            xpose(0, None)
            pipeline(pe, step)
            hxpose(SLOT_TILES - 1, None)
            down(SLOT_TILES - 2, None)
            down(SLOT_TILES - 1, None)

        @block.tensor
        def _(pe):
            mm = nc.tensor.matmul
            pe.wait_ge(s["const"], NC_TOTAL)
            pe.wait_ge(s["small"], 32)
            pe.wait_ge(s["wproj"], 16)
            pe.wait_ge(s["bd"], 1)
            mm(bank[7][:, 0:CH], BD[:, :], WP[:, :], start=True, stop=False)
            mm(bank[7][:, 0:CH], ONES[0:1, :], ROWS[0:1, 0:CH], start=False, stop=True)
            mm(bank[7][:, CH:CH + EXPERTS], ONES[0:1, :], ROWS[0:1, CH:CH + EXPERTS], start=True, stop=True
               ).then_inc(s["bias_ps"], 1)

            def turn(g):
                if g >= 2:
                    pe.wait_ge(s["xnT"], g - 1)
                transposes(pe, bank[g % 2], lambda t: XN[:, g * TG + t, :], g, 0, "xnT_ps")

            def project(g):
                if g == 0:
                    pe.wait_ge(s["wqkv"], 16)
                    pe.wait_ge(s["bias"], 1)
                pe.wait_ge(s["xnT"], g + 1)
                if g >= 1:
                    pe.wait_ge(s["rk"], g)
                for t in range(TG):
                    last = mm(bank[2][:, t * P:(t + 1) * P], XNT[:, g, t * P:(t + 1) * P],
                              WQKV[:, CH:2 * CH], start=True, stop=True)
                last.then_inc(s["k"], 1)
                if g >= 1:
                    pe.wait_ge(s["rq"], g)
                mm(bank[4][:, :], WQKV[:, 0:CH], XNT[:, g], start=True, stop=True).then_inc(s["q"], 1)
                if g >= 2:
                    pe.wait_ge(s["vr"], g - 1)
                for t in range(TG):
                    last = mm(v_bank[g][:, t * P:(t + 1) * P], XNT[:, g, t * P:(t + 1) * P],
                              WQKV[:, 2 * CH:3 * CH], start=True, stop=True)
                last.then_inc(s["v"], 1)

            def kv_sum(g):
                pe.wait_ge(s["k3"], g + 1)
                pe.wait_ge(s["vr"], g + 1)
                if g == 2:
                    pe.wait_ge(s["kvb"], 2)
                for t in range(TG):
                    last = mm(bank[5][:, 0:CH + HEADS], K[:, g, t * P:(t + 1) * P], VR[:, g % 2, t, :],
                              start=(g % 2 == 0 and t == 0), stop=(g % 2 == 1 and t == TG - 1))
                last.then_inc(s["kv"], 1)

            def attend(g):
                pe.wait_ge(s["kvb"], 2 * (g // 2 + 1))
                pe.wait_ge(s["q3"], g + 1)
                pe.wait_ge(s["rk"], GROUPS)
                pe.wait_ge(s["rq"], GROUPS)
                pe.wait_ge(s["xnT"], GROUPS)
                if g >= 2:
                    pe.wait_ge(s["ot"], g - 1)
                for t in range(TG):
                    q_t = Q[:, g, t * P:(t + 1) * P]
                    mm(num_bank[g][:, t * P:(t + 1) * P], q_t, KV[:, g // 2], start=True, stop=True)
                    last = mm(den_bank[g][:, t * HEADS:(t + 1) * HEADS], q_t, KSB[:, g // 2], start=True, stop=True)
                last.then_inc(s["num"], 1)

            def turn_out(g):
                pe.wait_ge(s["ot"], g + 1)
                pe.wait_ge(s["vr"], GROUPS - 1 + g % 2)
                if g >= 2:
                    pe.wait_ge(s["o"], g - 1)
                transposes(pe, v_bank[g], lambda t: OTM[:, g % 2, t, :], g, None, "oT_ps")

            def output(g):
                pe.wait_ge(s["o"], 2 * (g // 2) + 2)
                pe.wait_ge(s["wk"], 3)
                pe.wait_ge(s["xnT"], GROUPS)
                if g >= 2:
                    pe.wait_ge(s["x1a"], g - 1)
                    if upto >= 2:
                        pe.wait_ge(s["nT_0"], g - 1)
                b, first = g // 2, (g % 2) * GT
                for t in range(TG):
                    for k in range(3):
                        at = first + t * P + k
                        last = mm(bank[g % 2][:, t * P:(t + 1) * P], O[:, b, at:at + P], WK[:, k, :],
                                  start=(k == 0), stop=(k == 2))
                last.then_inc(s["proj"], 1)

            turn(0)
            turn(1)
            project(0)
            turn(2)
            project(1)
            kv_sum(0)
            turn(3)
            project(2)
            kv_sum(1)
            project(3)
            attend(0)
            attend(1)
            kv_sum(2)
            turn_out(0)
            turn_out(1)
            kv_sum(3)
            output(0)
            output(1)
            attend(2)
            attend(3)
            turn_out(2)
            turn_out(3)
            if upto >= 2:
                pe_turn(pe, 0, 0)
                pe_turn(pe, 0, 1)
                pe_logits(pe, 0, 0)
            output(2)
            output(3)

            if upto >= 2:
                pe_rank(pe, 0, 0)
                pe_turn(pe, 0, 2)
                pe_turn(pe, 0, 3)
                pe_logits(pe, 0, 1)
                pe_rank(pe, 0, 1)
            if upto >= 3:
                pe_ffn(pe, 0)
            if upto >= 4:
                pe.wait_ge(s["wawx"], 32)
                for g in range(GROUPS):
                    if g >= 2:
                        pe.wait_ge(s["t3"], g - 1)
                    transposes(pe, bank[g % 2], lambda t: XN[:, g * TG + t, :], g, 2, "t3_ps")
                    pe.wait_ge(s["t3"], g + 1)
                    if g >= 2:
                        pe.wait_ge(s["i"], g - 1)
                    mm(bank[2 + g % 2][:, :], WA[:, :], XNT[:, g], start=True, stop=True).then_inc(s["r_ps"], 1)
                    mm(bank[4 + g % 2][:, :], WX[:, :], XNT[:, g], start=True, stop=True).then_inc(s["i_ps"], 1)
                pe.wait_ge(s["ys"], SLOT_TILES)
                pe.wait_ge(s["r"], GROUPS)
                pe.wait_ge(s["i"], GROUPS)

                def scanned(g):
                    pe.wait_ge(s["yscan"], g + 1)
                    if g >= 2:
                        pe.wait_ge(s["xc"], g - 1)
                    b, first = g // 2, 1 + (g % 2) * GT
                    transposes(pe, bank[6 + g % 2], lambda t: O[:, b, first + t * P:first + (t + 1) * P], g,
                               None, "yT")
                scanned(0)
                scanned(1)
                if upto >= 5:
                    pe_turn(pe, 1, 0)
                    pe_turn(pe, 1, 1)
                    pe_logits(pe, 1, 0)
                scanned(2)
                scanned(3)
            if upto >= 5:
                pe_rank(pe, 1, 0)
                pe_turn(pe, 1, 2)
                pe_turn(pe, 1, 3)
                pe_logits(pe, 1, 1)
                pe_rank(pe, 1, 1)
                pe_ffn(pe, 1)

        def ln_stats(v, l, g, src):
            for t in range(g * TG, (g + 1) * TG):
                nc.vector.bn_stats(ST[:, l, t], src(t)).then_inc(s["stats"], 1)
            for t in range(g * TG, (g + 1) * TG):
                v.wait_ge(s["stats"], l * TILES + t + 1)
                nc.vector.bn_aggr(MV[:, l, t], ST[:, l, t]).then_inc(s["aggr"], 1)
            v.wait_ge(s["aggr"], l * TILES + TG * (g + 1))
            sl = slice(g * TG, (g + 1) * TG)
            nc.vector.tensor_scalar_add(VE[:, l, sl], MV[:, l, sl, 1], LN_EPS).then_inc(s["ve"], 1)

        def ln_norm(v, l, g, src, dst):
            v.wait_ge(s["rstd"], l * GROUPS + g + 1)
            for t in range(g * TG, (g + 1) * TG):
                nc.vector.tensor_scalar(dst(t), src(t), MV[:, l, t, 0:1], RSTD[:, l, t:t + 1],
                                        ALU.subtract, ALU.mult).then_inc(s["norm"], 1)

        def dve_mse(v, b):
            sl = slice(b * BT, (b + 1) * BT)
            v.wait_ge(s["rstd"], 3 * GROUPS + BG * (b + 1))
            ve = VE[:, 4, sl]
            nc.vector.tensor_tensor(ve, MV[:, 3, sl, 1], RSTD[:, 3, sl], ALU.mult).then_inc(s["msq"], 1)
            v.wait_ge(s["msq"], 2 * b + 1)
            nc.vector.tensor_tensor(ve, ve, RSTD[:, 3, sl], ALU.mult).then_inc(s["msq"], 1)
            v.wait_ge(s["msq"], 2 * b + 2)
            nc.vector.tensor_scalar_add(ve, ve, RMS_EPS).then_inc(s["mse_1"], 1)

        def dve_route(v, l, b, chain):
            V = nc.vector
            sl = slice(b * BT, (b + 1) * BT)

            def link(ins):
                chain[0] += 1
                ins.then_inc(s[f"chain_{l}"], 1)
                v.wait_ge(s[f"chain_{l}"], chain[0])

            def plain(ins):
                chain[0] += 1
                ins.then_inc(s[f"chain_{l}"], 1)
            logit = logit_bank[l][b][:, 0:BT * EXPERTS].rearrange("p (t e) -> p t e", e=EXPERTS)
            v.wait_ge(s[f"logit_ps_{l}"], b + 1)
            V.tensor_copy(LG[:, l, sl], logit).then_inc(s[f"lg_{l}"], 1)
            v.wait_ge(s[f"lg_{l}"], b + 1)
            for t in range(b * BT, (b + 1) * BT):
                plain(V.max(V8[:, l, t], LG[:, l, t]))
            v.wait_ge(s[f"chain_{l}"], chain[0])
            for t in range(b * BT, (b + 1) * BT):
                plain(V.max_index(I8[:, l, t], V8[:, l, t], LG[:, l, t]))
            v.wait_ge(s[f"chain_{l}"], chain[0])
            link(V.tensor_copy(IF[:, l, sl], I8[:, l, sl, 0:TOP]))
            full = [P, BT, TOP, EXPERTS]
            link(V.tensor_tensor(OH[:, l, sl], IOTA8[:, :].unsqueeze(1).unsqueeze(1).to_broadcast(full),
                                 IF[:, l, sl].unsqueeze(3).to_broadcast(full), ALU.is_equal))
            link(V.tensor_tensor(M[:, l, b].rearrange("p e t -> p t e"), OH[:, l, sl, 0], OH[:, l, sl, 1], ALU.add))
            flat = "p e t -> p (e t)"
            V.tensor_tensor_scan(MC[:, l, b].rearrange(flat), RESET[:, :, :].rearrange(flat),
                                 M[:, l, b].rearrange(flat), 0.0, ALU.mult, ALU.add
                                 ).then_inc(s[f"sel_{l}"], 1)
            less = V.tensor_tensor(EX[:, l, sl], V8[:, l, sl], V8[:, l, sl, 0:1].to_broadcast([P, BT, 8]),
                                   ALU.subtract)
            if l == 0:
                less.then_inc(s["exps_0"], 1)
            else:
                plain(less)
                v.wait_ge(s["rms_1"], b + 1)
                link(V.tensor_scalar_mul(RMS[:, sl], RSTD[:, 4, sl], float(np.float32(CH) ** np.float32(-0.5))))
                V.tensor_tensor(EX[:, l, sl], EX[:, l, sl], RMS[:, sl].unsqueeze(2).to_broadcast([P, BT, 8]),
                                ALU.mult).then_inc(s["exps_1"], 1)

        def dve_slots(v, l, b, chain):
            V = nc.vector
            sl = slice(b * BT, (b + 1) * BT)

            def link(ins):
                chain[0] += 1
                ins.then_inc(s[f"chain_{l}"], 1)
                v.wait_ge(s[f"chain_{l}"], chain[0])
            v.wait_ge(s[f"rank_ps_{l}"], b + 1)
            rank = rank_bank[l][b][:, 0:BT * EXPERTS].rearrange("p (t e) -> p t e", e=EXPERTS)
            sp8, spp = SP8[:, b], SPP[:, b]
            full = [P, BT, TOP, EXPERTS]
            link(V.tensor_tensor(sp8, rank, EBASE[:, :].unsqueeze(1).to_broadcast([P, BT, EXPERTS]), ALU.add))
            link(V.tensor_tensor(spp, sp8.unsqueeze(2).to_broadcast(full), OH[:, l, sl], ALU.mult))
            with nc.allow_low_precision(reason="whole numbers below 2**24: exact"):
                V.tensor_reduce(SL[:, l, sl], spp, AX.X, ALU.add).then_inc(s[f"slot_{l}"], 1)
            v.wait_ge(s[f"ex_{l}"], b + 1)
            pr = PR[:, l, sl]
            two = [P, BT, TOP]
            link(V.tensor_reduce(pr[:, :, 0:1], EX[:, l, sl], AX.X, ALU.add))
            link(V.reciprocal(pr[:, :, 1:2], pr[:, :, 0:1]))
            prob = pr[:, :, 2:4]
            link(V.tensor_tensor(prob, EX[:, l, sl, 0:TOP], pr[:, :, 1:2].to_broadcast(two), ALU.mult))
            link(V.tensor_tensor(pr[:, :, 4:5], prob[:, :, 0:1], prob[:, :, 1:2], ALU.add))
            if l == 1:
                link(V.tensor_scalar(pr[:, :, 6:7], pr[:, :, 4:5], 0.0, None, ALU.is_gt))
                link(V.tensor_tensor(pr[:, :, 4:5], pr[:, :, 4:5], pr[:, :, 6:7], ALU.mult))
                link(V.tensor_scalar(pr[:, :, 6:7], pr[:, :, 6:7], -1.0, 1.0, ALU.mult, ALU.add))
                link(V.tensor_tensor(pr[:, :, 4:5], pr[:, :, 4:5], pr[:, :, 6:7], ALU.add))
            link(V.reciprocal(pr[:, :, 5:6], pr[:, :, 4:5]))
            wt = PB[:, :, sl, CH + 1:CH + 2].rearrange("p k t a -> p t (k a)")
            if l == 0:
                V.tensor_tensor(wt, prob, pr[:, :, 5:6].to_broadcast(two), ALU.mult).then_inc(s["row_0"], 1)
            else:
                link(V.tensor_tensor(prob, prob, pr[:, :, 5:6].to_broadcast(two), ALU.mult))
                v.wait_ge(s["slot_1"], b + 1)
                link(V.tensor_tensor(spp, OH[:, l, sl],
                                     BIAS[:, CH:].unsqueeze(1).unsqueeze(1).to_broadcast(full), ALU.mult))
                link(V.tensor_reduce(pr[:, :, 6:8], spp, AX.X, ALU.add))
                V.tensor_tensor(wt, prob, pr[:, :, 6:8], ALU.mult).then_inc(s["row_1"], 1)

        def dve_table(v, l, chain):
            V = nc.vector

            def link(ins):
                chain[0] += 1
                ins.then_inc(s[f"chain_{l}"], 1)
                v.wait_ge(s[f"chain_{l}"], chain[0])
            v.wait_ge(s[f"rank_ps_{l}"], BATCH)
            n = rank_bank[l][1][:, BT * EXPERTS:(BT + 1) * EXPERTS]
            V.tensor_tensor(CNTI[:, l, 0], n, EBASE[:, :], ALU.add).then_inc(s[f"padrow_{l}"], 1)
            link(V.tensor_scalar_add(CNTI[:, l, 1], n, float(P - 1)))
            link(V.tensor_single_scalar(CNTI[:, l, 2], CNTI[:, l, 1], P.bit_length() - 1, ALU.logical_shift_right))
            link(V.tensor_copy(CNT[:, l, 0], CNTI[:, l, 2]))
            link(V.tensor_tensor_scan(CNT[:, l, 1], ONES[:, 0:EXPERTS], CNT[:, l, 0], 0.0, ALU.mult, ALU.add))
            full = [P, SLOT_TILES, EXPERTS]
            ends = CNT[:, l, 1].unsqueeze(1).to_broadcast(full)
            past = TE[:, 0].rearrange("p (j e) -> p j e", e=EXPERTS)
            begin = TE[:, 1].rearrange("p (j e) -> p j e", e=EXPERTS)
            link(V.tensor_tensor(past, JIDX[:, :].unsqueeze(2).to_broadcast(full), ends, ALU.is_ge))
            link(V.tensor_tensor(begin, past, ends, ALU.mult))
            link(V.tensor_reduce(TR[:, 0], past, AX.X, ALU.add))
            link(V.tensor_reduce(TR[:, 1], begin, AX.X, ALU.max))
            link(V.tensor_tensor(TR[:, 1], JIDX[:, :], TR[:, 1], ALU.subtract))
            link(V.tensor_scalar_mul(TR[:, 1], TR[:, 1], float(P)))
            link(V.scalar_tensor_tensor(TBL[:, l, 0], TR[:, 0], float(REG), TR[:, 1], ALU.mult, ALU.add))
            V.tensor_scalar_min(TBL[:, l, 1], TR[:, 0], float(EXPERTS - 1)).then_inc(s[f"table_{l}"], 1)

        def dve_ffn(v, l):
            B, RB = l * SLOT_TILES, l * 16 * (SLOT_TILES // 3)
            V = nc.vector
            F = HID0 if l == 0 else HID1

            def xlow(c, i):
                v.wait_ge(s["xh"], tile(c, i) + (B + 1))
                V.tensor_tensor(XL[c % 3][:, :], bank[0][:, 0:P], XH[c % 3][:, :].bitcast(f32), ALU.subtract
                                ).then_inc(s["xl"], 1)
                V.tensor_copy(META[:, l, column(c, i), :], XS[c % 3][:, CH:CH + 2].unsqueeze(1)
                              ).then_inc(s["meta"], 1)

            def weigh(c, i):
                v.wait_ge(s["ylo"], tile(c, i) + (B + 1))
                V.scalar_tensor_tensor(YS[c % 3][:, :], bank[6 + c % 2][:, 0:CH], META[:, l, column(c, i), 1],
                                       YS[c % 3][:, :], ALU.mult, ALU.add).then_inc(s["ys"], 1)
                V.tensor_copy(YROW[c % 3][:, :], META[:, l, column(c, i), 0]).then_inc(s["yrow"], 1)

            def gate(c, i):
                v.wait_ge(s["gel"], tile(c, i) + (B + 1))
                V.tensor_tensor(H[c % 3][:, 0:F], bank[1 + c % 3][:, F:2 * F], G0[c % 3][:, :], ALU.mult
                                ).then_inc(s["h"], 1)

            def hlow(c, i):
                v.wait_ge(s["hh"], tile(c, i) + (B + 1))
                V.tensor_tensor(HL[c % 3][:, 0:F], bank[4 + c % 2][:, 0:F], HH[c % 3][:, 0:F].bitcast(f32),
                                ALU.subtract).then_inc(s["hl"], 1)

            def step(c, i):
                if c + 1 < SLOT_TILES:
                    xlow(c + 1, i)
                if c >= 3:
                    weigh(c - 3, i)
                if l == 1:
                    gate(c, i)
                if c >= 1:
                    hlow(c - 1, i)
            xlow(0, None)
            pipeline(v, step)
            weigh(SLOT_TILES - 3, None)
            hlow(SLOT_TILES - 1, None)
            weigh(SLOT_TILES - 2, None)
            weigh(SLOT_TILES - 1, None)

        def dve_residual(v, l, g):
            v.wait_ge(s[f"sum_{l}"], g + 1)
            sl = slice(g * TG, (g + 1) * TG)
            nc.vector.tensor_tensor(X[:, sl], X[:, sl], Q[:, g].rearrange("p (t c) -> p t c", t=TG), ALU.add
                                    ).then_inc(s[f"res_{l}"], 1)

        @block.vector
        def _(v):
            V = nc.vector
            xrow = lambda t: X[:, t, :]
            v.wait_ge(s["small"], 32)
            v.wait_ge(s["const"], NC_TOTAL)
            V.tensor_scalar_mul(BD[:, :], ONES[:, :], COLS[:, C_BDWC:C_BDWC + 1]).then_inc(s["bd"], 1)
            V.tensor_scalar_mul(RSC[:, :], COLS[:, C_R1:C_R1 + EXPERTS], COLS[:, C_RS:C_RS + 1]
                                ).then_inc(s["rsc"], 1)
            def cube(src, g, i, ready, done):
                v.wait_ge(s[ready], g + 1)
                V.scalar_tensor_tensor(src[:, g], src[:, g], FOCUS_EPS, SQ[:, i, g % 2], ALU.add, ALU.mult
                                       ).then_inc(s[done], 1)

            def features(g):
                cube(K, g, 1, "k2", "k3")
                cube(Q, g, 0, "q2", "q3")
                v.wait_ge(s["k3"], g + 1)
                V.tensor_reduce(S3[:, g % 2], K[:, g].rearrange("p (t h d) -> p t h d", t=TG, d=HD), AX.X, ALU.add
                                ).then_inc(s["s3"], 1)
                v.wait_ge(s["s3"], g + 1)
                if g >= 2:
                    v.wait_ge(s["kv"], g - 1)
                V.reciprocal(VR[:, g % 2, :, CH:], S3[:, g % 2]).then_inc(s["r3"], 1)
                v.wait_ge(s["r3"], g + 1)
                v.wait_ge(s["v"], g + 1)
                full = [P, TG, HEADS, HD]
                V.tensor_tensor(VR[:, g % 2, :, 0:CH].rearrange("p t (h d) -> p t h d", d=HD),
                                v_bank[g][:, :].rearrange("p (t h d) -> p t h d", t=TG, d=HD),
                                VR[:, g % 2, :, CH:].unsqueeze(3).to_broadcast(full), ALU.mult).then_inc(s["vr"], 1)

            def kv_block(b):
                v.wait_ge(s["kv"], 2 * b + 2)
                V.tensor_tensor(KV[:, b], bank[5][:, 0:CH], HEADM[:, :], ALU.mult).then_inc(s["kvb"], 1)
                V.scalar_tensor_tensor(KSB[:, b], bank[5][:, CH:CH + HEADS], FOCUS_EPS, HEADM[:, 0:P:HD],
                                       ALU.add, ALU.mult).then_inc(s["kvb"], 1)

            def attended(g):
                v.wait_ge(s["num"], g + 1)
                V.reciprocal(RD[:, g % 2], den_bank[g][:, 0:TG * HEADS].rearrange(
                    "p (t h) -> p t h", t=TG)).then_inc(s["rden"], 1)
                v.wait_ge(s["rden"], g + 1)
                if g >= 2:
                    v.wait_ge(s["oT_ps"], g - 1)
                V.tensor_tensor(OTM[:, g % 2].rearrange("p t (h d) -> p t h d", d=HD),
                                num_bank[g][:, :].rearrange("p (t h d) -> p t h d", t=TG, d=HD),
                                RD[:, g % 2].unsqueeze(3).to_broadcast([P, TG, HEADS, HD]), ALU.mult
                                ).then_inc(s["ot"], 1)

            def projected(g):
                v.wait_ge(s["proj"], g + 1)
                v.wait_ge(s["xb"], g + 1)
                V.tensor_tensor(X[:, g * TG:(g + 1) * TG, :],
                                bank[g % 2][:, :].rearrange("p (t c) -> p t c", t=TG),
                                X[:, g * TG:(g + 1) * TG, :], ALU.add).then_inc(s["x1a"], 1)

            def stats(g):
                v.wait_ge(s[f"x{g}"], 16)
                ln_stats(v, 0, g, xrow)

            def norm(g):
                ln_norm(v, 0, g, xrow, lambda t: XN[:, t, :])
            stats(0)
            stats(1)
            norm(0)
            stats(2)
            norm(1)
            v.wait_ge(s["wproj"], 16)
            V.tensor_scalar_mul(WK[:, 0], WP[:, :], COLS[:, 0:1]).then_inc(s["wk"], 1)
            V.tensor_scalar_mul(WK[:, 2], WP[:, :], COLS[:, 2:3]).then_inc(s["wk"], 1)
            V.scalar_tensor_tensor(WK[:, 1], WP[:, :], COLS[:, 1:2], WP[:, :], ALU.mult, ALU.add
                                   ).then_inc(s["wk"], 1)
            norm(2)
            features(0)
            stats(3)
            norm(3)
            features(1)
            features(2)
            kv_block(0)
            attended(0)
            attended(1)
            features(3)
            kv_block(1)
            projected(0)
            projected(1)
            pbrow = lambda t: PB[:, 0, t, 0:CH]

            def stats_in(l, g, done, n):
                v.wait_ge(s[done], n)
                ln_stats(v, l, g, xrow)

            def low(first, end):
                for k in range(first, end):
                    v.wait_ge(s["whi"], k + 1)
                    v.wait_ge(s["wlo"], k)
                    V.tensor_tensor(part(k, 1), chunk(k), part(k, 0).bitcast(f32), ALU.subtract
                                    ).then_inc(s["wlo"], 1)
            if upto < 2:
                attended(2)
                attended(3)
                projected(2)
                projected(3)
            if upto >= 2:
                chain = [0]
                stats_in(1, 0, "x1a", 1)
                stats_in(1, 1, "x1a", 2)
                attended(2)
                attended(3)
                ln_norm(v, 1, 0, xrow, pbrow)
                ln_norm(v, 1, 1, xrow, pbrow)
                dve_route(v, 0, 0, chain)
                projected(2)
                projected(3)
                stats_in(1, 2, "x1a", 3)
                stats_in(1, 3, "x1a", 4)
                dve_slots(v, 0, 0, chain)
                ln_norm(v, 1, 2, xrow, pbrow)
                ln_norm(v, 1, 3, xrow, pbrow)
                dve_route(v, 0, 1, chain)
                dve_slots(v, 0, 1, chain)
                dve_table(v, 0, chain)
            if upto >= 3:
                dve_ffn(v, 0)
                if upto == 3:
                    for g in range(GROUPS):
                        dve_residual(v, 0, g)
            if upto >= 4:
                v.wait_ge(s["y"], SLOT_TILES)
                low(CHUNKS0, CHUNKS0 + 2)

                def norm3(g):
                    ln_norm(v, 2, g, xrow, lambda t: XN[:, t, :])
                for g in range(GROUPS):
                    dve_residual(v, 0, g)
                    stats_in(2, g, "res_0", g + 1)
                    if g >= 1:
                        norm3(g - 1)
                norm3(GROUPS - 1)

                def carried(g):
                    v.wait_ge(s["alam"], 1)
                    v.wait_ge(s["e"], g + 1)
                    v.wait_ge(s["t2"], g + 1)
                    V.tensor_scalar_mul(Q[:, g], Q[:, g], ALAM[:, :]).then_inc(s["at"], 1)

                def recurrence(g):
                    v.wait_ge(s["sq"], g + 1)
                    v.wait_ge(s["ix"], g + 1)
                    V.tensor_tensor(K[:, g], K[:, g], XN[:, g * TG:(g + 1) * TG].rearrange("p t c -> p (t c)"),
                                    ALU.mult).then_inc(s["bt"], 1)
                    v.wait_ge(s["bt"], g + 1)
                    v.wait_ge(s["at"], g + 1)
                    if g:
                        v.wait_ge(s["yscan"], g)
                    b, first = g // 2, 1 + (g % 2) * GT
                    V.tensor_tensor_scan(O[:, b, first:first + GT], Q[:, g], K[:, g],
                                         0.0 if g % 2 == 0 else O[:, b, first - 1:first],
                                         ALU.mult, ALU.add).then_inc(s["yscan"], 1)

                def added(g):
                    v.wait_ge(s["yT"], g + 1)
                    V.tensor_tensor(X[:, g * TG:(g + 1) * TG, :],
                                    bank[6 + g % 2][:, :].rearrange("p (t c) -> p t c", t=TG),
                                    X[:, g * TG:(g + 1) * TG, :], ALU.add).then_inc(s["xc"], 1)
                carried(0)
                carried(1)
                recurrence(0)
                recurrence(1)
            if upto == 4:
                carried(2)
                carried(3)
                for g in (2, 3):
                    recurrence(g)
                for g in range(GROUPS):
                    added(g)
                low(CHUNKS0 + 2, CHUNKS)
            if upto >= 5:
                chain = [0]
                added(0)
                stats_in(3, 0, "xc", 1)
                added(1)
                stats_in(3, 1, "xc", 2)
                ln_norm(v, 3, 0, xrow, pbrow)
                ln_norm(v, 3, 1, xrow, pbrow)
                dve_mse(v, 0)
                carried(2)
                carried(3)
                recurrence(2)
                recurrence(3)
                dve_route(v, 1, 0, chain)
                added(2)
                stats_in(3, 2, "xc", 3)
                added(3)
                stats_in(3, 3, "xc", 4)
                dve_slots(v, 1, 0, chain)
                ln_norm(v, 3, 2, xrow, pbrow)
                ln_norm(v, 3, 3, xrow, pbrow)
                dve_mse(v, 1)
                dve_route(v, 1, 1, chain)
                dve_slots(v, 1, 1, chain)
                dve_table(v, 1, chain)
                low(CHUNKS0 + 2, CHUNKS)
                dve_ffn(v, 1)
                for g in range(GROUPS):
                    dve_residual(v, 1, g)


NC_TOTAL = 21


_INS = ["x", "wqkv", "wproj", "cols", "rows", "wpack", "wa", "wx"]


def layout(i):
    import numpy as np
    c = np.ascontiguousarray
    cols = np.concatenate([
        i["L0_attn_w_dwc"], i["L0_attn_b_dwc"][:, None], i["L1_attn_ba"][:, None], i["L1_attn_bx"][:, None],
        i["L1_attn_Lam"][:, None], i["L1_ffn_router_scale"][:, None], i["L0_ffn_router_w"].T,
        i["L1_ffn_router_w"]], axis=1)
    rows = np.concatenate([i["L0_attn_b_proj"], i["L1_ffn_per_expert_scale"]])[None, :]
    w1 = i["L0_ffn_w1"].transpose(1, 0, 2).reshape(P, -1)
    w2 = i["L0_ffn_w2"].reshape(EXPERTS, HID0 // P, P, CH).transpose(2, 0, 1, 3).reshape(P, -1)
    gate = i["L1_ffn_gating_w"].transpose(3, 0, 1, 2).reshape(P, -1)
    lin = i["L1_ffn_linear_w"].reshape(EXPERTS, HID1 // P, P, CH).transpose(2, 0, 1, 3).reshape(P, -1)
    return {"x": c(i["L0_attn_x"]), "wqkv": c(i["L0_attn_w_qkv"].T), "wproj": c(i["L0_attn_w_proj"].T),
            "cols": c(cols), "rows": c(rows), "wpack": c(np.concatenate([w1, w2, gate, lin], axis=1)),
            "wa": c(i["L1_attn_Wa"]), "wx": c(i["L1_attn_Wx"])}


def kernel(**inputs):
    import numpy as _np
    import concourse.bacc as _bacc
    from concourse import mybir as _mybir
    from concourse.bass_utils import run_bass_kernel_spmd as _run

    nc = _bacc.Bacc("TRN2", target_bir_lowering=False, num_devices=1)
    laid = layout({k: _np.asarray(v) for k, v in inputs.items()})
    args = [nc.dram_tensor(f"in_{n}", laid[n].shape, _mybir.dt.from_np(laid[n].dtype), kind="ExternalInput").ap()
            for n in _INS]
    out = nc.dram_tensor("out_0", (BATCH, SEQ, CH), _mybir.dt.float32, kind="ExternalOutput").ap()
    two_layers(nc, *args, out, upto=UPTO)
    r = _run(nc, [{f"in_{n}": laid[n] for n in _INS}], core_ids=[0])
    return r.results[0]["out_0"]


UPTO = 5
```

```python
import concourse.bass as bass
from concourse import mybir
from contextlib import ExitStack

BATCH, SEQ, CH = 2, 1024, 128
TOKENS = BATCH * SEQ
P = 128
TILES = TOKENS // P
TG = 4
GROUPS = TILES // TG
GT = TG * P
BT = TILES // BATCH
BG = GROUPS // BATCH
HEADS = 16
HD = CH // HEADS
FOCUS_EPS = 1e-6
LN_EPS = 1e-5
RMS_EPS = 1e-6
EXPERTS, TOP = 8, 2
HID0, HID1 = 512, 256
SLOT_TILES = TOKENS * TOP // P + EXPERTS - 1
PEEL, STEPS = 3, 6
ROUNDS = (SLOT_TILES - PEEL - 1) // STEPS
LAST = PEEL + ROUNDS * STEPS
EARLY = -((EXPERTS * (P - 1) - BT * P * TOP) // P)
assert PEEL + STEPS <= EARLY
SEGMENTS = 2 * EXPERTS
REG = TOKENS + P
DUMP = EXPERTS * REG
DUMP_TILES = SLOT_TILES - TOKENS * TOP // P + 1
XROWS = DUMP + DUMP_TILES * P
XW = CH + 2
NO_ROW = 1 << 20
CHUNK = 1024
WCOLS = EXPERTS * (HID0 + HID0 + 2 * HID1 + HID1)
CHUNKS = WCOLS // CHUNK
LOW_POOL = 5
CHUNKS0 = EXPERTS * 2 * HID0 // CHUNK
WRES = EXPERTS * 2 * HID0
UP_COLS = EXPERTS * 512
CONSTS = 28
C_DWC, C_BDWC, C_BA, C_BX, C_LAM, C_RS, C_R0, C_R1, C_END = 0, 3, 4, 5, 6, 7, 8, 16, 24


def two_layers(nc, x, wqkv, wproj, cols, rows, wpack, wa, wx, out):
    f32, f32r, i32, u32 = mybir.dt.float32, mybir.dt.float32r, mybir.dt.int32, mybir.dt.uint32
    ALU, ACT, AX = mybir.AluOpType, mybir.ActivationFunctionType, mybir.AxisListType
    import numpy as np

    x_v = x.rearrange("b (t p) c -> p (b t) c", p=P)
    out_v = out.rearrange("b (t p) c -> p (b t) c", p=P)
    slots_d = [nc.dram_tensor(f"slots{l}", [XROWS, XW], f32).ap() for l in range(2)]
    ys_d = [nc.dram_tensor(f"expert_out{l}", [TOP * TOKENS, CH], f32).ap() for l in range(2)]

    ctx = ExitStack()
    with ctx:
        def sb(name, shape, dt=f32):
            return ctx.enter_context(nc.sbuf_tensor(name, shape, dt))

        def sem(name):
            return ctx.enter_context(nc.semaphore(name))

        X = sb("X", [P, TILES, CH])
        XN = sb("XN", [P, TILES, CH])
        XNT = sb("XNT", [P, GROUPS, GT])
        BQ = sb("BQ", [P, 2, GROUPS, GT])
        O = sb("O", [P, BATCH, SEQ + 2])
        PBF = sb("PBF", [P, TOP * TILES * XW])
        PB = PBF[:, :].rearrange("p (k t c) -> p k t c", k=TOP, t=TILES)
        SQ = PBF[:, 0:4 * GT].rearrange("p (a b n) -> p a b n", a=2, b=2)
        OTM = PBF[:, 4 * GT:6 * GT].rearrange("p (b t c) -> p b t c", b=2, t=TG)
        W = sb("W", [P, 2 * WRES], f32r)
        RAW = sb("RAW", [P, 2, CHUNK])
        WQKV = sb("WQKV", [P, 3 * CH])
        WP = sb("WP", [P, CH])
        WK = sb("WK", [P, 3, CH])
        WA = sb("WA", [P, CH])
        WX = sb("WX", [P, CH])
        COLS = sb("COLS", [P, C_END])
        ROWS = sb("ROWS", [1, CH + EXPERTS])
        BIAS = sb("BIAS", [P, CH + EXPERTS])
        BD = sb("BD", [P, P])
        IDENT = sb("IDENT", [P, P])
        NLOWER = sb("NLOWER", [P, P])
        RESET = sb("RESET", [P, EXPERTS, BT])
        ONES = sb("ONES", [P, P])
        HEADM = sb("HEADM", [P, P])
        NEGHALF = sb("NEGHALF", [P, TG])
        PAD = sb("PAD", [P, XW])
        IOTA8 = sb("IOTA8", [P, EXPERTS])
        EBASE = sb("EBASE", [P, EXPERTS])
        SBASE = sb("SBASE", [P, SEGMENTS + 1])
        ESTEP = sb("ESTEP", [P, SEGMENTS])
        SOFF = sb("SOFF", [P, 2, SEGMENTS + 1])
        SLEN = sb("SLEN", [P, 2, SEGMENTS])
        SEND = sb("SEND", [P, 2, SEGMENTS + 1])
        SROW = sb("SROW", [P, 2, SEGMENTS + 1])
        SDIF = sb("SDIF", [P, 2, SEGMENTS])
        JIDX = sb("JIDX", [P, SLOT_TILES])
        KV = sb("KV", [P, BATCH, CH])
        KSB = sb("KSB", [P, BATCH, HEADS])
        VR = sb("VR", [P, 2, TG, CH + HEADS])
        S3 = sb("S3", [P, 2, TG, HEADS])
        RD = sb("RD", [P, 2, TG, HEADS])
        EPSC = sb("EPSC", [P, 1])
        ST = sb("ST", [P, 4, TILES, 6])
        MV = sb("MV", [P, 4, TILES, 2])
        VE = sb("VE", [P, 5, TILES])
        RSTD = sb("RSTD", [P, 5, TILES])
        ALAM = sb("ALAM", [P, 1])
        RSC = sb("RSC", [P, EXPERTS])
        RMS = sb("RMS", [P, TILES])
        LG = sb("LG", [P, 2, TILES, EXPERTS])
        V8 = sb("V8", [P, 2, TILES, 8])
        I8 = sb("I8", [P, 2, TILES, 8], u32)
        IF = sb("IF", [P, 2, TILES, TOP])
        OH = sb("OH", [P, 2, TILES, TOP, EXPERTS])
        M = sb("M", [P, 2, BATCH, EXPERTS, BT])
        MC = sb("MC", [P, 2, BATCH, EXPERTS, BT])
        EX = sb("EX", [P, 2, TILES, 8])
        PR = sb("PR", [P, 2, TILES, 8])
        SP8 = sb("SP8", [P, 2, BT, EXPERTS])
        SPP = sb("SPP", [P, 2, BT, TOP, EXPERTS])
        SPS = sb("SPS", [P, 2, BT, TOP, EXPERTS])
        WARM = sb("WARM", [P, 2])
        SL = sb("SL", [P, 2, TILES, TOP], i32)
        CNT = sb("CNT", [P, 2, 4, EXPERTS])
        CNTI = sb("CNTI", [P, 2, 3, EXPERTS], i32)
        TE = sb("TE", [P, 2, SLOT_TILES * SEGMENTS])
        TR = sb("TR", [P, 3, SLOT_TILES])
        TBL = sb("TBL", [P, 2, 2, SLOT_TILES], i32)
        xnt = XNT[:, :, :].rearrange("p g n -> p (g n)")
        xn = XN[:, :, :].rearrange("p t c -> p (t c)")
        XS = [xnt[:, i * XW:(i + 1) * XW] for i in range(3)]
        META = sb("META", [P, 2, SLOT_TILES, 2])
        YROW = [sb(f"YROW{i}", [P, 1], i32) for i in range(3)]
        XH = [sb(f"XH{i}", [P, P], f32r) for i in range(3)]
        XL = [sb(f"XL{i}", [P, P], f32r) for i in range(3)]
        H = [xn[:, i * HID0:(i + 1) * HID0] for i in range(3)]
        G0 = [xnt[:, 512 + i * HID1:512 + (i + 1) * HID1] for i in range(3)]
        HH = [sb(f"HH{i}", [P, HID0], f32r) for i in range(3)]
        HL = [sb(f"HL{i}", [P, HID0], f32r) for i in range(3)]
        YS = [xnt[:, 1280 + i * CH:1280 + (i + 1) * CH] for i in range(3)]

        bank = [ctx.enter_context(nc.psum_tensor(f"bank{i}", [P, 512], f32)) for i in range(8)]

        Q, K = BQ[:, 0], BQ[:, 1]
        v_bank = [bank[3], bank[7]] * 2
        num_bank = [bank[6], bank[4]] * 2
        den_bank = [bank[2], bank[1], bank[2], bank[5]]
        turn_bank = [[bank[0], bank[1], bank[3], bank[7]], [bank[0], bank[1]] * 2]
        logit_bank = [[bank[6], bank[2]], [bank[2], bank[3]]]
        rank_bank = [[bank[4], bank[5]], [bank[4], bank[5]]]

        def part(c, low):
            at = (c if c < CHUNKS0 else c - CHUNKS0) * CHUNK
            if at < UP_COLS:
                at += low * UP_COLS
                return W[:, at:at + CHUNK]
            pairs = W[:, 2 * at:2 * (at + CHUNK)].rearrange("p (n two c) -> p n two c", two=2, c=CH)
            return pairs[:, :, low, :]

        def chunk(c):
            at = (c if c < CHUNKS0 else c - CHUNKS0) * CHUNK
            raw = RAW[:, c % 2, :]
            return raw if at < UP_COLS else raw.rearrange("p (n c) -> p n c", c=CH)

        s = {}
        names = """x0 x1 x2 x3 wqkv wproj small wawx const dest wraw0 wraw1 whi wlo dumped out
          xnT_ps xnT q k v rq rk q2 k2 q3 k3 s3 r3 vr kv kvb
          num rden ot oT_ps o proj xb x1a bias_ps bias wk bd rsc alam
          t3_ps t3 r_ps i_ps r i e t2 sq at msq ix bt yscan yT xc""".split()
        for n in names:
            s[n] = sem("s_" + n)
        for n in """stats aggr ve rstd norm xs0 xs1 xs2 xt xh xl h1 gel h ht hh hl y ys yo0 yo1 yo2
              meta sent yrow ylo ysfree""".split():
            s[n] = sem("s_" + n)
        for l in range(2):
            for n in """nT_ps nT logit_ps lg exps ex sel rank_ps slot row copy scat0 scat1 rows padrow pads table
              mse rms sum half
              yl0 yl1 yl2 yl3 res chain""".split():
                s[f"{n}_{l}"] = sem(f"s_{n}_{l}")

        block = ctx.enter_context(nc.Block())

        def tile(c, i):
            return c if i is None else i * STEPS + c

        def column(c, i):
            return slice(c, c + 1) if i is None else bass.ds(i * STEPS + c, 1)

        def dma_count(c, i):
            return 16 * (c // 3 + 1) if i is None else (i * (STEPS // 3) + (c // 3 + 1)) * 16

        def pipeline(engine, step):
            for c in range(PEEL):
                step(c, None)
            with engine.Fori(0, ROUNDS) as i:
                for c in range(PEEL, PEEL + STEPS):
                    step(c, i)
            for c in range(LAST, SLOT_TILES):
                step(c, None)

        def sp_ffn(sp, l):
            B, RB = l * SLOT_TILES, l * 16 * (SLOT_TILES // 3)
            sp.wait_ge(s[f"rows_{l}"], 1)
            sp.wait_ge(s[f"scat0_{l}"], 16 * BT * TOP)

            def load(c, i):
                row = sp.value_load(TBL[0:1, l, 0, column(c, i)], min_val=0, max_val=XROWS - P)
                if c >= 3:
                    sp.wait_ge(s["meta"], tile(c, i) + (B - 2))
                sp.dma_start(XS[c % 3][:, :], slots_d[l][bass.ds(row, P), :]).then_inc(s[f"xs{c % 3}"], 16)
            for c in range(PEEL + STEPS):
                load(c, None)
                if c < EXPERTS:
                    if c == 0:
                        sp.wait_ge(s[f"padrow_{l}"], 1)
                    row = sp.value_load(CNTI[0:1, l, 0, c:c + 1], min_val=c * REG, max_val=c * REG + TOKENS)
                    sp.dma_start(slots_d[l][bass.ds(row, P), :], PAD[:, :]).then_inc(s[f"pads_{l}"], 16)
            sp.wait_ge(s[f"scat1_{l}"], 16 * BT * TOP)
            sp.wait_ge(s[f"pads_{l}"], 16 * EXPERTS)
            with sp.Fori(1, ROUNDS) as i:
                for c in range(PEEL, PEEL + STEPS):
                    load(c, i)
            for c in range(LAST, SLOT_TILES):
                load(c, None)

            for u in range(3):
                sp.wait_ge(s[f"yo{u}"], RB + 16 * (SLOT_TILES // 3))
            for g in range(GROUPS):
                for k in range(TOP):
                    r0 = k * TOKENS + g * GT
                    sp.dma_start(BQ[:, k, g].rearrange("p (t c) -> p t c", t=TG),
                                 ys_d[l][r0:r0 + GT, :].rearrange("(t p) c -> p t c", p=P)
                                 ).then_inc(s[f"yl{g}_{l}"], 16)

        @block.sync
        def _(sp):
            for g in range(GROUPS):
                sp.dma_start(X[:, g * TG:(g + 1) * TG, :], x_v[:, g * TG:(g + 1) * TG, :]
                             ).then_inc(s[f"x{g}"], 16)
                if g == 0:
                    sp.dma_start(WQKV[:, :], wqkv).then_inc(s["wqkv"], 16)

            def weights(first, end):
                for c in range(first, end):
                    if c >= 2:
                        sp.wait_ge(s["whi"], c - 1)
                        sp.wait_ge(s["wlo"], c - 1)
                    sp.dma_start(RAW[:, c % 2, :], wpack[:, c * CHUNK:(c + 1) * CHUNK]
                                 ).then_inc(s[f"wraw{c % 2}"], 16)
            weights(0, 2)
            sp.wait_ge(s["const"], CONSTS)
            for l in range(2):
                for d in range(DUMP_TILES):
                    sp.dma_start(slots_d[l][DUMP + d * P:DUMP + (d + 1) * P, :], PAD[:, :]
                                 ).then_inc(s["dumped"], 16)
            weights(2, CHUNKS0 + 2)
            sp.wait_ge(s["dumped"], 16 * 2 * DUMP_TILES)
            sp_ffn(sp, 0)
            weights(CHUNKS0 + 2, CHUNKS)
            sp_ffn(sp, 1)
            for g in range(GROUPS):
                sp.wait_ge(s["res_1"], g + 1)
                sp.dma_start(out_v[:, g * TG:(g + 1) * TG, :], X[:, g * TG:(g + 1) * TG, :]
                             ).then_inc(s["out"], 16)
            sp.wait_ge(s["out"], 16 * GROUPS)

        def pool_rstd(pool, l, g):
            sl = slice(g * TG, (g + 1) * TG)
            pool.wait_ge(s["ve"], l * GROUPS + g + 1)
            nc.gpsimd.tensor_tensor(RSTD[:, l, sl], VE[:, l, sl], NEGHALF[:, :], ALU.pow
                                    ).then_inc(s["rstd"], 1)

        def pool_rms(pool, b):
            sl = slice(b * BT, (b + 1) * BT)
            pool.wait_ge(s["mse_1"], b + 1)
            nc.gpsimd.tensor_tensor(RSTD[:, 4, sl], VE[:, 4, sl],
                                    NEGHALF[:, 0:1].to_broadcast([P, BT]), ALU.pow).then_inc(s["rms_1"], 1)

        def pool_scatter(pool, l, b, tiles):
            pool.wait_ge(s[f"slot_{l}"], b + 1)
            pool.wait_ge(s[f"row_{l}"], b + 1)
            pool.wait_ge(s[f"copy_{l}"], b + 1)
            for t in range(b * BT + tiles.start, b * BT + tiles.stop):
                for k in range(TOP):
                    nc.gpsimd.indirect_dma_start(
                        slots_d[l][:, :], bass.IndirectOffsetOnAxis(SL[:, l, t, k:k + 1], 0),
                        PB[:, k, t, :], None, bounds_check=XROWS - 1, oob_is_err=False
                    ).then_inc(s[f"scat{b}_{l}"], 16)

        def pool_ffn(pool, l):
            B, RB = l * SLOT_TILES, l * 16 * (SLOT_TILES // 3)

            def send(c, i):
                if c >= 3:
                    pool.wait_ge(s[f"yo{c % 3}"], dma_count(c - 3, i) + RB)
                pool.sem_inc(s["ysfree"], 1)
                pool.wait_ge(s["yrow"], tile(c, i) + (B + 1))
                pool.sem_inc(s["sent"], 1)
                nc.gpsimd.indirect_dma_start(
                    ys_d[l][:, :], bass.IndirectOffsetOnAxis(YROW[c % 3][:, :], 0),
                    YS[c % 3][:, :], None, bounds_check=TOP * TOKENS - 1, oob_is_err=False
                ).then_inc(s[f"yo{c % 3}"], 16)
            pipeline(pool, send)

        def pool_sum(pool, l, g):
            pool.wait_ge(s[f"yl{g}_{l}"], 16 * TOP)
            nc.gpsimd.tensor_tensor(Q[:, g], Q[:, g], K[:, g], ALU.add).then_inc(s[f"sum_{l}"], 1)

        @block.gpsimd
        def _(pool):
            g_ = nc.gpsimd
            c = [0]

            def const(ins, wait=True):
                c[0] += 1
                ins.then_inc(s["const"], 1)
                if wait:
                    pool.wait_ge(s["const"], c[0])
            const(g_.memset(NEGHALF[:, :], -0.5), False)
            const(g_.memset(ONES[:, :], 1.0), False)
            const(g_.memset(IDENT[:, :], 0.0), False)
            const(g_.memset(NLOWER[:, :], -1.0), False)
            const(g_.memset(RESET[:, :, :], 1.0), False)
            const(g_.memset(HEADM[:, :], 1.0), False)
            const(g_.memset(PAD[:, :], 0.0))
            const(g_.affine_select(out=IDENT[:, :], in_=IDENT[:, :], compare_op=ALU.not_equal, fill=1.0,
                                   base=0, pattern=[[-1, P]], channel_multiplier=1), False)
            const(g_.affine_select(out=NLOWER[:, :], in_=NLOWER[:, :], compare_op=ALU.is_ge, fill=0.0,
                                   base=0, pattern=[[-1, P]], channel_multiplier=1), False)
            const(g_.memset(RESET[:, :, 0:1], 0.0), False)
            hm = HEADM[:, :].rearrange("p (h d) -> p h d", d=HD)
            const(g_.affine_select(out=hm, in_=hm, compare_op=ALU.is_ge, fill=0.0,
                                   base=0, pattern=[[-HD, HEADS], [0, HD]], channel_multiplier=1))
            const(g_.affine_select(out=hm, in_=hm, compare_op=ALU.is_ge, fill=0.0,
                                   base=HD - 1, pattern=[[HD, HEADS], [0, HD]], channel_multiplier=-1), False)
            const(g_.memset(PAD[:, CH:CH + 1], float(NO_ROW)), False)
            for b in range(BATCH):
                const(g_.memset(O[:, b, 0:1], 0.0), False)
                const(g_.memset(O[:, b, SEQ + 1:SEQ + 2], 0.0), False)
            const(g_.memset(EPSC[:, :], FOCUS_EPS), False)
            const(g_.iota(IOTA8[:, :], pattern=[[1, EXPERTS]], base=0, channel_multiplier=0,
                          allow_small_or_imprecise_dtypes=True), False)
            const(g_.iota(SBASE[:, 0:SEGMENTS].rearrange("p (a e) -> p a e", a=2),
                          pattern=[[0, 2], [REG, EXPERTS]], base=0, channel_multiplier=0,
                          allow_small_or_imprecise_dtypes=True), False)
            const(g_.memset(SBASE[:, SEGMENTS:], float(DUMP)), False)
            const(g_.memset(ESTEP[:, :], 1.0), False)
            const(g_.memset(SOFF[:, :, :], 0.0), False)
            const(g_.memset(SEND[:, :, 0:1], 0.0))
            const(g_.memset(ESTEP[:, EXPERTS - 1:EXPERTS], float(1 - EXPERTS)), False)
            const(g_.memset(ESTEP[:, SEGMENTS - 1:], 0.0), False)
            const(g_.iota(EBASE[:, :], pattern=[[REG, EXPERTS]], base=0, channel_multiplier=0,
                          allow_small_or_imprecise_dtypes=True), False)
            const(g_.iota(JIDX[:, :], pattern=[[1, SLOT_TILES]], base=0, channel_multiplier=0,
                          allow_small_or_imprecise_dtypes=True))
            assert c[0] == CONSTS, c[0]

            for g in range(GROUPS):
                pool_rstd(pool, 0, g)
            wl = [0]

            def low(n, end=LOW_POOL):
                for _ in range(n):
                    k = wl[0]
                    if k >= end:
                        return
                    wl[0] += 1
                    pool.wait_ge(s["whi"], k + 1)
                    g_.tensor_tensor(part(k, 1), chunk(k), part(k, 0).bitcast(f32), ALU.subtract
                                     ).then_inc(s["wlo"], 1)
            pool.wait_ge(s["bias"], 1)
            for g in range(GROUPS):
                pool.wait_ge(s["norm"], TG * (g + 1))
                g_.tensor_tensor(X[:, g * TG:(g + 1) * TG, :], X[:, g * TG:(g + 1) * TG, :],
                                 BIAS[:, 0:CH].unsqueeze(1).to_broadcast([P, TG, CH]), ALU.add
                                 ).then_inc(s["xb"], 1)
                low(1)
            pool_rstd(pool, 1, 0)
            pool_rstd(pool, 1, 1)
            pool.wait_ge(s["o"], GROUPS)
            g_.iota(PB[:, :, :, CH:CH + 1].rearrange("p k t a -> p k (t a)"),
                    pattern=[[TOKENS, TOP], [P, TILES]], base=0, channel_multiplier=1,
                    allow_small_or_imprecise_dtypes=True).then_inc(s["dest"], 1)
            low(1)
            pool.wait_ge(s["dest"], 1)
            pool_scatter(pool, 0, 0, range(0, 2))
            pool_rstd(pool, 1, 2)
            pool_rstd(pool, 1, 3)
            pool_scatter(pool, 0, 0, range(2, BT))
            pool_scatter(pool, 0, 1, range(BT))
            pool_ffn(pool, 0)
            for b in range(BATCH):
                pool_sum(pool, 0, b * BG + 1)
                for g in range(b * BG, (b + 1) * BG):
                    pool_rstd(pool, 2, g)

            def gated_in(g):
                pool.wait_ge(s["i"], g + 1)
                g_.tensor_tensor(K[:, g], K[:, g], XNT[:, g], ALU.mult).then_inc(s["ix"], 1)
            gated_in(0)
            gated_in(1)
            pool_rstd(pool, 3, 0)
            pool_rstd(pool, 3, 1)
            pool_rms(pool, 0)
            gated_in(2)
            gated_in(3)
            pool_scatter(pool, 1, 0, range(0, 3))
            pool_rstd(pool, 3, 2)
            pool_rstd(pool, 3, 3)
            pool_scatter(pool, 1, 0, range(3, 4))
            pool_rms(pool, 1)
            pool_scatter(pool, 1, 0, range(4, BT))
            pool_scatter(pool, 1, 1, range(BT))
            pool_ffn(pool, 1)
            for g in range(1, GROUPS, 2):
                pool_sum(pool, 1, g)

        def act_copy(act, dst, src, sm):
            nc.scalar.activation(dst, src, ACT.Copy).then_inc(s[sm], 1)

        def act_turned(act, l, g):
            act.wait_ge(s[f"nT_ps_{l}"], g + 1)
            act_copy(act, XNT[:, g], turn_bank[l][g][:, :], f"nT_{l}")

        def act_second(act, l, b):
            sl = slice(b * BT, (b + 1) * BT)
            act.wait_ge(s["norm"], (2 * l + 1) * TILES + BT * (b + 1))
            act_copy(act, PB[:, 1, sl, 0:CH], PB[:, 0, sl, 0:CH], f"copy_{l}")

        def act_exps(act, l, b):
            sl = slice(b * BT, (b + 1) * BT)
            act.wait_ge(s[f"exps_{l}"], b + 1)
            nc.scalar.activation(EX[:, l, sl], EX[:, l, sl], ACT.Exp).then_inc(s[f"ex_{l}"], 1)

        def act_ffn(act, l):
            B, RB = l * SLOT_TILES, l * 16 * (SLOT_TILES // 3)
            F = HID0 if l == 0 else HID1

            def first(c, i):
                act.wait_ge(s["xt"], tile(c, i) + (B + 1))
                act_copy(act, XH[c % 3][:, :], bank[0][:, 0:P], "xh")

            def gelu(c, i):
                act.wait_ge(s["h1"], tile(c, i) + (B + 1))
                if l == 0:
                    nc.scalar.activation(H[c % 3][:, :], bank[1 + c % 3][:, :], ACT.Gelu).then_inc(s["gel"], 1)
                else:
                    nc.scalar.activation(G0[c % 3][:, :], bank[1 + c % 3][:, 0:F], ACT.Gelu_apprx_tanh
                                         ).then_inc(s["gel"], 1)

            def high(c, i):
                act.wait_ge(s["ht"], tile(c, i) + (B + 1))
                act_copy(act, HH[c % 3][:, 0:F], bank[4 + c % 2][:, 0:F], "hh")

            def weigh_low(c, i):
                act.wait_ge(s["y"], tile(c, i) + (B + 1))
                act.wait_ge(s["ysfree"], tile(c, i) + (B + 1))
                nc.scalar.activation(YS[c % 3][:, :], bank[6 + c % 2][:, CH:2 * CH], ACT.Copy,
                                     scale=META[:, l, column(c, i), 1]).then_inc(s["ylo"], 1)

            def step(c, i):
                if c + 1 < SLOT_TILES:
                    first(c + 1, i)
                if c >= 3:
                    weigh_low(c - 3, i)
                gelu(c, i)
                if c >= 1:
                    high(c - 1, i)
            first(0, None)
            pipeline(act, step)
            weigh_low(SLOT_TILES - 3, None)
            high(SLOT_TILES - 1, None)
            weigh_low(SLOT_TILES - 2, None)
            weigh_low(SLOT_TILES - 1, None)

        @block.scalar
        def _(act):
            a_ = nc.scalar
            act.dma_start(COLS[:, :], cols).then_inc(s["small"], 16)
            act.dma_start(ROWS[:, :], rows).then_inc(s["small"], 16)
            act.dma_start(WP[:, :], wproj).then_inc(s["wproj"], 16)
            act.dma_start(WA[:, :], wa).then_inc(s["wawx"], 16)
            act.dma_start(WX[:, :], wx).then_inc(s["wawx"], 16)
            wh = [0]

            def high(n, end=CHUNKS0):
                for _ in range(n):
                    k = wh[0]
                    if k >= end:
                        return
                    wh[0] += 1
                    act.wait_ge(s[f"wraw{k % 2}"], 16 * (k // 2 + 1))
                    act_copy(act, part(k, 0), chunk(k), "whi")
            act.wait_ge(s["bias_ps"], 1)
            act_copy(act, BIAS[:, :], bank[7][:, 0:CH + EXPERTS], "bias")

            def turned(g):
                act.wait_ge(s["xnT_ps"], g + 1)
                act_copy(act, XNT[:, g], bank[g % 2][:, :], "xnT")

            def squares(g):
                act.wait_ge(s["k"], g + 1)
                a_.activation(K[:, g], bank[2][:, :], ACT.Relu).then_inc(s["rk"], 1)
                act.wait_ge(s["rk"], g + 1)
                if g >= 2:
                    act.wait_ge(s["k3"], g - 1)
                a_.activation(SQ[:, 1, g % 2], K[:, g], ACT.Square, bias=EPSC[:, :]).then_inc(s["k2"], 1)
                act.wait_ge(s["q"], g + 1)
                a_.activation(Q[:, g], bank[4][:, :], ACT.Relu).then_inc(s["rq"], 1)
                act.wait_ge(s["rq"], g + 1)
                if g >= 2:
                    act.wait_ge(s["q3"], g - 1)
                a_.activation(SQ[:, 0, g % 2], Q[:, g], ACT.Square, bias=EPSC[:, :]).then_inc(s["q2"], 1)

            def attention_out(g):
                act.wait_ge(s["oT_ps"], g + 1)
                act_copy(act, O[:, g // 2, 1 + (g % 2) * GT:1 + (g % 2 + 1) * GT], v_bank[g][:, :],
                         "o")
            turned(0)
            for g in range(GROUPS):
                if g + 1 < GROUPS:
                    turned(g + 1)
                squares(g)
                if g < 2:
                    high(1)
            high(1)
            attention_out(0)
            attention_out(1)
            high(1)
            attention_out(2)
            high(1)
            attention_out(3)
            act_turned(act, 0, 0)
            act_turned(act, 0, 1)
            act_second(act, 0, 0)
            act_exps(act, 0, 0)
            high(2)
            act_turned(act, 0, 2)
            act_turned(act, 0, 3)
            high(CHUNKS0)
            act_second(act, 0, 1)
            act_exps(act, 0, 1)
            a_.activation(WARM[:, 0:1], EPSC[:, :], ACT.Gelu)
            act_ffn(act, 0)
            act.wait_ge(s["y"], SLOT_TILES)
            high(2, CHUNKS)
            act.wait_ge(s["small"], 32)
            a_.activation(ALAM[:, :], COLS[:, C_LAM:C_LAM + 1], ACT.Sigmoid).then_inc(s["alam"], 1)

            def turned_in(g):
                act.wait_ge(s["t3_ps"], g + 1)
                act_copy(act, XNT[:, g], bank[g % 2][:, :], "t3")

            def gates(g):
                act.wait_ge(s["res_0"], g + 1)
                act.wait_ge(s["r_ps"], g + 1)
                a_.activation(Q[:, g], bank[2 + g % 2][:, :], ACT.Sigmoid,
                              bias=COLS[:, C_BA:C_BA + 1]).then_inc(s["r"], 1)
                act.wait_ge(s["i_ps"], g + 1)
                a_.activation(K[:, g], bank[4 + g % 2][:, :], ACT.Sigmoid,
                              bias=COLS[:, C_BX:C_BX + 1]).then_inc(s["i"], 1)

            def decay(groups):
                for g in groups:
                    act.wait_ge(s["r"], g + 1)
                    a_.activation(Q[:, g], Q[:, g], ACT.Exp, scale=-float(np.log(8.0))).then_inc(s["e"], 1)

            def scale_in(groups):
                for g in groups:
                    act.wait_ge(s["t2"], g + 1)
                    a_.activation(XN[:, g * TG:(g + 1) * TG], XN[:, g * TG:(g + 1) * TG],
                                  ACT.Sqrt, scale=-1.0, bias=ONES[:, 0:1]).then_inc(s["sq"], 1)
            turned_in(0)
            turned_in(1)
            gates(0)
            gates(1)
            decay((0, 1))
            scale_in((0, 1))
            turned_in(2)
            turned_in(3)
            gates(2)
            gates(3)
            decay((2, 3))
            act_turned(act, 1, 0)
            act_turned(act, 1, 1)
            act_second(act, 1, 0)
            act_exps(act, 1, 0)
            scale_in((2, 3))
            high(2, CHUNKS)
            act_turned(act, 1, 2)
            act_turned(act, 1, 3)
            act_second(act, 1, 1)
            act_exps(act, 1, 1)
            high(CHUNKS, CHUNKS)
            a_.activation(WARM[:, 1:2], EPSC[:, :], ACT.Gelu_apprx_tanh)
            act_ffn(act, 1)

        def transposes(pe, dst, src, g, ln, sm_out):
            for t in range(TG):
                if ln is not None:
                    pe.wait_ge(s["norm"], ln * TILES + g * TG + t + 1)
                last = nc.tensor.transpose(dst[:, t * P:(t + 1) * P], src(t), IDENT[:, :])
            last.then_inc(s[sm_out], 1)

        def pe_turn(pe, l, g):
            if l == 1 and g >= 2:
                pe.wait_ge(s["nT_1"], g - 1)
            transposes(pe, turn_bank[l][g], lambda t: PB[:, 0, g * TG + t, 0:CH], g, 2 * l + 1, f"nT_ps_{l}")

        def pe_logits(pe, l, b):
            if l == 1:
                pe.wait_ge(s["rsc"], 1)
            rw = COLS[:, C_R0:C_R0 + EXPERTS] if l == 0 else RSC[:, :]
            for g in range(b * BG, (b + 1) * BG):
                pe.wait_ge(s[f"nT_{l}"], g + 1)
                for t in range(TG):
                    at = ((g % BG) * TG + t) * EXPERTS
                    last = nc.tensor.matmul(logit_bank[l][b][:, at:at + EXPERTS], XNT[:, g, t * P:(t + 1) * P],
                                            rw, start=True, stop=True)
            last.then_inc(s[f"logit_ps_{l}"], 1)

        def pe_rank(pe, l, b):
            pe.wait_ge(s[f"sel_{l}"], b + 1)
            o = rank_bank[l][b][:, 0:BT * EXPERTS].rearrange("p (t e) -> p t e", e=EXPERTS)
            nc.tensor.matmul(o, NLOWER[:, :], M[:, l, b].rearrange("p e t -> p t e"), start=True, stop=False)
            nc.tensor.matmul(o, ONES[:, :], MC[:, l, b].rearrange("p e t -> p t e"), start=False, stop=(b == 0))
            n = rank_bank[l][b][:, BT * EXPERTS:(BT + 1) * EXPERTS]
            before = MC[:, l, 0, :, BT - 1]
            if b == 1:
                nc.tensor.matmul(o, ONES[:, :], before.unsqueeze(1).to_broadcast([P, BT, EXPERTS]),
                                 start=False, stop=True)
            last = nc.tensor.matmul(n, ONES[:, :], before, start=True, stop=(b == 0))
            if b == 1:
                last = nc.tensor.matmul(n, ONES[:, :], MC[:, l, 1, :, BT - 1], start=False, stop=True)
            last.then_inc(s[f"rank_ps_{l}"], 1)

        def pe_ffn(pe, l):
            B, RB = l * SLOT_TILES, l * 16 * (SLOT_TILES // 3)
            F = HID0 if l == 0 else HID1
            up_h, up_l = (W[:, i * UP_COLS:(i + 1) * UP_COLS].rearrange("p (e n) -> p e n", e=EXPERTS)
                          for i in range(2))
            dn = W[:, 2 * UP_COLS:2 * UP_COLS + 2 * EXPERTS * F].rearrange("p (e k n) -> p e k n", e=EXPERTS, n=2 * CH)
            held = [pe.alloc_register(f"expert{u}_{l}") for u in range(STEPS)]

            def fetch(c, i):
                pe.reg_load(held[c % STEPS], TBL[0:1, l, 1, column(c, i)])

            known = {}

            def expert(c):
                if c not in known:
                    known[c] = pe.snap(held[c % STEPS], min_val=0, max_val=EXPERTS - 1)
                return known[c]

            def xpose(c, i):
                pe.wait_ge(s[f"xs{c % 3}"], dma_count(c, i) + RB)
                if c >= 1:
                    pe.wait_ge(s["xl"], tile(c, i) + B)
                nc.tensor.transpose(bank[0][:, 0:P], XS[c % 3][:, 0:CH], IDENT[:, :]).then_inc(s["xt"], 1)

            def up(c):
                e = expert(c)
                o = bank[1 + c % 3][:, :]
                nc.tensor.matmul(o, XH[c % 3][:, :], up_h[:, bass.ds(e, 1), :], start=True, stop=False)
                nc.tensor.matmul(o, XH[c % 3][:, :], up_l[:, bass.ds(e, 1), :], start=False, stop=False)
                nc.tensor.matmul(o, XL[c % 3][:, :], up_h[:, bass.ds(e, 1), :], start=False, stop=True
                                 ).then_inc(s["h1"], 1)

            def hxpose(c, i):
                if l == 0:
                    pe.wait_ge(s["gel"], tile(c, i) + 1)
                else:
                    pe.wait_ge(s["h"], tile(c, i) + 1)
                for k in range(F // P):
                    last = nc.tensor.transpose(bank[4 + c % 2][:, k * P:(k + 1) * P],
                                               H[c % 3][:, k * P:(k + 1) * P], IDENT[:, :])
                last.then_inc(s["ht"], 1)

            def down(c, i):
                e = expert(c)
                pe.wait_ge(s["hl"], tile(c, i) + (B + 1))
                if c >= 2:
                    pe.wait_ge(s["ys"], tile(c, i) + (B - 1))
                nk, o = F // P, bank[6 + c % 2]
                for k in range(nk):
                    ks = slice(k * P, (k + 1) * P)
                    nc.tensor.matmul(o[:, 0:2 * CH], HH[c % 3][:, ks], dn[:, bass.ds(e, 1), k, :],
                                     start=(k == 0), stop=False)
                for k in range(nk):
                    ks = slice(k * P, (k + 1) * P)
                    last = nc.tensor.matmul(o[:, 0:CH], HL[c % 3][:, ks], dn[:, bass.ds(e, 1), k, 0:CH],
                                            start=False, stop=(k == nk - 1))
                last.then_inc(s["y"], 1)

            def step(c, i):
                if c in (PEEL, LAST):
                    known.clear()
                if c + 1 < SLOT_TILES:
                    xpose(c + 1, i)
                else:
                    pe.wait_ge(s["xl"], B + SLOT_TILES)
                up(c)
                if c + 1 < SLOT_TILES:
                    fetch(c + 1, i)
                if c >= 1:
                    hxpose(c - 1, i)
                if c >= 2:
                    down(c - 2, i)
            pe.wait_ge(s[f"table_{l}"], 1)
            fetch(0, None)
            xpose(0, None)
            pipeline(pe, step)
            hxpose(SLOT_TILES - 1, None)
            down(SLOT_TILES - 2, None)
            down(SLOT_TILES - 1, None)

        @block.tensor
        def _(pe):
            mm = nc.tensor.matmul
            pe.wait_ge(s["const"], CONSTS)
            pe.wait_ge(s["small"], 32)
            pe.wait_ge(s["wproj"], 16)
            pe.wait_ge(s["bd"], 1)
            mm(bank[7][:, 0:CH], BD[:, :], WP[:, :], start=True, stop=False)
            mm(bank[7][:, 0:CH], ONES[0:1, :], ROWS[0:1, 0:CH], start=False, stop=True)
            mm(bank[7][:, CH:CH + EXPERTS], ONES[0:1, :], ROWS[0:1, CH:CH + EXPERTS], start=True, stop=True
               ).then_inc(s["bias_ps"], 1)

            def turn(g):
                if g >= 2:
                    pe.wait_ge(s["xnT"], g - 1)
                transposes(pe, bank[g % 2], lambda t: XN[:, g * TG + t, :], g, 0, "xnT_ps")

            def project(g):
                if g == 0:
                    pe.wait_ge(s["wqkv"], 16)
                    pe.wait_ge(s["bias"], 1)
                pe.wait_ge(s["xnT"], g + 1)
                if g >= 1:
                    pe.wait_ge(s["rk"], g)
                for t in range(TG):
                    last = mm(bank[2][:, t * P:(t + 1) * P], XNT[:, g, t * P:(t + 1) * P],
                              WQKV[:, CH:2 * CH], start=True, stop=True)
                last.then_inc(s["k"], 1)
                if g >= 1:
                    pe.wait_ge(s["rq"], g)
                mm(bank[4][:, :], WQKV[:, 0:CH], XNT[:, g], start=True, stop=True).then_inc(s["q"], 1)
                if g >= 2:
                    pe.wait_ge(s["vr"], g - 1)
                for t in range(TG):
                    last = mm(v_bank[g][:, t * P:(t + 1) * P], XNT[:, g, t * P:(t + 1) * P],
                              WQKV[:, 2 * CH:3 * CH], start=True, stop=True)
                last.then_inc(s["v"], 1)

            def kv_sum(g):
                pe.wait_ge(s["k3"], g + 1)
                pe.wait_ge(s["vr"], g + 1)
                if g == 2:
                    pe.wait_ge(s["kvb"], 2)
                for t in range(TG):
                    last = mm(bank[5][:, 0:CH + HEADS], K[:, g, t * P:(t + 1) * P], VR[:, g % 2, t, :],
                              start=(g % 2 == 0 and t == 0), stop=(g % 2 == 1 and t == TG - 1))
                last.then_inc(s["kv"], 1)

            def attend(g):
                pe.wait_ge(s["kvb"], 2 * (g // 2 + 1))
                pe.wait_ge(s["q3"], g + 1)
                pe.wait_ge(s["rk"], GROUPS)
                pe.wait_ge(s["rq"], GROUPS)
                pe.wait_ge(s["xnT"], GROUPS)
                if g >= 2:
                    pe.wait_ge(s["ot"], g - 1)
                for t in range(TG):
                    q_t = Q[:, g, t * P:(t + 1) * P]
                    mm(num_bank[g][:, t * P:(t + 1) * P], q_t, KV[:, g // 2], start=True, stop=True)
                    last = mm(den_bank[g][:, t * HEADS:(t + 1) * HEADS], q_t, KSB[:, g // 2], start=True, stop=True)
                last.then_inc(s["num"], 1)

            def turn_out(g):
                pe.wait_ge(s["ot"], g + 1)
                pe.wait_ge(s["vr"], GROUPS - 1 + g % 2)
                if g >= 2:
                    pe.wait_ge(s["o"], g - 1)
                transposes(pe, v_bank[g], lambda t: OTM[:, g % 2, t, :], g, None, "oT_ps")

            def output(g):
                pe.wait_ge(s["o"], 2 * (g // 2) + 2)
                pe.wait_ge(s["wk"], 3)
                pe.wait_ge(s["xnT"], GROUPS)
                if g >= 2:
                    pe.wait_ge(s["x1a"], g - 1)
                    pe.wait_ge(s["nT_0"], g - 1)
                b, first = g // 2, (g % 2) * GT
                for t in range(TG):
                    for k in range(3):
                        at = first + t * P + k
                        last = mm(bank[g % 2][:, t * P:(t + 1) * P], O[:, b, at:at + P], WK[:, k, :],
                                  start=(k == 0), stop=(k == 2))
                last.then_inc(s["proj"], 1)

            turn(0)
            turn(1)
            project(0)
            turn(2)
            project(1)
            kv_sum(0)
            turn(3)
            project(2)
            kv_sum(1)
            project(3)
            attend(0)
            attend(1)
            kv_sum(2)
            turn_out(0)
            turn_out(1)
            kv_sum(3)
            output(0)
            output(1)
            attend(2)
            attend(3)
            turn_out(2)
            turn_out(3)
            pe_turn(pe, 0, 0)
            pe_turn(pe, 0, 1)
            pe_logits(pe, 0, 0)
            output(2)
            pe_rank(pe, 0, 0)
            output(3)

            pe_turn(pe, 0, 2)
            pe_turn(pe, 0, 3)
            pe_logits(pe, 0, 1)
            pe_rank(pe, 0, 1)
            pe_ffn(pe, 0)
            pe.wait_ge(s["wawx"], 32)

            def turned_in(g):
                if g >= 2:
                    pe.wait_ge(s["t3"], g - 1)
                transposes(pe, bank[g % 2], lambda t: XN[:, g * TG + t, :], g, 2, "t3_ps")

            def gate_products(g):
                pe.wait_ge(s["t3"], g + 1)
                if g >= 2:
                    pe.wait_ge(s["i"], g - 1)
                mm(bank[2 + g % 2][:, :], WA[:, :], XNT[:, g], start=True, stop=True).then_inc(s["r_ps"], 1)
                mm(bank[4 + g % 2][:, :], WX[:, :], XNT[:, g], start=True, stop=True).then_inc(s["i_ps"], 1)

            def scanned(g):
                pe.wait_ge(s["yscan"], g + 1)
                if g >= 2:
                    pe.wait_ge(s["xc"], g - 1)
                b, first = g // 2, 1 + (g % 2) * GT
                transposes(pe, bank[6 + g % 2], lambda t: O[:, b, first + t * P:first + (t + 1) * P], g,
                           None, "yT")
            turned_in(0)
            turned_in(1)
            gate_products(0)
            gate_products(1)
            turned_in(2)
            turned_in(3)
            pe.wait_ge(s["ys"], SLOT_TILES)
            scanned(0)
            scanned(1)
            gate_products(2)
            gate_products(3)
            pe.wait_ge(s["r"], GROUPS)
            pe.wait_ge(s["i"], GROUPS)
            pe_turn(pe, 1, 0)
            pe_turn(pe, 1, 1)
            pe_logits(pe, 1, 0)
            pe_rank(pe, 1, 0)
            scanned(2)
            scanned(3)
            pe_turn(pe, 1, 2)
            pe_turn(pe, 1, 3)
            pe_logits(pe, 1, 1)
            pe_rank(pe, 1, 1)
            pe_ffn(pe, 1)

        def ln_stats(v, l, g, src):
            for t in range(g * TG, (g + 1) * TG):
                nc.vector.bn_stats(ST[:, l, t], src(t)).then_inc(s["stats"], 1)
            for t in range(g * TG, (g + 1) * TG):
                v.wait_ge(s["stats"], l * TILES + t + 1)
                nc.vector.bn_aggr(MV[:, l, t], ST[:, l, t]).then_inc(s["aggr"], 1)
            v.wait_ge(s["aggr"], l * TILES + TG * (g + 1))
            sl = slice(g * TG, (g + 1) * TG)
            nc.vector.tensor_scalar_add(VE[:, l, sl], MV[:, l, sl, 1], LN_EPS).then_inc(s["ve"], 1)

        def ln_norm(v, l, g, src, dst):
            v.wait_ge(s["rstd"], l * GROUPS + g + 1)
            for t in range(g * TG, (g + 1) * TG):
                nc.vector.tensor_scalar(dst(t), src(t), MV[:, l, t, 0:1], RSTD[:, l, t:t + 1],
                                        ALU.subtract, ALU.mult).then_inc(s["norm"], 1)

        def dve_mse(v, b):
            sl = slice(b * BT, (b + 1) * BT)
            v.wait_ge(s["rstd"], 3 * GROUPS + BG * (b + 1))
            ve = VE[:, 4, sl]
            nc.vector.tensor_tensor(ve, MV[:, 3, sl, 1], RSTD[:, 3, sl], ALU.mult).then_inc(s["msq"], 1)
            v.wait_ge(s["msq"], 2 * b + 1)
            nc.vector.tensor_tensor(ve, ve, RSTD[:, 3, sl], ALU.mult).then_inc(s["msq"], 1)
            v.wait_ge(s["msq"], 2 * b + 2)
            nc.vector.tensor_scalar_add(ve, ve, RMS_EPS).then_inc(s["mse_1"], 1)

        def dve_route(v, l, b, chain):
            V = nc.vector
            sl = slice(b * BT, (b + 1) * BT)

            def link(ins):
                chain[0] += 1
                ins.then_inc(s[f"chain_{l}"], 1)
                v.wait_ge(s[f"chain_{l}"], chain[0])

            def plain(ins):
                chain[0] += 1
                ins.then_inc(s[f"chain_{l}"], 1)
            logit = logit_bank[l][b][:, 0:BT * EXPERTS].rearrange("p (t e) -> p t e", e=EXPERTS)
            v.wait_ge(s[f"logit_ps_{l}"], b + 1)
            V.tensor_copy(LG[:, l, sl], logit).then_inc(s[f"lg_{l}"], 1)
            v.wait_ge(s[f"lg_{l}"], b + 1)
            for t in range(b * BT, (b + 1) * BT):
                plain(V.max(V8[:, l, t], LG[:, l, t]))
            v.wait_ge(s[f"chain_{l}"], chain[0])
            for t in range(b * BT, (b + 1) * BT):
                plain(V.max_index(I8[:, l, t], V8[:, l, t], LG[:, l, t]))
            v.wait_ge(s[f"chain_{l}"], chain[0])
            link(V.tensor_copy(IF[:, l, sl], I8[:, l, sl, 0:TOP]))
            full = [P, BT, TOP, EXPERTS]
            link(V.tensor_tensor(OH[:, l, sl], IOTA8[:, :].unsqueeze(1).unsqueeze(1).to_broadcast(full),
                                 IF[:, l, sl].unsqueeze(3).to_broadcast(full), ALU.is_equal))
            link(V.tensor_tensor(M[:, l, b].rearrange("p e t -> p t e"), OH[:, l, sl, 0], OH[:, l, sl, 1], ALU.add))
            flat = "p e t -> p (e t)"
            V.tensor_tensor_scan(MC[:, l, b].rearrange(flat), RESET[:, :, :].rearrange(flat),
                                 M[:, l, b].rearrange(flat), 0.0, ALU.mult, ALU.add
                                 ).then_inc(s[f"sel_{l}"], 1)
            less = V.tensor_tensor(EX[:, l, sl], V8[:, l, sl], V8[:, l, sl, 0:1].to_broadcast([P, BT, 8]),
                                   ALU.subtract)
            if l == 0:
                less.then_inc(s["exps_0"], 1)
            else:
                plain(less)
                v.wait_ge(s["rms_1"], b + 1)
                link(V.tensor_scalar_mul(RMS[:, sl], RSTD[:, 4, sl], float(np.float32(CH) ** np.float32(-0.5))))
                V.tensor_tensor(EX[:, l, sl], EX[:, l, sl], RMS[:, sl].unsqueeze(2).to_broadcast([P, BT, 8]),
                                ALU.mult).then_inc(s["exps_1"], 1)

        def dve_slots(v, l, b, chain):
            V = nc.vector
            sl = slice(b * BT, (b + 1) * BT)

            def link(ins):
                chain[0] += 1
                ins.then_inc(s[f"chain_{l}"], 1)
                v.wait_ge(s[f"chain_{l}"], chain[0])
            v.wait_ge(s[f"rank_ps_{l}"], b + 1)
            rank = rank_bank[l][b][:, 0:BT * EXPERTS].rearrange("p (t e) -> p t e", e=EXPERTS)
            sp8, spp = SP8[:, b], SPP[:, b]
            full = [P, BT, TOP, EXPERTS]
            link(V.tensor_tensor(sp8, rank, EBASE[:, :].unsqueeze(1).to_broadcast([P, BT, EXPERTS]), ALU.add))
            link(V.tensor_tensor(spp, sp8.unsqueeze(2).to_broadcast(full), OH[:, l, sl], ALU.mult))
            with nc.allow_low_precision(reason="whole numbers below 2**24: exact"):
                V.tensor_reduce(SL[:, l, sl], spp, AX.X, ALU.add).then_inc(s[f"slot_{l}"], 1)

        def dve_weights(v, l, b, chain):
            V = nc.vector
            sl = slice(b * BT, (b + 1) * BT)

            def link(ins):
                chain[0] += 1
                ins.then_inc(s[f"chain_{l}"], 1)
                v.wait_ge(s[f"chain_{l}"], chain[0])
            full = [P, BT, TOP, EXPERTS]
            v.wait_ge(s[f"ex_{l}"], b + 1)
            pr = PR[:, l, sl]
            two = [P, BT, TOP]
            link(V.tensor_reduce(pr[:, :, 0:1], EX[:, l, sl], AX.X, ALU.add))
            link(V.reciprocal(pr[:, :, 1:2], pr[:, :, 0:1]))
            prob = pr[:, :, 2:4]
            link(V.tensor_tensor(prob, EX[:, l, sl, 0:TOP], pr[:, :, 1:2].to_broadcast(two), ALU.mult))
            link(V.tensor_tensor(pr[:, :, 4:5], prob[:, :, 0:1], prob[:, :, 1:2], ALU.add))
            if l == 1:
                link(V.tensor_scalar(pr[:, :, 6:7], pr[:, :, 4:5], 0.0, None, ALU.is_gt))
                link(V.tensor_tensor(pr[:, :, 4:5], pr[:, :, 4:5], pr[:, :, 6:7], ALU.mult))
                link(V.tensor_scalar(pr[:, :, 6:7], pr[:, :, 6:7], -1.0, 1.0, ALU.mult, ALU.add))
                link(V.tensor_tensor(pr[:, :, 4:5], pr[:, :, 4:5], pr[:, :, 6:7], ALU.add))
            link(V.reciprocal(pr[:, :, 5:6], pr[:, :, 4:5]))
            wt = PB[:, :, sl, CH + 1:CH + 2].rearrange("p k t a -> p t (k a)")
            if l == 0:
                V.tensor_tensor(wt, prob, pr[:, :, 5:6].to_broadcast(two), ALU.mult).then_inc(s["row_0"], 1)
            else:
                link(V.tensor_tensor(prob, prob, pr[:, :, 5:6].to_broadcast(two), ALU.mult))
                spp = SPS[:, b]
                link(V.tensor_tensor(spp, OH[:, l, sl],
                                     BIAS[:, CH:].unsqueeze(1).unsqueeze(1).to_broadcast(full), ALU.mult))
                link(V.tensor_reduce(pr[:, :, 6:8], spp, AX.X, ALU.add))
                V.tensor_tensor(wt, prob, pr[:, :, 6:8], ALU.mult).then_inc(s["row_1"], 1)

        def dve_early(v, l, chain):
            V = nc.vector

            def link(ins):
                chain[0] += 1
                ins.then_inc(s[f"chain_{l}"], 1)
                v.wait_ge(s[f"chain_{l}"], chain[0])
            n = rank_bank[l][0][:, BT * EXPERTS:(BT + 1) * EXPERTS]
            link(V.tensor_copy(CNTI[:, l, 1], n))
            link(V.tensor_single_scalar(CNTI[:, l, 2], CNTI[:, l, 1], P.bit_length() - 1, ALU.logical_shift_right))
            link(V.tensor_copy(SLEN[:, l, 0:EXPERTS], CNTI[:, l, 2]))
            link(V.tensor_copy(SOFF[:, l, EXPERTS:SEGMENTS], CNTI[:, l, 2]))

        def dve_table(v, l, chain, make_low_parts):
            V = nc.vector

            def link(ins):
                chain[0] += 1
                ins.then_inc(s[f"chain_{l}"], 1)
                v.wait_ge(s[f"chain_{l}"], chain[0])
            v.wait_ge(s[f"rank_ps_{l}"], BATCH)
            n = rank_bank[l][1][:, BT * EXPERTS:(BT + 1) * EXPERTS]
            V.tensor_tensor(CNTI[:, l, 0], n, EBASE[:, :], ALU.add).then_inc(s[f"padrow_{l}"], 1)
            link(V.tensor_scalar_add(CNTI[:, l, 1], n, float(P - 1)))
            link(V.tensor_single_scalar(CNTI[:, l, 2], CNTI[:, l, 1], P.bit_length() - 1, ALU.logical_shift_right))
            link(V.tensor_copy(CNT[:, l, 0], CNTI[:, l, 2]))
            link(V.tensor_tensor(SLEN[:, l, EXPERTS:], CNT[:, l, 0], SLEN[:, l, 0:EXPERTS], ALU.subtract))
            link(V.tensor_tensor_scan(SEND[:, l, 1:], ONES[:, 0:SEGMENTS], SLEN[:, l], 0.0, ALU.mult, ALU.add))
            full = [P, SLOT_TILES, SEGMENTS]
            past = TE[:, 0].rearrange("p (j s) -> p j s", s=SEGMENTS)
            steps = TE[:, 1].rearrange("p (j s) -> p j s", s=SEGMENTS)

            def over(row):
                return row.unsqueeze(1).to_broadcast(full)
            link(V.tensor_tensor(SROW[:, l], SOFF[:, l], SEND[:, l], ALU.subtract))
            link(V.scalar_tensor_tensor(SROW[:, l], SROW[:, l], float(P), SBASE[:, :], ALU.mult, ALU.add))
            link(V.tensor_tensor(SDIF[:, l], SROW[:, l, 1:], SROW[:, l, 0:SEGMENTS], ALU.subtract))
            link(V.tensor_tensor(past, JIDX[:, :].unsqueeze(2).to_broadcast(full), over(SEND[:, l, 1:]), ALU.is_ge))
            link(V.tensor_tensor(steps, past, over(SDIF[:, l]), ALU.mult))
            link(V.tensor_reduce(TR[:, 0], steps, AX.X, ALU.add))
            V.scalar_tensor_tensor(TBL[:, l, 0], JIDX[:, :], float(P), TR[:, 0], ALU.mult, ALU.add
                                   ).then_inc(s[f"rows_{l}"], 1)
            make_low_parts()
            link(V.tensor_tensor(steps, past, over(ESTEP[:, :]), ALU.mult))
            link(V.tensor_reduce(TR[:, 1], steps, AX.X, ALU.add))
            V.tensor_copy(TBL[:, l, 1], TR[:, 1]).then_inc(s[f"table_{l}"], 1)

        def dve_ffn(v, l):
            B, RB = l * SLOT_TILES, l * 16 * (SLOT_TILES // 3)
            V = nc.vector
            F = HID0 if l == 0 else HID1

            def xlow(c, i):
                v.wait_ge(s["xh"], tile(c, i) + (B + 1))
                V.tensor_tensor(XL[c % 3][:, :], bank[0][:, 0:P], XH[c % 3][:, :].bitcast(f32), ALU.subtract
                                ).then_inc(s["xl"], 1)
                V.tensor_copy(META[:, l, column(c, i), :], XS[c % 3][:, CH:CH + 2].unsqueeze(1)
                              ).then_inc(s["meta"], 1)

            def weigh(c, i):
                v.wait_ge(s["ylo"], tile(c, i) + (B + 1))
                V.scalar_tensor_tensor(YS[c % 3][:, :], bank[6 + c % 2][:, 0:CH], META[:, l, column(c, i), 1],
                                       YS[c % 3][:, :], ALU.mult, ALU.add).then_inc(s["ys"], 1)
                V.tensor_copy(YROW[c % 3][:, :], META[:, l, column(c, i), 0]).then_inc(s["yrow"], 1)

            def gate(c, i):
                v.wait_ge(s["gel"], tile(c, i) + (B + 1))
                V.tensor_tensor(H[c % 3][:, 0:F], bank[1 + c % 3][:, F:2 * F], G0[c % 3][:, :], ALU.mult
                                ).then_inc(s["h"], 1)

            def hlow(c, i):
                v.wait_ge(s["hh"], tile(c, i) + (B + 1))
                V.tensor_tensor(HL[c % 3][:, 0:F], bank[4 + c % 2][:, 0:F], HH[c % 3][:, 0:F].bitcast(f32),
                                ALU.subtract).then_inc(s["hl"], 1)

            def step(c, i):
                if c + 1 < SLOT_TILES:
                    xlow(c + 1, i)
                if c >= 3:
                    weigh(c - 3, i)
                if l == 1:
                    gate(c, i)
                if c >= 1:
                    hlow(c - 1, i)
            xlow(0, None)
            pipeline(v, step)
            weigh(SLOT_TILES - 3, None)
            hlow(SLOT_TILES - 1, None)
            weigh(SLOT_TILES - 2, None)
            weigh(SLOT_TILES - 1, None)

        def dve_residual(v, l, g):
            sl = slice(g * TG, (g + 1) * TG)
            q, k = (y[:, g].rearrange("p (t c) -> p t c", t=TG) for y in (Q, K))
            if g % 2 == 0:
                v.wait_ge(s[f"yl{g}_{l}"], 16 * TOP)
                nc.vector.tensor_tensor(X[:, sl], X[:, sl], k, ALU.add).then_inc(s[f"half_{l}"], 1)
                v.wait_ge(s[f"half_{l}"], g // 2 + 1)
            else:
                v.wait_ge(s[f"sum_{l}"], g // 2 + 1)
            nc.vector.tensor_tensor(X[:, sl], X[:, sl], q, ALU.add).then_inc(s[f"res_{l}"], 1)

        @block.vector
        def _(v):
            V = nc.vector
            xrow = lambda t: X[:, t, :]
            v.wait_ge(s["small"], 32)
            v.wait_ge(s["const"], CONSTS)
            V.tensor_scalar_mul(BD[:, :], ONES[:, :], COLS[:, C_BDWC:C_BDWC + 1]).then_inc(s["bd"], 1)
            V.tensor_scalar_mul(RSC[:, :], COLS[:, C_R1:C_R1 + EXPERTS], COLS[:, C_RS:C_RS + 1]
                                ).then_inc(s["rsc"], 1)
            def cube(src, g, i, ready, done):
                v.wait_ge(s[ready], g + 1)
                V.scalar_tensor_tensor(src[:, g], src[:, g], FOCUS_EPS, SQ[:, i, g % 2], ALU.add, ALU.mult
                                       ).then_inc(s[done], 1)

            def features(g):
                cube(K, g, 1, "k2", "k3")
                cube(Q, g, 0, "q2", "q3")
                v.wait_ge(s["k3"], g + 1)
                V.tensor_reduce(S3[:, g % 2], K[:, g].rearrange("p (t h d) -> p t h d", t=TG, d=HD), AX.X, ALU.add
                                ).then_inc(s["s3"], 1)
                v.wait_ge(s["s3"], g + 1)
                if g >= 2:
                    v.wait_ge(s["kv"], g - 1)
                V.reciprocal(VR[:, g % 2, :, CH:], S3[:, g % 2]).then_inc(s["r3"], 1)
                v.wait_ge(s["r3"], g + 1)
                v.wait_ge(s["v"], g + 1)
                full = [P, TG, HEADS, HD]
                V.tensor_tensor(VR[:, g % 2, :, 0:CH].rearrange("p t (h d) -> p t h d", d=HD),
                                v_bank[g][:, :].rearrange("p (t h d) -> p t h d", t=TG, d=HD),
                                VR[:, g % 2, :, CH:].unsqueeze(3).to_broadcast(full), ALU.mult).then_inc(s["vr"], 1)

            def kv_block(b):
                v.wait_ge(s["kv"], 2 * b + 2)
                V.tensor_tensor(KV[:, b], bank[5][:, 0:CH], HEADM[:, :], ALU.mult).then_inc(s["kvb"], 1)
                V.scalar_tensor_tensor(KSB[:, b], bank[5][:, CH:CH + HEADS], FOCUS_EPS, HEADM[:, 0:P:HD],
                                       ALU.add, ALU.mult).then_inc(s["kvb"], 1)

            def attended(g):
                v.wait_ge(s["num"], g + 1)
                V.reciprocal(RD[:, g % 2], den_bank[g][:, 0:TG * HEADS].rearrange(
                    "p (t h) -> p t h", t=TG)).then_inc(s["rden"], 1)
                v.wait_ge(s["rden"], g + 1)
                if g >= 2:
                    v.wait_ge(s["oT_ps"], g - 1)
                V.tensor_tensor(OTM[:, g % 2].rearrange("p t (h d) -> p t h d", d=HD),
                                num_bank[g][:, :].rearrange("p (t h d) -> p t h d", t=TG, d=HD),
                                RD[:, g % 2].unsqueeze(3).to_broadcast([P, TG, HEADS, HD]), ALU.mult
                                ).then_inc(s["ot"], 1)

            def projected(g):
                v.wait_ge(s["proj"], g + 1)
                v.wait_ge(s["xb"], g + 1)
                V.tensor_tensor(X[:, g * TG:(g + 1) * TG, :],
                                bank[g % 2][:, :].rearrange("p (t c) -> p t c", t=TG),
                                X[:, g * TG:(g + 1) * TG, :], ALU.add).then_inc(s["x1a"], 1)

            def stats(g):
                v.wait_ge(s[f"x{g}"], 16)
                ln_stats(v, 0, g, xrow)

            def norm(g):
                ln_norm(v, 0, g, xrow, lambda t: XN[:, t, :])
            stats(0)
            stats(1)
            norm(0)
            stats(2)
            norm(1)
            v.wait_ge(s["wproj"], 16)
            V.tensor_scalar_mul(WK[:, 0], WP[:, :], COLS[:, 0:1]).then_inc(s["wk"], 1)
            V.tensor_scalar_mul(WK[:, 2], WP[:, :], COLS[:, 2:3]).then_inc(s["wk"], 1)
            V.scalar_tensor_tensor(WK[:, 1], WP[:, :], COLS[:, 1:2], WP[:, :], ALU.mult, ALU.add
                                   ).then_inc(s["wk"], 1)
            norm(2)
            features(0)
            stats(3)
            norm(3)
            features(1)
            features(2)
            kv_block(0)
            attended(0)
            attended(1)
            features(3)
            kv_block(1)
            projected(0)
            projected(1)
            pbrow = lambda t: PB[:, 0, t, 0:CH]

            def stats_in(l, g, done, n):
                v.wait_ge(s[done], n)
                ln_stats(v, l, g, xrow)

            def low(first, end):
                for k in range(first, end):
                    v.wait_ge(s["whi"], k + 1)
                    v.wait_ge(s["wlo"], k)
                    V.tensor_tensor(part(k, 1), chunk(k), part(k, 0).bitcast(f32), ALU.subtract
                                    ).then_inc(s["wlo"], 1)
            chain = [0]
            stats_in(1, 0, "x1a", 1)
            stats_in(1, 1, "x1a", 2)
            attended(2)
            attended(3)
            ln_norm(v, 1, 0, xrow, pbrow)
            ln_norm(v, 1, 1, xrow, pbrow)
            dve_route(v, 0, 0, chain)
            dve_weights(v, 0, 0, chain)
            dve_slots(v, 0, 0, chain)
            projected(2)
            projected(3)
            stats_in(1, 2, "x1a", 3)
            stats_in(1, 3, "x1a", 4)
            dve_early(v, 0, chain)
            ln_norm(v, 1, 2, xrow, pbrow)
            ln_norm(v, 1, 3, xrow, pbrow)
            low(LOW_POOL, LOW_POOL + 2)
            dve_route(v, 0, 1, chain)
            dve_weights(v, 0, 1, chain)
            dve_slots(v, 0, 1, chain)
            dve_table(v, 0, chain, lambda: low(LOW_POOL + 2, CHUNKS0))
            dve_ffn(v, 0)
            v.wait_ge(s["y"], SLOT_TILES)
            low(CHUNKS0, CHUNKS0 + 2)

            def norm3(g):
                ln_norm(v, 2, g, xrow, lambda t: XN[:, t, :])
            for b in range(BATCH):
                for g in range(b * BG, (b + 1) * BG):
                    dve_residual(v, 0, g)
                    stats_in(2, g, "res_0", g + 1)
                for g in range(b * BG, (b + 1) * BG):
                    norm3(g)

            def carried(g):
                v.wait_ge(s["alam"], 1)
                v.wait_ge(s["e"], g + 1)
                V.tensor_scalar_mul(Q[:, g], Q[:, g], ALAM[:, :]).then_inc(s["at"], 1)
                v.wait_ge(s["at"], g + 1)
                at = Q[:, g].rearrange("p (t c) -> p t c", t=TG)
                V.tensor_tensor(XN[:, g * TG:(g + 1) * TG], at, at, ALU.mult).then_inc(s["t2"], 1)

            def recurrence(g):
                v.wait_ge(s["sq"], g + 1)
                v.wait_ge(s["ix"], g + 1)
                V.tensor_tensor(K[:, g], K[:, g], XN[:, g * TG:(g + 1) * TG].rearrange("p t c -> p (t c)"),
                                ALU.mult).then_inc(s["bt"], 1)
                v.wait_ge(s["bt"], g + 1)
                v.wait_ge(s["at"], g + 1)
                if g:
                    v.wait_ge(s["yscan"], g)
                b, first = g // 2, 1 + (g % 2) * GT
                V.tensor_tensor_scan(O[:, b, first:first + GT], Q[:, g], K[:, g],
                                     0.0 if g % 2 == 0 else O[:, b, first - 1:first],
                                     ALU.mult, ALU.add).then_inc(s["yscan"], 1)

            def added(g):
                v.wait_ge(s["yT"], g + 1)
                V.tensor_tensor(X[:, g * TG:(g + 1) * TG, :],
                                bank[6 + g % 2][:, :].rearrange("p (t c) -> p t c", t=TG),
                                X[:, g * TG:(g + 1) * TG, :], ALU.add).then_inc(s["xc"], 1)
            carried(0)
            carried(1)
            recurrence(0)
            recurrence(1)
            chain = [0]
            added(0)
            stats_in(3, 0, "xc", 1)
            added(1)
            stats_in(3, 1, "xc", 2)
            ln_norm(v, 3, 0, xrow, pbrow)
            ln_norm(v, 3, 1, xrow, pbrow)
            dve_mse(v, 0)
            carried(2)
            carried(3)
            dve_route(v, 1, 0, chain)
            dve_weights(v, 1, 0, chain)
            dve_slots(v, 1, 0, chain)
            recurrence(2)
            recurrence(3)
            added(2)
            stats_in(3, 2, "xc", 3)
            added(3)
            stats_in(3, 3, "xc", 4)
            dve_early(v, 1, chain)
            ln_norm(v, 3, 2, xrow, pbrow)
            ln_norm(v, 3, 3, xrow, pbrow)
            dve_mse(v, 1)
            low(CHUNKS0 + 2, CHUNKS0 + 4)
            dve_route(v, 1, 1, chain)
            dve_weights(v, 1, 1, chain)
            dve_slots(v, 1, 1, chain)
            dve_table(v, 1, chain, lambda: low(CHUNKS0 + 4, CHUNKS))
            dve_ffn(v, 1)
            for g in range(GROUPS):
                dve_residual(v, 1, g)



_INS = ["x", "wqkv", "wproj", "cols", "rows", "wpack", "wa", "wx"]


def layout(i):
    import numpy as np
    c = np.ascontiguousarray
    cols = np.concatenate([
        i["L0_attn_w_dwc"], i["L0_attn_b_dwc"][:, None], i["L1_attn_ba"][:, None], i["L1_attn_bx"][:, None],
        i["L1_attn_Lam"][:, None], i["L1_ffn_router_scale"][:, None], i["L0_ffn_router_w"].T,
        i["L1_ffn_router_w"]], axis=1)
    rows = np.concatenate([i["L0_attn_b_proj"], i["L1_ffn_per_expert_scale"]])[None, :]
    w1 = i["L0_ffn_w1"].transpose(1, 0, 2).reshape(P, -1)
    w2 = i["L0_ffn_w2"].reshape(EXPERTS, HID0 // P, P, CH).transpose(2, 0, 1, 3).reshape(P, -1)
    gate = i["L1_ffn_gating_w"].transpose(3, 0, 1, 2).reshape(P, -1)
    lin = i["L1_ffn_linear_w"].reshape(EXPERTS, HID1 // P, P, CH).transpose(2, 0, 1, 3).reshape(P, -1)
    return {"x": c(i["L0_attn_x"]), "wqkv": c(i["L0_attn_w_qkv"].T), "wproj": c(i["L0_attn_w_proj"].T),
            "cols": c(cols), "rows": c(rows), "wpack": c(np.concatenate([w1, w2, gate, lin], axis=1)),
            "wa": c(i["L1_attn_Wa"]), "wx": c(i["L1_attn_Wx"])}


def kernel(**inputs):
    import numpy as _np
    import concourse.bacc as _bacc
    from concourse import mybir as _mybir
    from concourse.bass_utils import run_bass_kernel_spmd as _run

    nc = _bacc.Bacc("TRN2", target_bir_lowering=False, num_devices=1)
    laid = layout({k: _np.asarray(v) for k, v in inputs.items()})
    args = [nc.dram_tensor(f"in_{n}", laid[n].shape, _mybir.dt.from_np(laid[n].dtype), kind="ExternalInput").ap()
            for n in _INS]
    out = nc.dram_tensor("out_0", (BATCH, SEQ, CH), _mybir.dt.float32, kind="ExternalOutput").ap()
    two_layers(nc, *args, out)
    r = _run(nc, [{f"in_{n}": laid[n] for n in _INS}], core_ids=[0])
    return r.results[0]["out_0"]
```
